# Optimizing a Trainium2 kernel written in Bass

```python
import numpy as np
import jax
import jax.numpy as jnp

def _softmax(x, axis=-1):
    return jax.nn.softmax(x, axis=axis)

def _gelu(x):
    return jax.nn.gelu(x, approximate=True)

def _silu(x):
    return jax.nn.silu(x)

def _sigmoid(x):
    return jax.nn.sigmoid(x)

def _layernorm(x, axis=-1, eps=1e-05):
    m = jnp.mean(x, axis=axis, keepdims=True)
    v = jnp.var(x, axis=axis, keepdims=True)
    return (x - m) / jnp.sqrt(v + eps)

def _scatter_add(tgt, idx, src, axis=0):
    return tgt.at[idx].add(src)

def _segment_sum(src, seg, n):
    return jax.ops.segment_sum(src, seg, n)
kernel_name = 'mk_xattn_seq_d4_seqx_r8_6b38f7'

def setup_inputs(seed: int=0):
    np.random.seed(seed)
    _w = jnp.asarray

    def _rec_inputs():
        import jax
        import jax.numpy as jnp
        _rk = jax.random.key(seed)
        x = 7.22e-05 + 1 * jax.random.normal(jax.random.fold_in(_rk, 1), (16, 128, 256), jnp.float32)
        _lenS = 128 - jax.random.randint(jax.random.fold_in(_rk, 7), (16,), 0, max(1, 128 // 4) + 1, jnp.int32)
        _lenS2 = 128 - jax.random.randint(jax.random.fold_in(_rk, 8), (16,), 0, max(1, 128 // 4) + 1, jnp.int32)
        _ctx_2048P = jax.random.normal(jax.random.fold_in(_rk, 11), (16, 16, 256), jnp.float32)
        _ctx_2048c = jax.random.dirichlet(jax.random.fold_in(_rk, 511), 0.3 * jnp.ones((16,), jnp.float32), (16, 128))
        _ctx_2048t = jnp.einsum('bsk,bkd->bsd', _ctx_2048c, _ctx_2048P)
        _ctx_2048t = _ctx_2048t * jax.lax.rsqrt(jnp.mean(jnp.square(_ctx_2048t)) + 1e-12) * 0.953939
        ctx_2048 = 0.000189249 + 0.0999589 * (_ctx_2048t + 0.3 * jax.random.normal(jax.random.fold_in(_rk, 611), (16, 128, 256), jnp.float32))
        _validS = jnp.arange(128)[None, :] < _lenS[:, None]
        _validS2 = jnp.arange(128)[None, :] < _lenS2[:, None]
        _causal = jnp.tril(jnp.ones((128, 128), dtype=bool))
        mask_BxS2_ik0 = jnp.where(jnp.broadcast_to(_validS2[:, :], (16, 128)), 0, 1).astype(jnp.int32)
        return (x, ctx_2048, mask_BxS2_ik0)
    x, ctx_2048, mask_BxS2_ik0 = _rec_inputs()

    def _L0_xattn_setup():
        import jax, jax.numpy as jnp
        import numpy as np
        E, H, L, B = (256, 32, 128, 4)
        S = E // H
        DM, DD = (32, 64)

        def _ln(x, w, b, eps=1e-05):
            m = x.mean(-1, keepdims=True)
            v = ((x - m) ** 2).mean(-1, keepdims=True)
            return (x - m) / jnp.sqrt(v + eps) * w + b

        def _block(x, state, ln1_w, ln1_b, ln2_w, ln2_b, maa_x, maa_w1, maa_w2, maa_stack, time_decay, td_w1, td_w2, u, Wr, Wk, Wv, Wg, Wo, gn_w, gn_b, ffn_maa_k, ffn_maa_r, Wfk, Wfr, Wfv):
            b, l, e = x.shape
            h = u.shape[0]
            s_ = e // h
            xa = _ln(x, ln1_w, ln1_b)
            sx = jnp.concatenate([state[:, 1:2] - xa[:, :1], xa[:, :-1] - xa[:, 1:]], axis=1)
            xxx = jnp.tanh((xa + sx * maa_x) @ maa_w1).reshape(b, l, 5, DM)
            xxx = jnp.einsum('blfd,fde->blfe', xxx, maa_w2)
            xm = xa[:, :, None] + sx[:, :, None] * (maa_stack + xxx)
            xk, xw, xv, xr, xg = (xm[:, :, j] for j in range(5))
            w = jnp.exp(-jnp.exp(time_decay + jnp.tanh(xw @ td_w1) @ td_w2)).reshape(b, l, h, s_)
            r = (xr @ Wr.T).reshape(b, l, h, s_)
            k = (xk @ Wk.T).reshape(b, l, h, s_)
            v = (xv @ Wv.T).reshape(b, l, h, s_)
            g = jax.nn.silu(xg @ Wg.T)
            s0 = state[:, 2:2 + s_].reshape(b, h, s_, s_)

            def step(s, rkvw):
                r_t, k_t, v_t, w_t = rkvw
                a = k_t[..., :, None] * v_t[..., None, :]
                out = jnp.einsum('bhi,bhij->bhj', r_t, u * a + s)
                s = a + w_t[..., :, None] * s
                return (s, out)
            rkvw = tuple((jnp.moveaxis(t, 1, 0) for t in (r, k, v, w)))
            _, out = jax.lax.scan(step, s0, rkvw)
            out = jnp.moveaxis(out, 0, 1).reshape(b, l, e)
            og = out.reshape(b, l, h, s_)
            m = og.mean(-1, keepdims=True)
            va = ((og - m) ** 2).mean(-1, keepdims=True)
            og = ((og - m) / jnp.sqrt(va + 1e-05)).reshape(b, l, e) * gn_w + gn_b
            x1 = x + og * g @ Wo.T
            xc = _ln(x1, ln2_w, ln2_b)
            sx2 = jnp.concatenate([state[:, 0:1] - xc[:, :1], xc[:, :-1] - xc[:, 1:]], axis=1)
            xk2 = xc + sx2 * ffn_maa_k
            xr2 = xc + sx2 * ffn_maa_r
            rr = jax.nn.sigmoid(xr2 @ Wfr.T)
            kk = jnp.square(jax.nn.relu(xk2 @ Wfk.T))
            return x1 + rr * (kk @ Wfv.T)
        key = jax.random.key(seed)
        ks = jax.random.split(key, 24)
        sc = 0.02
        d = {'x': jax.random.normal(ks[0], (B, L, E), jnp.float32), 'state': jax.random.normal(ks[1], (B, 2 + S, E), jnp.float32) * 0.1, 'ln1_w': jnp.ones((E,), jnp.float32), 'ln1_b': jnp.zeros((E,), jnp.float32), 'ln2_w': jnp.ones((E,), jnp.float32), 'ln2_b': jnp.zeros((E,), jnp.float32), 'maa_x': jax.random.normal(ks[2], (E,), jnp.float32) * 0.1, 'maa_w1': jax.random.normal(ks[3], (E, 5 * DM), jnp.float32) * sc, 'maa_w2': jax.random.normal(ks[4], (5, DM, E), jnp.float32) * sc, 'maa_stack': jax.random.normal(ks[5], (1, 5, E), jnp.float32) * 0.1, 'time_decay': jax.random.normal(ks[6], (E,), jnp.float32) * 0.5, 'td_w1': jax.random.normal(ks[7], (E, DD), jnp.float32) * sc, 'td_w2': jax.random.normal(ks[8], (DD, E), jnp.float32) * sc, 'u': jax.random.normal(ks[9], (H, S, 1), jnp.float32) * 0.1, 'Wr': jax.random.normal(ks[10], (E, E), jnp.float32) * sc, 'Wk': jax.random.normal(ks[11], (E, E), jnp.float32) * sc, 'Wv': jax.random.normal(ks[12], (E, E), jnp.float32) * sc, 'Wg': jax.random.normal(ks[13], (E, E), jnp.float32) * sc, 'Wo': jax.random.normal(ks[14], (E, E), jnp.float32) * sc, 'gn_w': jnp.ones((E,), jnp.float32), 'gn_b': jnp.zeros((E,), jnp.float32), 'ffn_maa_k': jax.random.normal(ks[15], (E,), jnp.float32) * 0.1, 'ffn_maa_r': jax.random.normal(ks[16], (E,), jnp.float32) * 0.1, 'Wfk': jax.random.normal(ks[17], (E, E), jnp.float32) * sc, 'Wfr': jax.random.normal(ks[18], (E, E), jnp.float32) * sc, 'Wfv': jax.random.normal(ks[19], (E, E), jnp.float32) * sc}
        return d
    _L0_xattn_all = _L0_xattn_setup()
    _L0_xattn_in = {k: v for k, v in _L0_xattn_all.items() if k in ('ln1_w', 'ln1_b', 'ln2_w', 'ln2_b', 'maa_x', 'maa_w1', 'maa_w2', 'maa_stack', 'time_decay', 'td_w1', 'td_w2', 'u', 'Wr', 'Wk', 'Wv', 'Wg', 'Wo', 'gn_w', 'gn_b', 'ffn_maa_k', 'ffn_maa_r', 'Wfk', 'Wfr', 'Wfv')}
    del _L0_xattn_all

    def _L1_xattn_setup():
        import jax, jax.numpy as jnp
        import numpy as np
        D_MODEL = 128
        N_HEAD = 16
        D_HEAD = 64
        IDX_LIST = [128, 256]
        SCALE = 1.0 / D_HEAD ** 0.5
        LN_EPS = 1e-05
        key = jax.random.key(seed)
        ks = jax.random.split(key, 9)
        s = 0.02
        B, L = (2, 256)
        return {'z1ss': jax.random.normal(ks[0], (B, D_MODEL, L), dtype=jnp.float32), 'u1ss': jax.random.normal(ks[1], (B, D_MODEL, L), dtype=jnp.float32), 'Wqkv0': jax.random.normal(ks[2], (3 * N_HEAD * D_HEAD, D_MODEL), dtype=jnp.float32) * s, 'Wqkv1': jax.random.normal(ks[3], (3 * N_HEAD * D_HEAD, D_MODEL), dtype=jnp.float32) * s, 'Winj0': jax.random.normal(ks[4], (3 * N_HEAD * D_HEAD, D_MODEL), dtype=jnp.float32) * s, 'Winj1': jax.random.normal(ks[5], (3 * N_HEAD * D_HEAD, D_MODEL), dtype=jnp.float32) * s, 'Wo': jax.random.normal(ks[6], (D_MODEL, N_HEAD * D_HEAD), dtype=jnp.float32) * s, 'bo': jax.random.normal(ks[7], (D_MODEL,), dtype=jnp.float32) * s, 'r_w_bias': jax.random.uniform(ks[8], (N_HEAD, D_HEAD), minval=-0.05, maxval=0.05, dtype=jnp.float32)}
    _L1_xattn_all = _L1_xattn_setup()
    _L1_xattn_in = {k: v for k, v in _L1_xattn_all.items() if k in ('Wqkv0', 'Wqkv1', 'Winj0', 'Winj1', 'Wo', 'bo', 'r_w_bias')}
    del _L1_xattn_all

    def _L2_xattn_setup():
        import jax, jax.numpy as jnp
        import numpy as np
        B, P, K, H, NH = (4, 256, 32, 256, 16)
        DH = H // NH
        EPS = 1e-06

        def rmsnorm(x, w):
            var = jnp.mean(jnp.square(x), axis=-1, keepdims=True)
            return x * jax.lax.rsqrt(var + EPS) * w
        key = jax.random.key(seed)
        ks = jax.random.split(key, 12)
        s = 0.02
        return {'x': jax.random.normal(ks[0], (B, P, H), jnp.float32), 'latents': jax.random.normal(ks[1], (B, K, H), jnp.float32), 'attention_mask': jax.random.randint(ks[2], (B, P), 0, 2, jnp.int32), 'q_w': s * jax.random.normal(ks[3], (H, H), jnp.float32), 'q_b': jnp.zeros((H,), jnp.float32), 'kv_w': s * jax.random.normal(ks[4], (H, 2 * H), jnp.float32), 'kv_b': jnp.zeros((2 * H,), jnp.float32), 'out_w': s * jax.random.normal(ks[5], (H, H), jnp.float32), 'out_b': jnp.zeros((H,), jnp.float32), 'postnorm_w': jnp.ones((H,), jnp.float32), 'mlp_w1': s * jax.random.normal(ks[6], (H, 4 * H), jnp.float32), 'mlp_b1': jnp.zeros((4 * H,), jnp.float32), 'mlp_w2': s * jax.random.normal(ks[7], (4 * H, H), jnp.float32), 'mlp_b2': jnp.zeros((H,), jnp.float32)}
    _L2_xattn_all = _L2_xattn_setup()
    _L2_xattn_in = {k: v for k, v in _L2_xattn_all.items() if k in ('q_w', 'q_b', 'kv_w', 'kv_b', 'out_w', 'out_b', 'postnorm_w', 'mlp_w1', 'mlp_b1', 'mlp_w2', 'mlp_b2')}
    del _L2_xattn_all

    def _L3_xattn_setup():
        import jax, jax.numpy as jnp
        import numpy as np
        B, Q, S1, S2 = (4, 32, 256, 256)
        D, H, K, F = (256, 16, 128, 1024)
        LN_EPS = 1e-05

        def _layer_norm(x, scale, offset):
            mu = jnp.mean(x, axis=-1, keepdims=True)
            var = jnp.var(x, axis=-1, keepdims=True)
            return (x - mu) * jax.lax.rsqrt(var + LN_EPS) * scale + offset

        def _cross_attention(q_in, kv_in, wq, bq, wk, bk, wv, bv, wo, bo, bias_k, bias_v):
            b, q_len, _ = q_in.shape
            t = kv_in.shape[1]
            qh = (q_in @ wq + bq).reshape(b, q_len, H, K)
            kh = (kv_in @ wk + bk).reshape(b, t, H, K)
            vh = (kv_in @ wv + bv).reshape(b, t, H, K)
            kh = jnp.concatenate([kh, jnp.broadcast_to(bias_k, (b, 1, H, K))], axis=1)
            vh = jnp.concatenate([vh, jnp.broadcast_to(bias_v, (b, 1, H, K))], axis=1)
            scale = jnp.sqrt(jnp.asarray(K, q_in.dtype))
            logits = jnp.einsum('bqhk,bthk->bhqt', qh, kh) / scale
            weights = jax.nn.softmax(logits, axis=-1)
            ctx = jnp.einsum('bhqt,bthk->bqhk', weights, vh).reshape(b, q_len, H * K)
            return ctx @ wo + bo

        def _forward(x, xf_1, xf_2, ln1_scale, ln1_offset, wq1, bq1, wk1, bk1, wv1, bv1, wo1, bo1, bias_k1, bias_v1, ln2_scale, ln2_offset, wq2, bq2, wk2, bk2, wv2, bv2, wo2, bo2, bias_k2, bias_v2, ln_mlp_scale, ln_mlp_offset, w_fc1, b_fc1, w_fc2, b_fc2):
            res = x
            h = _layer_norm(x, ln1_scale, ln1_offset)
            x = res + _cross_attention(h, xf_1, wq1, bq1, wk1, bk1, wv1, bv1, wo1, bo1, bias_k1, bias_v1)
            res = x
            h = _layer_norm(x, ln2_scale, ln2_offset)
            x = res + _cross_attention(h, xf_2, wq2, bq2, wk2, bk2, wv2, bv2, wo2, bo2, bias_k2, bias_v2)
            h = _layer_norm(x, ln_mlp_scale, ln_mlp_offset)
            h = jax.nn.gelu(h @ w_fc1 + b_fc1, approximate=False) @ w_fc2 + b_fc2
            return x + h
        key = jax.random.key(seed)
        ks = iter(jax.random.split(key, 64))

        def rn(shape, s=0.02):
            return jax.random.normal(next(ks), shape, jnp.float32) * s
        inp = {'x': rn((B, Q, D), 1.0), 'xf_1': rn((B, S1, D), 1.0), 'xf_2': rn((B, S2, D), 1.0)}
        for i in (1, 2):
            inp[f'ln{i}_scale'] = jnp.ones((D,), jnp.float32)
            inp[f'ln{i}_offset'] = jnp.zeros((D,), jnp.float32)
            inp[f'wq{i}'] = rn((D, H * K))
            inp[f'bq{i}'] = jnp.zeros((H * K,), jnp.float32)
            inp[f'wk{i}'] = rn((D, H * K))
            inp[f'bk{i}'] = jnp.zeros((H * K,), jnp.float32)
            inp[f'wv{i}'] = rn((D, H * K))
            inp[f'bv{i}'] = jnp.zeros((H * K,), jnp.float32)
            inp[f'wo{i}'] = rn((H * K, D))
            inp[f'bo{i}'] = jnp.zeros((D,), jnp.float32)
            inp[f'bias_k{i}'] = rn((1, 1, H, K))
            inp[f'bias_v{i}'] = rn((1, 1, H, K))
        inp['ln_mlp_scale'] = jnp.ones((D,), jnp.float32)
        inp['ln_mlp_offset'] = jnp.zeros((D,), jnp.float32)
        inp['w_fc1'] = rn((D, F))
        inp['b_fc1'] = jnp.zeros((F,), jnp.float32)
        inp['w_fc2'] = rn((F, D))
        inp['b_fc2'] = jnp.zeros((D,), jnp.float32)
        return inp
    _L3_xattn_all = _L3_xattn_setup()
    _L3_xattn_in = {k: v for k, v in _L3_xattn_all.items() if k in ('ln1_scale', 'ln1_offset', 'wq1', 'bq1', 'wk1', 'bk1', 'wv1', 'bv1', 'wo1', 'bo1', 'bias_k1', 'bias_v1', 'ln2_scale', 'ln2_offset', 'wq2', 'bq2', 'wk2', 'bk2', 'wv2', 'bv2', 'wo2', 'bo2', 'bias_k2', 'bias_v2', 'ln_mlp_scale', 'ln_mlp_offset', 'w_fc1', 'b_fc1', 'w_fc2', 'b_fc2')}
    del _L3_xattn_all
    return {'x': x, 'ctx_2048': ctx_2048, 'mask_BxS2_ik0': mask_BxS2_ik0, 'L0_xattn_ln1_w': _L0_xattn_in['ln1_w'], 'L0_xattn_ln1_b': _L0_xattn_in['ln1_b'], 'L0_xattn_ln2_w': _L0_xattn_in['ln2_w'], 'L0_xattn_ln2_b': _L0_xattn_in['ln2_b'], 'L0_xattn_maa_x': _L0_xattn_in['maa_x'], 'L0_xattn_maa_w1': _L0_xattn_in['maa_w1'], 'L0_xattn_maa_w2': _L0_xattn_in['maa_w2'], 'L0_xattn_maa_stack': _L0_xattn_in['maa_stack'], 'L0_xattn_time_decay': _L0_xattn_in['time_decay'], 'L0_xattn_td_w1': _L0_xattn_in['td_w1'], 'L0_xattn_td_w2': _L0_xattn_in['td_w2'], 'L0_xattn_u': _L0_xattn_in['u'], 'L0_xattn_Wr': _L0_xattn_in['Wr'], 'L0_xattn_Wk': _L0_xattn_in['Wk'], 'L0_xattn_Wv': _L0_xattn_in['Wv'], 'L0_xattn_Wg': _L0_xattn_in['Wg'], 'L0_xattn_Wo': _L0_xattn_in['Wo'], 'L0_xattn_gn_w': _L0_xattn_in['gn_w'], 'L0_xattn_gn_b': _L0_xattn_in['gn_b'], 'L0_xattn_ffn_maa_k': _L0_xattn_in['ffn_maa_k'], 'L0_xattn_ffn_maa_r': _L0_xattn_in['ffn_maa_r'], 'L0_xattn_Wfk': _L0_xattn_in['Wfk'], 'L0_xattn_Wfr': _L0_xattn_in['Wfr'], 'L0_xattn_Wfv': _L0_xattn_in['Wfv'], 'L1_xattn_Wqkv0': _L1_xattn_in['Wqkv0'], 'L1_xattn_Wqkv1': _L1_xattn_in['Wqkv1'], 'L1_xattn_Winj0': _L1_xattn_in['Winj0'], 'L1_xattn_Winj1': _L1_xattn_in['Winj1'], 'L1_xattn_Wo': _L1_xattn_in['Wo'], 'L1_xattn_bo': _L1_xattn_in['bo'], 'L1_xattn_r_w_bias': _L1_xattn_in['r_w_bias'], 'L2_xattn_q_w': _L2_xattn_in['q_w'], 'L2_xattn_q_b': _L2_xattn_in['q_b'], 'L2_xattn_kv_w': _L2_xattn_in['kv_w'], 'L2_xattn_kv_b': _L2_xattn_in['kv_b'], 'L2_xattn_out_w': _L2_xattn_in['out_w'], 'L2_xattn_out_b': _L2_xattn_in['out_b'], 'L2_xattn_postnorm_w': _L2_xattn_in['postnorm_w'], 'L2_xattn_mlp_w1': _L2_xattn_in['mlp_w1'], 'L2_xattn_mlp_b1': _L2_xattn_in['mlp_b1'], 'L2_xattn_mlp_w2': _L2_xattn_in['mlp_w2'], 'L2_xattn_mlp_b2': _L2_xattn_in['mlp_b2'], 'L3_xattn_ln1_scale': _L3_xattn_in['ln1_scale'], 'L3_xattn_ln1_offset': _L3_xattn_in['ln1_offset'], 'L3_xattn_wq1': _L3_xattn_in['wq1'], 'L3_xattn_bq1': _L3_xattn_in['bq1'], 'L3_xattn_wk1': _L3_xattn_in['wk1'], 'L3_xattn_bk1': _L3_xattn_in['bk1'], 'L3_xattn_wv1': _L3_xattn_in['wv1'], 'L3_xattn_bv1': _L3_xattn_in['bv1'], 'L3_xattn_wo1': _L3_xattn_in['wo1'], 'L3_xattn_bo1': _L3_xattn_in['bo1'], 'L3_xattn_bias_k1': _L3_xattn_in['bias_k1'], 'L3_xattn_bias_v1': _L3_xattn_in['bias_v1'], 'L3_xattn_ln2_scale': _L3_xattn_in['ln2_scale'], 'L3_xattn_ln2_offset': _L3_xattn_in['ln2_offset'], 'L3_xattn_wq2': _L3_xattn_in['wq2'], 'L3_xattn_bq2': _L3_xattn_in['bq2'], 'L3_xattn_wk2': _L3_xattn_in['wk2'], 'L3_xattn_bk2': _L3_xattn_in['bk2'], 'L3_xattn_wv2': _L3_xattn_in['wv2'], 'L3_xattn_bv2': _L3_xattn_in['bv2'], 'L3_xattn_wo2': _L3_xattn_in['wo2'], 'L3_xattn_bo2': _L3_xattn_in['bo2'], 'L3_xattn_bias_k2': _L3_xattn_in['bias_k2'], 'L3_xattn_bias_v2': _L3_xattn_in['bias_v2'], 'L3_xattn_ln_mlp_scale': _L3_xattn_in['ln_mlp_scale'], 'L3_xattn_ln_mlp_offset': _L3_xattn_in['ln_mlp_offset'], 'L3_xattn_w_fc1': _L3_xattn_in['w_fc1'], 'L3_xattn_b_fc1': _L3_xattn_in['b_fc1'], 'L3_xattn_w_fc2': _L3_xattn_in['w_fc2'], 'L3_xattn_b_fc2': _L3_xattn_in['b_fc2']}

def reference(x, ctx_2048, mask_BxS2_ik0, L0_xattn_ln1_w, L0_xattn_ln1_b, L0_xattn_ln2_w, L0_xattn_ln2_b, L0_xattn_maa_x, L0_xattn_maa_w1, L0_xattn_maa_w2, L0_xattn_maa_stack, L0_xattn_time_decay, L0_xattn_td_w1, L0_xattn_td_w2, L0_xattn_u, L0_xattn_Wr, L0_xattn_Wk, L0_xattn_Wv, L0_xattn_Wg, L0_xattn_Wo, L0_xattn_gn_w, L0_xattn_gn_b, L0_xattn_ffn_maa_k, L0_xattn_ffn_maa_r, L0_xattn_Wfk, L0_xattn_Wfr, L0_xattn_Wfv, L1_xattn_Wqkv0, L1_xattn_Wqkv1, L1_xattn_Winj0, L1_xattn_Winj1, L1_xattn_Wo, L1_xattn_bo, L1_xattn_r_w_bias, L2_xattn_q_w, L2_xattn_q_b, L2_xattn_kv_w, L2_xattn_kv_b, L2_xattn_out_w, L2_xattn_out_b, L2_xattn_postnorm_w, L2_xattn_mlp_w1, L2_xattn_mlp_b1, L2_xattn_mlp_w2, L2_xattn_mlp_b2, L3_xattn_ln1_scale, L3_xattn_ln1_offset, L3_xattn_wq1, L3_xattn_bq1, L3_xattn_wk1, L3_xattn_bk1, L3_xattn_wv1, L3_xattn_bv1, L3_xattn_wo1, L3_xattn_bo1, L3_xattn_bias_k1, L3_xattn_bias_v1, L3_xattn_ln2_scale, L3_xattn_ln2_offset, L3_xattn_wq2, L3_xattn_bq2, L3_xattn_wk2, L3_xattn_bk2, L3_xattn_wv2, L3_xattn_bv2, L3_xattn_wo2, L3_xattn_bo2, L3_xattn_bias_k2, L3_xattn_bias_v2, L3_xattn_ln_mlp_scale, L3_xattn_ln_mlp_offset, L3_xattn_w_fc1, L3_xattn_b_fc1, L3_xattn_w_fc2, L3_xattn_b_fc2):
    import jax
    import jax.numpy as jnp

    def _L0_xattn_ref(x, state, ln1_w, ln1_b, ln2_w, ln2_b, maa_x, maa_w1, maa_w2, maa_stack, time_decay, td_w1, td_w2, u, Wr, Wk, Wv, Wg, Wo, gn_w, gn_b, ffn_maa_k, ffn_maa_r, Wfk, Wfr, Wfv):
        import jax, jax.numpy as jnp
        import numpy as np
        E, H, L, B = (256, 32, 128, 4)
        S = E // H
        DM, DD = (32, 64)

        def _ln(x, w, b, eps=1e-05):
            m = x.mean(-1, keepdims=True)
            v = ((x - m) ** 2).mean(-1, keepdims=True)
            return (x - m) / jnp.sqrt(v + eps) * w + b

        def _block(x, state, ln1_w, ln1_b, ln2_w, ln2_b, maa_x, maa_w1, maa_w2, maa_stack, time_decay, td_w1, td_w2, u, Wr, Wk, Wv, Wg, Wo, gn_w, gn_b, ffn_maa_k, ffn_maa_r, Wfk, Wfr, Wfv):
            b, l, e = x.shape
            h = u.shape[0]
            s_ = e // h
            xa = _ln(x, ln1_w, ln1_b)
            sx = jnp.concatenate([state[:, 1:2] - xa[:, :1], xa[:, :-1] - xa[:, 1:]], axis=1)
            xxx = jnp.tanh((xa + sx * maa_x) @ maa_w1).reshape(b, l, 5, DM)
            xxx = jnp.einsum('blfd,fde->blfe', xxx, maa_w2)
            xm = xa[:, :, None] + sx[:, :, None] * (maa_stack + xxx)
            xk, xw, xv, xr, xg = (xm[:, :, j] for j in range(5))
            w = jnp.exp(-jnp.exp(time_decay + jnp.tanh(xw @ td_w1) @ td_w2)).reshape(b, l, h, s_)
            r = (xr @ Wr.T).reshape(b, l, h, s_)
            k = (xk @ Wk.T).reshape(b, l, h, s_)
            v = (xv @ Wv.T).reshape(b, l, h, s_)
            g = jax.nn.silu(xg @ Wg.T)
            s0 = state[:, 2:2 + s_].reshape(b, h, s_, s_)

            def step(s, rkvw):
                r_t, k_t, v_t, w_t = rkvw
                a = k_t[..., :, None] * v_t[..., None, :]
                out = jnp.einsum('bhi,bhij->bhj', r_t, u * a + s)
                s = a + w_t[..., :, None] * s
                return (s, out)
            rkvw = tuple((jnp.moveaxis(t, 1, 0) for t in (r, k, v, w)))
            _, out = jax.lax.scan(step, s0, rkvw)
            out = jnp.moveaxis(out, 0, 1).reshape(b, l, e)
            og = out.reshape(b, l, h, s_)
            m = og.mean(-1, keepdims=True)
            va = ((og - m) ** 2).mean(-1, keepdims=True)
            og = ((og - m) / jnp.sqrt(va + 1e-05)).reshape(b, l, e) * gn_w + gn_b
            x1 = x + og * g @ Wo.T
            xc = _ln(x1, ln2_w, ln2_b)
            sx2 = jnp.concatenate([state[:, 0:1] - xc[:, :1], xc[:, :-1] - xc[:, 1:]], axis=1)
            xk2 = xc + sx2 * ffn_maa_k
            xr2 = xc + sx2 * ffn_maa_r
            rr = jax.nn.sigmoid(xr2 @ Wfr.T)
            kk = jnp.square(jax.nn.relu(xk2 @ Wfk.T))
            return x1 + rr * (kk @ Wfv.T)
        return _block(x, state, ln1_w, ln1_b, ln2_w, ln2_b, maa_x, maa_w1, maa_w2, maa_stack, time_decay, td_w1, td_w2, u, Wr, Wk, Wv, Wg, Wo, gn_w, gn_b, ffn_maa_k, ffn_maa_r, Wfk, Wfr, Wfv)

    def _L1_xattn_ref(z1ss, u1ss, Wqkv0, Wqkv1, Winj0, Winj1, Wo, bo, r_w_bias):
        import jax, jax.numpy as jnp
        import numpy as np
        D_MODEL = 128
        N_HEAD = 16
        D_HEAD = 64
        IDX_LIST = [128, 256]
        SCALE = 1.0 / D_HEAD ** 0.5
        LN_EPS = 1e-05
        bsz, d_model, qlen = z1ss.shape
        bounds = [0] + IDX_LIST
        Wq_list, Wi_list = ([Wqkv0, Wqkv1], [Winj0, Winj1])
        chunks = []
        for i in range(len(IDX_LIST)):
            s, e = (bounds[i], bounds[i + 1])
            h = jnp.einsum('od,bdl->bol', Wq_list[i], z1ss[:, :, s:e])
            h = h + jnp.einsum('od,bdl->bol', Wi_list[i], u1ss[:, :, s:e])
            chunks.append(h)
        w_heads = jnp.concatenate(chunks, axis=2)
        q, k, v = jnp.split(w_heads, 3, axis=1)
        q = q[:, :, -qlen:]
        klen = k.shape[2]
        q = q.reshape(bsz, N_HEAD, D_HEAD, qlen)
        k = k.reshape(bsz, N_HEAD, D_HEAD, klen)
        v = v.reshape(bsz, N_HEAD, D_HEAD, klen)
        rq = q + r_w_bias[None, :, :, None]
        score = jnp.einsum('bndi,bndj->bnij', rq, k) * SCALE
        prob = jax.nn.softmax(score, axis=-1)
        attn_vec = jnp.einsum('bnij,bndj->bndi', prob, v)
        attn_vec = attn_vec.reshape(bsz, N_HEAD * D_HEAD, qlen)
        attn_out = jnp.einsum('od,bdl->bol', Wo, attn_vec) + bo[None, :, None]
        x = attn_out + z1ss
        m = jnp.mean(x, axis=1, keepdims=True)
        var = jnp.var(x, axis=1, keepdims=True)
        return (x - m) * jax.lax.rsqrt(var + LN_EPS)

    def _L2_xattn_ref(x, latents, attention_mask, q_w, q_b, kv_w, kv_b, out_w, out_b, postnorm_w, mlp_w1, mlp_b1, mlp_w2, mlp_b2):
        import jax, jax.numpy as jnp
        import numpy as np
        B, P, K, H, NH = (4, 256, 32, 256, 16)
        DH = H // NH
        EPS = 1e-06

        def rmsnorm(x, w):
            var = jnp.mean(jnp.square(x), axis=-1, keepdims=True)
            return x * jax.lax.rsqrt(var + EPS) * w
        b, p, _ = x.shape
        k_len = latents.shape[1]
        residual = latents
        h = jnp.concatenate([x, latents], axis=1)
        q = (latents @ q_w + q_b).reshape(b, k_len, NH, DH)
        kv = (h @ kv_w + kv_b).reshape(b, p + k_len, NH, DH, 2)
        kmat, v = (kv[..., 0], kv[..., 1])
        attn = jnp.einsum('bkhd,bnhd->bhkn', q, kmat) / DH
        full_mask = jnp.concatenate([attention_mask.astype(bool), jnp.ones((b, k_len), bool)], axis=-1)
        attn = jnp.where(full_mask[:, None, None, :], attn, -jnp.inf)
        attn = jax.nn.softmax(attn.astype(jnp.float32), axis=-1).astype(q.dtype)
        attn_out = jnp.einsum('bhkn,bnhd->bkhd', attn, v).reshape(b, k_len, H)
        attn_out = attn_out @ out_w + out_b + residual
        out = rmsnorm(attn_out, postnorm_w)
        out = jax.nn.gelu(out @ mlp_w1 + mlp_b1) @ mlp_w2 + mlp_b2
        return out + residual

    def _L3_xattn_ref(x, xf_1, xf_2, ln1_scale, ln1_offset, wq1, bq1, wk1, bk1, wv1, bv1, wo1, bo1, bias_k1, bias_v1, ln2_scale, ln2_offset, wq2, bq2, wk2, bk2, wv2, bv2, wo2, bo2, bias_k2, bias_v2, ln_mlp_scale, ln_mlp_offset, w_fc1, b_fc1, w_fc2, b_fc2):
        import jax, jax.numpy as jnp
        import numpy as np
        B, Q, S1, S2 = (4, 32, 256, 256)
        D, H, K, F = (256, 16, 128, 1024)
        LN_EPS = 1e-05

        def _layer_norm(x, scale, offset):
            mu = jnp.mean(x, axis=-1, keepdims=True)
            var = jnp.var(x, axis=-1, keepdims=True)
            return (x - mu) * jax.lax.rsqrt(var + LN_EPS) * scale + offset

        def _cross_attention(q_in, kv_in, wq, bq, wk, bk, wv, bv, wo, bo, bias_k, bias_v):
            b, q_len, _ = q_in.shape
            t = kv_in.shape[1]
            qh = (q_in @ wq + bq).reshape(b, q_len, H, K)
            kh = (kv_in @ wk + bk).reshape(b, t, H, K)
            vh = (kv_in @ wv + bv).reshape(b, t, H, K)
            kh = jnp.concatenate([kh, jnp.broadcast_to(bias_k, (b, 1, H, K))], axis=1)
            vh = jnp.concatenate([vh, jnp.broadcast_to(bias_v, (b, 1, H, K))], axis=1)
            scale = jnp.sqrt(jnp.asarray(K, q_in.dtype))
            logits = jnp.einsum('bqhk,bthk->bhqt', qh, kh) / scale
            weights = jax.nn.softmax(logits, axis=-1)
            ctx = jnp.einsum('bhqt,bthk->bqhk', weights, vh).reshape(b, q_len, H * K)
            return ctx @ wo + bo

        def _forward(x, xf_1, xf_2, ln1_scale, ln1_offset, wq1, bq1, wk1, bk1, wv1, bv1, wo1, bo1, bias_k1, bias_v1, ln2_scale, ln2_offset, wq2, bq2, wk2, bk2, wv2, bv2, wo2, bo2, bias_k2, bias_v2, ln_mlp_scale, ln_mlp_offset, w_fc1, b_fc1, w_fc2, b_fc2):
            res = x
            h = _layer_norm(x, ln1_scale, ln1_offset)
            x = res + _cross_attention(h, xf_1, wq1, bq1, wk1, bk1, wv1, bv1, wo1, bo1, bias_k1, bias_v1)
            res = x
            h = _layer_norm(x, ln2_scale, ln2_offset)
            x = res + _cross_attention(h, xf_2, wq2, bq2, wk2, bk2, wv2, bv2, wo2, bo2, bias_k2, bias_v2)
            h = _layer_norm(x, ln_mlp_scale, ln_mlp_offset)
            h = jax.nn.gelu(h @ w_fc1 + b_fc1, approximate=False) @ w_fc2 + b_fc2
            return x + h
        return _forward(x, xf_1, xf_2, ln1_scale, ln1_offset, wq1, bq1, wk1, bk1, wv1, bv1, wo1, bo1, bias_k1, bias_v1, ln2_scale, ln2_offset, wq2, bq2, wk2, bk2, wv2, bv2, wo2, bo2, bias_k2, bias_v2, ln_mlp_scale, ln_mlp_offset, w_fc1, b_fc1, w_fc2, b_fc2)
    x = _L0_xattn_ref(x, ctx_2048, L0_xattn_ln1_w, L0_xattn_ln1_b, L0_xattn_ln2_w, L0_xattn_ln2_b, L0_xattn_maa_x, L0_xattn_maa_w1, L0_xattn_maa_w2, L0_xattn_maa_stack, L0_xattn_time_decay, L0_xattn_td_w1, L0_xattn_td_w2, L0_xattn_u, L0_xattn_Wr, L0_xattn_Wk, L0_xattn_Wv, L0_xattn_Wg, L0_xattn_Wo, L0_xattn_gn_w, L0_xattn_gn_b, L0_xattn_ffn_maa_k, L0_xattn_ffn_maa_r, L0_xattn_Wfk, L0_xattn_Wfr, L0_xattn_Wfv)
    x = _L1_xattn_ref(x, ctx_2048, L1_xattn_Wqkv0, L1_xattn_Wqkv1, L1_xattn_Winj0, L1_xattn_Winj1, L1_xattn_Wo, L1_xattn_bo, L1_xattn_r_w_bias)
    x = _L2_xattn_ref(ctx_2048, x, mask_BxS2_ik0, L2_xattn_q_w, L2_xattn_q_b, L2_xattn_kv_w, L2_xattn_kv_b, L2_xattn_out_w, L2_xattn_out_b, L2_xattn_postnorm_w, L2_xattn_mlp_w1, L2_xattn_mlp_b1, L2_xattn_mlp_w2, L2_xattn_mlp_b2)
    x = _L3_xattn_ref(x, ctx_2048, ctx_2048, L3_xattn_ln1_scale, L3_xattn_ln1_offset, L3_xattn_wq1, L3_xattn_bq1, L3_xattn_wk1, L3_xattn_bk1, L3_xattn_wv1, L3_xattn_bv1, L3_xattn_wo1, L3_xattn_bo1, L3_xattn_bias_k1, L3_xattn_bias_v1, L3_xattn_ln2_scale, L3_xattn_ln2_offset, L3_xattn_wq2, L3_xattn_bq2, L3_xattn_wk2, L3_xattn_bk2, L3_xattn_wv2, L3_xattn_bv2, L3_xattn_wo2, L3_xattn_bo2, L3_xattn_bias_k2, L3_xattn_bias_v2, L3_xattn_ln_mlp_scale, L3_xattn_ln_mlp_offset, L3_xattn_w_fc1, L3_xattn_b_fc1, L3_xattn_w_fc2, L3_xattn_b_fc2)
    return x

_drawn_inputs = setup_inputs


def setup_inputs(seed=0):
    import zlib

    import numpy as np

    out = dict(_drawn_inputs(seed))
    spreads = {'L0_xattn_ln1_w': (1.0, 0.568),
     'L0_xattn_ln1_b': (0.0, 0.573),
     'L0_xattn_ln2_w': (1.0, 0.6),
     'L0_xattn_ln2_b': (0.0, 0.8),
     'L0_xattn_gn_w': (1.0, 0.6),
     'L0_xattn_gn_b': (0.0, 0.8),
     'L2_xattn_q_b': (0.0, 0.8),
     'L2_xattn_kv_b': (0.0, 0.8),
     'L2_xattn_out_b': (0.0, 0.654),
     'L2_xattn_postnorm_w': (1.0, 0.6),
     'L2_xattn_mlp_b1': (0.0, 0.1),
     'L2_xattn_mlp_b2': (0.0, 0.1),
     'L3_xattn_ln1_scale': (1.0, 0.6),
     'L3_xattn_ln1_offset': (0.0, 0.8),
     'L3_xattn_bq1': (0.0, 0.8),
     'L3_xattn_bk1': (0.0, 2.0),
     'L3_xattn_bv1': (0.0, 0.1),
     'L3_xattn_bo1': (0.0, 0.1),
     'L3_xattn_ln2_scale': (1.0, 0.6),
     'L3_xattn_ln2_offset': (0.0, 0.8),
     'L3_xattn_bq2': (0.0, 0.8),
     'L3_xattn_bk2': (0.0, 2.0),
     'L3_xattn_bv2': (0.0, 0.1),
     'L3_xattn_bo2': (0.0, 0.1),
     'L3_xattn_ln_mlp_scale': (1.0, 0.6),
     'L3_xattn_ln_mlp_offset': (0.0, 0.78),
     'L3_xattn_b_fc1': (0.0, 0.1),
     'L3_xattn_b_fc2': (0.0, 0.1)}
    factors = {'ctx_2048': 3.046,
     'L0_xattn_maa_x': 8.0,
     'L0_xattn_maa_w1': 7.02,
     'L0_xattn_maa_w2': 7.019,
     'L0_xattn_maa_stack': 2.708,
     'L0_xattn_time_decay': 2.801,
     'L0_xattn_td_w1': 8.0,
     'L0_xattn_td_w2': 8.0,
     'L0_xattn_u': 5.499,
     'L0_xattn_ffn_maa_k': 8.0,
     'L0_xattn_ffn_maa_r': 8.0,
     'L0_xattn_Wfk': 3.064,
     'L0_xattn_Wfr': 8.0,
     'L0_xattn_Wfv': 3.055,
     'L1_xattn_Wqkv0': 8.0,
     'L1_xattn_Wqkv1': 8.0,
     'L1_xattn_Winj0': 8.0,
     'L1_xattn_Winj1': 8.0,
     'L1_xattn_Wo': 6.322,
     'L1_xattn_bo': 104.014,
     'L1_xattn_r_w_bias': 8.0,
     'L2_xattn_q_w': 8.0,
     'L2_xattn_kv_w': 8.0,
     'L2_xattn_out_w': 8.0,
     'L3_xattn_wq1': 8.0,
     'L3_xattn_wk1': 8.0,
     'L3_xattn_wv1': 4.034,
     'L3_xattn_bias_k1': 49.183,
     'L3_xattn_bias_v1': 32.781,
     'L3_xattn_wq2': 8.0,
     'L3_xattn_wk2': 8.0,
     'L3_xattn_wv2': 3.956,
     'L3_xattn_bias_k2': 55.49,
     'L3_xattn_bias_v2': 36.721}
    for name, (base, spread) in spreads.items():
        noise = np.random.default_rng([zlib.crc32(name.encode()), seed]).standard_normal(out[name].shape)
        drawn = base * np.exp(spread * noise) if base else spread * noise
        out[name] = jnp.asarray(drawn.astype(out[name].dtype))
    for name, factor in factors.items():
        out[name] = (out[name] * factor).astype(out[name].dtype)
    return out
```

```python
from contextlib import ExitStack

import numpy as np

import concourse.bass as bass
from concourse import mybir

F32 = mybir.dt.float32
I32 = mybir.dt.int32
ALU = mybir.AluOpType
ACT = mybir.ActivationFunctionType
X_AXIS = mybir.AxisListType.X

P = 128
E = 256
KT = E // P
REGION = 16384


def per_batch(b, count, done):
    return b * count + done


class Semaphores:

    def __init__(self, nc):
        self.nc, self.all = nc, []

    def new(self, name):
        self.all.append(self.nc.alloc_semaphore(name=name))
        return self.all[-1]

    def __enter__(self):
        return self

    def __exit__(self, *_):
        self.nc.clear_and_free_semaphores(self.all)
        self.nc.all_engine_barrier()


class Chain:

    def __init__(self, eng, sem, per, b):
        self.eng, self.sem, self.per, self.b, self.n = eng, sem, per, b, 0

    def link(self, ins):
        self.n += 1
        ins.then_inc(self.sem, 1)
        self.eng.wait_ge(self.sem, per_batch(self.b, self.per, self.n))

    def link_before_aggregate(self, ins):
        self.link(ins)
        self.n += 1
        self.eng.sem_inc(self.sem, 1)

    def close(self):
        assert self.n == self.per, (self.n, self.per)


def rwkv_block(nc, NB, w, work, consts, src, state, v_dram, dst, prefetch):
    G, HS, NH = 2, 8, 16
    NI, N = NB // G, G * P
    MIX = dict(k=0, w=1, v=2, r=3, g=4)
    ORDER = "vkwrg"
    ident, mhalf, pick = consts["ident"], consts["mhalf"], consts["pick"]
    col = w["col"]

    with ExitStack() as st:
        sems = st.enter_context(Semaphores(nc))

        def sb(name, shape, dt=F32):
            return st.enter_context(nc.sbuf_tensor("l0_" + name, shape, dt))

        def sem(name):
            return sems.new("l0_" + name)

        def carve(size):
            work["at"] -= size
            return work["region"][:, work["at"]:work["at"] + size]

        x, xn, x1, out = sb("x", [P, G, E]), sb("xn", [P, G, E]), sb("x1", [P, G, E]), sb("out", [P, G, E])
        first_rows, s0 = sb("first_rows", [2, G, E]), sb("s0", [P, KT, G, HS])
        stats, mv, ve, rstd = sb("stats", [P, G, 6]), sb("mv", [P, G, 2]), sb("ve", [P, G]), sb("rstd", [P, G])
        xa, sx, xx = sb("xa", [P, KT, G, P + 1]), sb("sx", [P, KT, N]), sb("xx", [P, KT, N])
        mix_a, mix_b, mix_tmp = sb("mix_a", [P, N]), sb("mix_b", [32, N]), sb("mix_tmp", [P, 2, KT, N])
        xm = sb("xm", [P, 5, KT, N])
        td, decay_log, decay = sb("td", [64, N]), sb("decay_log", [P, KT, N]), sb("decay", [P, KT, N])
        r, k, v, th, sg = sb("r", [P, KT, N]), sb("k", [P, KT, N]), sb("v", [P, KT, N]), sb("th", [P, KT, N]), sb("sg", [P, KT, N])
        v_rep = [carve(HS * P) for _ in range(2)]
        kv = [carve(HS * P) for _ in range(2)]
        swept = [carve(HS * (P + 1)) for _ in range(2)]
        read_out = [carve(HS * P) for _ in range(2)]
        sums, nmean, sq_sums, gve, grstd = (sb(n, [P, G * KT, NH]) for n in ("sums", "nmean", "sq_sums", "gve", "grstd"))
        state0 = sb("state0", [P, KT, G])
        oc, oc_sq = sb("oc", [P, G, E]), sb("oc_sq", [P, G, E])
        og = sb("og", [P, KT, N])
        xc, sx2, xk2, xr2 = xa, sx, xx, sb("xr2", [P, KT, N])
        relu, kk, rr = sb("relu", [P, KT, N]), sb("kk", [P, KT, N]), sb("rr", [P, G, E])
        bank = [st.enter_context(nc.psum_tensor(f"l0_B{i}", [P, 512], F32)) for i in range(8)]

        USES = [("xt", "vp", "wo"), ("ct", "kp", "xt2"), ("m1", "td1", "rr"), ("m2v", "td2", "kk"), ("m2k", "rp", "kvp"),
                ("m2w", "gp"), ("m2r", "wkv"), ("m2g", "ogt")]
        at = {name: bank[n] for n, names in enumerate(USES) for name in names}
        ready = {name: sem(name + "_ready") for names in USES for name in names}
        used = {name: sem(name + "_used") for names in USES for name in names}
        loaded, s0_loaded, stored = sem("loaded"), sem("s0_loaded"), sem("stored")
        v_stored, v_rep_loaded = sem("v_stored"), [sem(f"v_rep{n}_loaded") for n in range(2)]
        chain_sem, ve_ready, rstd_ready = sem("chain"), sem("ve_ready"), sem("rstd_ready")
        xn_ready, sx_ready, xx_ready = sem("xn_ready"), sem("sx_ready"), sem("xx_ready")
        mix_ready, xm_ready, tmp_ready = sem("mix_ready"), sem("xm_ready"), sem("tmp_ready")
        dlog_ready, decay_ready, th_ready, sg_ready = sem("dlog_ready"), sem("decay_ready"), sem("th_ready"), sem("sg_ready")
        kv_ready, col0_ready, swept_ready, read_ready, out_prod_ready = (sem(n) for n in ("kv_ready", "col0_ready", "swept_ready", "read_ready", "out_prod_ready"))
        units_done = sem("units_done")
        oc_ready, oc_sq_ready, gve_ready, grstd_ready, ocn_ready = (sem(n) for n in ("oc_ready", "oc_sq_ready", "gve_ready", "grstd_ready", "ocn_ready"))
        og1_ready, og_ready, x1_ready = sem("og1_ready"), sem("og_ready"), sem("x1_ready")
        xk2_ready, kk_ready, out_ready = (sem(n) for n in ("xk2_ready", "relu_squared", "out_ready"))
        block = st.enter_context(nc.Block())
        UNITS = [(g, hf) for g in range(G) for hf in range(KT)]
        NU = len(UNITS)

        def by_batch(ap):
            return ap.rearrange("p (g t) -> p g t", g=G)

        @block.sync
        def _(sp):
            with sp.Fori(0, NI) as i:
                sp.wait_ge(x1_ready, i + 1)
                sp.dma_start(x[:], src.rearrange("(n g) t e -> n t g e", g=G)[i]).then_inc(loaded, 16)
                sp.wait_ge(used["ct"], i + 1)
                sp.dma_start(first_rows[:], state.rearrange("(n g) t e -> n t g e", g=G)[i, 0:2]).then_inc(loaded, 16)
                sp.wait_ge(units_done, i + 1)
                for g in range(G):
                    rows = state.rearrange("(n g) t e -> n g (t e)", g=G)[i, g, 2 * E:(2 + HS) * E]
                    sp.dma_start(s0[:, :, g, :], rows.rearrange("(h p j) -> p h j", h=KT, j=HS)).then_inc(s0_loaded, 16)
                sp.wait_ge(used["vp"], i + 2)
                for hf in range(KT):
                    sp.dma_start(v_dram[:, hf * P:(hf + 1) * P, :].rearrange("g c t -> c g t"), by_batch(v[:, hf, :])).then_inc(v_stored, 16)
                sp.wait_ge(v_stored, per_batch(i, 32, 64))
                for n, (g, hf) in enumerate(UNITS):
                    sp.wait_ge(kv_ready, per_batch(i, NU, n + 1))
                    rows = v_dram[g, hf * P:(hf + 1) * P, :].rearrange("(h j) t -> h (j t)", j=HS)
                    sp.dma_start(v_rep[n % 2], rows.unsqueeze(1).broadcast_to([NH, HS, HS * P])).then_inc(v_rep_loaded[n % 2], 16)
                sp.wait_ge(out_ready, i + 1)
                sp.dma_start(dst.rearrange("(n g) t e -> n t g e", g=G)[i], out[:]).then_inc(stored, 16)
            sp.wait_ge(stored, 16 * NI + 16)
            if prefetch:
                prefetch[1](sp)

        @block.tensor
        def _(pe):
            with pe.Fori(0, NI) as i:
                def take(name):
                    names = next(n for n in USES if name in n)
                    k = names.index(name)
                    pe.wait_ge(used[names[k - 1]], i + (2 if k else 1))
                    return at[name]

                def by_channel(name, wt, moving):
                    o = take(name)
                    for ho in range(KT):
                        for kt in range(KT):
                            last = pe.matmul(o[:, ho * N:(ho + 1) * N], wt[:, kt, ho * P:(ho + 1) * P], moving[:, kt, :], start=(kt == 0), stop=(kt == KT - 1))
                    last.then_inc(ready[name], 1)

                def by_token(name, lhs, wt):
                    o = take(name)
                    for g in range(G):
                        for kt in range(KT):
                            last = pe.matmul(o[:, g * E:(g + 1) * E], lhs[:, kt, g * P:(g + 1) * P], wt[:, kt, :], start=(kt == 0), stop=(kt == KT - 1))
                    last.then_inc(ready[name], 1)

                def turn(name, rows):
                    o = take(name)
                    for kt in range(KT):
                        for g in range(G):
                            last = pe.transpose(o[:, kt * N + g * P:kt * N + (g + 1) * P], rows[:, g, kt * P:(kt + 1) * P], ident[:])
                    last.then_inc(ready[name], 1)

                pe.wait_ge(loaded, per_batch(i, 32, 32))
                o = take("ct")
                for kt in range(KT):
                    for g in range(G):
                        c = 2 * (kt * G + g)
                        last = pe.matmul(o[:, c:c + 2], first_rows[:, g, kt * P:(kt + 1) * P], ident[0:2, 0:2], start=True, stop=True)
                last.then_inc(ready["ct"], 1)
                pe.wait_ge(xn_ready, per_batch(i, 2, 1))
                turn("xt", xn)
                pe.wait_ge(xx_ready, i + 1)
                o = take("m1")
                for kt in range(KT):
                    pe.matmul(o[:, 0:N], w["maa_w1"][:, kt, 0:P], xx[:, kt, :], start=(kt == 0), stop=(kt == KT - 1))
                for kt in range(KT):
                    last = pe.matmul(o[0:32, N:2 * N], w["maa_w1"][:, kt, P:P + 32], xx[:, kt, :], start=(kt == 0), stop=(kt == KT - 1))
                last.then_inc(ready["m1"], 1)
                pe.wait_ge(mix_ready, per_batch(i, 2, 2))
                for name in ORDER:
                    f = MIX[name]
                    o = take("m2" + name)
                    wt, mv_, r0 = (w["maa_w2a"], mix_a, 32 * f) if f < 4 else (w["maa_w2b"], mix_b, 0)
                    for ho in range(KT):
                        last = pe.matmul(o[:, ho * N:(ho + 1) * N], wt[r0:r0 + 32, ho * P:(ho + 1) * P], mv_[r0:r0 + 32, :], start=True, stop=True,
                                         tile_position=(r0, 0))
                    last.then_inc(ready["m2" + name], 1)

                def xm_wait(name):
                    pe.wait_ge(xm_ready, per_batch(i, 5, ORDER.index(name) + 1))
                    return xm[:, MIX[name]]

                by_channel("vp", w["wv"], xm_wait("v"))
                by_channel("kp", w["wk"], xm_wait("k"))
                mixed = xm_wait("w")
                o = take("td1")
                for kt in range(KT):
                    last = pe.matmul(o[0:64, 0:N], w["td_w1"][:, kt, :], mixed[:, kt, :], start=(kt == 0), stop=(kt == KT - 1))
                last.then_inc(ready["td1"], 1)
                by_channel("rp", w["wr"], xm_wait("r"))
                pe.wait_ge(used["td1"], i + 2)
                o = take("td2")
                for ho in range(KT):
                    last = pe.matmul(o[:, ho * N:(ho + 1) * N], w["td_w2"][:, ho * P:(ho + 1) * P], td[:], start=True, stop=True)
                last.then_inc(ready["td2"], 1)
                by_channel("gp", w["wg"], xm_wait("g"))
                o = take("wkv")
                for n, (g, hf) in enumerate(UNITS):
                    pe.wait_ge(out_prod_ready, per_batch(i, NU, n + 1))
                    for j in range(HS):
                        c = ((g * KT + hf) * HS + j) * NH
                        last = pe.matmul(o[:, c:c + NH], read_out[n % 2][:, j * P:(j + 1) * P], pick[:], start=True, stop=True)
                    last.then_inc(units_done, 1)
                last = pe.wait_ge(units_done, per_batch(i, NU, NU + 2))
                pe.sem_inc(ready["wkv"], 1)
                pe.wait_ge(ocn_ready, i + 1)
                turn("ogt", oc)
                pe.wait_ge(og_ready, i + 1)
                by_token("wo", og, w["wo"])
                pe.wait_ge(xn_ready, per_batch(i, 2, 2))
                turn("xt2", xn)
                pe.wait_ge(xk2_ready, per_batch(i, 2, 1))
                by_channel("kk", w["wfk"], xk2)
                pe.wait_ge(xk2_ready, per_batch(i, 2, 2))
                by_token("rr", xr2, w["wfr"])
                pe.wait_ge(kk_ready, i + 1)
                by_token("kvp", kk, w["wfv"])

        @block.vector
        def _(dve):
            for name in ("m2v", "m2k", "m2w", "m2r", "m2g", "wkv", "wo", "kvp", "gp"):
                dve.sem_inc(used[name], 1)
            dve.sem_inc(x1_ready, 1)
            dve.sem_inc(kv_ready, 2)
            with dve.Fori(0, NI) as i:
                chain = Chain(dve, chain_sem, 6 + 3 + 2, i)

                def normalise(rows, turn):
                    for g in range(G):
                        last = dve.bn_stats(stats[:, g, :], rows[:, g, :])
                    chain.link_before_aggregate(last)
                    for g in range(G):
                        last = dve.bn_aggr(mv[:, g, :], stats[:, g, :])
                    chain.link(last)
                    dve.tensor_scalar(ve[:], mv[:, :, 1], 1e-5, None, ALU.add).then_inc(ve_ready, 1)
                    dve.wait_ge(rstd_ready, per_batch(i, 2, turn + 1))
                    for g in range(G):
                        last = dve.tensor_scalar(xn[:, g, :], rows[:, g, :], mv[:, g, 0:1], rstd[:, g:g + 1], ALU.subtract, ALU.mult)
                    last.then_inc(xn_ready, 1)

                dve.wait_ge(loaded, per_batch(i, 32, 32))
                normalise(x, 0)
                dve.wait_ge(used["xt"], i + 2)
                dve.wait_ge(used["ct"], i + 2)
                sx4, xx4 = (t[:].rearrange("p k (g t) -> p k g t", g=G) for t in (sx, xx))
                xa_now = xa[:, :, :, 1:P + 1]
                dve.tensor_tensor(sx4, xa[:, :, :, 0:P], xa_now, ALU.subtract).then_inc(sx_ready, 1)
                dve.wait_ge(sx_ready, per_batch(i, 2, 1))
                for hf in range(KT):
                    last = dve.scalar_tensor_tensor(xx4[:, hf], sx4[:, hf], col("maa_x")[:, hf:hf + 1], xa_now[:, hf], ALU.mult, ALU.add)
                last.then_inc(xx_ready, 1)
                for n, name in enumerate(ORDER):
                    f = MIX[name]
                    dve.wait_ge(ready["m2" + name], i + 1)
                    for hf in range(KT):
                        last = dve.scalar_tensor_tensor(mix_tmp[:, n % 2, hf, :], at["m2" + name][:, hf * N:(hf + 1) * N], col(f"stack{f}")[:, hf:hf + 1],
                                                        sx[:, hf, :], ALU.add, ALU.mult)
                    last.then_inc(used["m2" + name], 1)
                    dve.wait_ge(used["m2" + name], i + 2)
                    dve.tensor_tensor(xm[:, f].rearrange("p k (g t) -> p k g t", g=G), mix_tmp[:, n % 2].rearrange("p k (g t) -> p k g t", g=G), xa_now, ALU.add)\
                        .then_inc(xm_ready, 1)
                dve.wait_ge(used["kp"], i + 2)
                dve.wait_ge(s0_loaded, per_batch(i, 32, 32))
                for n, (g, hf) in enumerate(UNITS):
                    p = n % 2
                    sw = swept[p].rearrange("p (j t) -> p j t", j=HS)
                    kv3, vr3, ro3 = (t[p].rearrange("p (j t) -> p j t", j=HS) for t in (kv, v_rep, read_out))
                    now = slice(g * P, (g + 1) * P)
                    dve.wait_ge(v_rep_loaded[p], per_batch(i, 32, 16 * (n // 2) + 16))
                    dve.tensor_tensor(kv3, vr3, k[:, hf, now].unsqueeze(1).broadcast_to([P, HS, P]), ALU.mult).then_inc(kv_ready, 1)
                    dve.tensor_copy(sw[:, :, 0], s0[:, hf, g, :]).then_inc(col0_ready, 1)
                    dve.wait_ge(kv_ready, per_batch(i, NU, n + 3))
                    dve.wait_ge(col0_ready, per_batch(i, NU, n + 1))
                    if n == 0:
                        dve.wait_ge(decay_ready, i + 1)
                    for j in range(HS):
                        last = dve.tensor_tensor_scan(sw[:, j, 1:P + 1], decay[:, hf, now], kv3[:, j, :], sw[:, j, 0:1], ALU.mult, ALU.add)
                    last.then_inc(swept_ready, 1)
                    dve.wait_ge(swept_ready, per_batch(i, NU, n + 1))
                    dve.wait_ge(units_done, per_batch(i, NU, n + 1))
                    dve.scalar_tensor_tensor(ro3, kv3, col("u")[:, hf:hf + 1], sw[:, :, 0:P], ALU.mult, ALU.add).then_inc(read_ready, 1)
                dve.wait_ge(th_ready, per_batch(i, 2, 1))
                dve.scalar_tensor_tensor(sg[:].rearrange("p k n -> p (k n)"), th[:].rearrange("p k n -> p (k n)"), 1.0, at["gp"][:], ALU.add, ALU.mult)\
                    .then_inc(used["gp"], 1)
                dve.wait_ge(ready["wkv"], i + 1)
                heads = at["wkv"][:].rearrange("p (a j h) -> p a h j", a=G * KT, j=HS)
                oc4 = oc[:].rearrange("p g (k h j) -> p (g k) h j", k=KT, j=HS)
                chain.link(dve.tensor_reduce(sums[:], heads, X_AXIS, ALU.add))
                chain.link(dve.tensor_scalar(nmean[:], sums[:], -1.0 / HS, None, ALU.mult))
                dve.tensor_tensor(oc4, heads, nmean[:].unsqueeze(3).broadcast_to([P, G * KT, NH, HS]), ALU.add).then_inc(oc_ready, 1)
                dve.wait_ge(oc_sq_ready, i + 1)
                dve.sem_inc(used["wkv"], 1)
                chain.link(dve.tensor_reduce(sq_sums[:], oc_sq[:].rearrange("p g (k h j) -> p (g k) h j", k=KT, j=HS), X_AXIS, ALU.add))
                dve.tensor_scalar(gve[:], sq_sums[:], 1.0 / HS, 1e-5, ALU.mult, ALU.add).then_inc(gve_ready, 1)
                dve.wait_ge(grstd_ready, i + 1)
                dve.tensor_tensor(oc4, oc4, grstd[:].unsqueeze(3).broadcast_to([P, G * KT, NH, HS]), ALU.mult).then_inc(ocn_ready, 1)
                dve.wait_ge(used["ogt"], i + 2)
                dve.wait_ge(used["gp"], i + 2)
                dve.scalar_tensor_tensor(og[:], og[:], 0.5, sg[:], ALU.mult, ALU.mult).then_inc(og_ready, 1)
                dve.wait_ge(ready["wo"], i + 1)
                dve.tensor_tensor(x1[:], at["wo"][:].rearrange("p (g e) -> p g e", g=G), x[:], ALU.add).then_inc(used["wo"], 1)
                dve.wait_ge(used["wo"], i + 2)
                dve.sem_inc(x1_ready, 1)
                normalise(x1, 1)
                dve.wait_ge(used["xt2"], i + 2)
                dve.tensor_tensor(sx4, xc[:, :, :, 0:P], xa_now, ALU.subtract).then_inc(sx_ready, 1)
                dve.wait_ge(sx_ready, per_batch(i, 2, 2))
                for name, to in (("ffn_k", xk2), ("ffn_r", xr2)):
                    to4 = to[:].rearrange("p k (g t) -> p k g t", g=G)
                    for hf in range(KT):
                        last = dve.scalar_tensor_tensor(to4[:, hf], sx4[:, hf], col(name)[:, hf:hf + 1], xa_now[:, hf], ALU.mult, ALU.add)
                    last.then_inc(xk2_ready, 1)
                dve.wait_ge(used["rr"], i + 2)
                chain.link(dve.tensor_scalar(rr[:], rr[:], 0.5, 0.5, ALU.mult, ALU.add))
                dve.wait_ge(ready["kvp"], i + 1)
                chain.link(dve.tensor_tensor(rr[:], at["kvp"][:].rearrange("p (g e) -> p g e", g=G), rr[:], ALU.mult))
                dve.sem_inc(used["kvp"], 1)
                dve.wait_ge(stored, per_batch(i, 16, 16))
                dve.tensor_tensor(out[:], rr[:], x1[:], ALU.add).then_inc(out_ready, 1)
                chain.close()

        @block.gpsimd
        def _(pool):
            pool.sem_inc(stored, 16)
            pool.sem_inc(v_stored, 32)
            if prefetch:
                prefetch[0](pool)
            with pool.Fori(0, NI) as i:
                pool.wait_ge(ve_ready, per_batch(i, 2, 1))
                pool.tensor_tensor(rstd[:], ve[:], mhalf[:, 0:G], ALU.pow).then_inc(rstd_ready, 1)
                pool.wait_ge(used["rp"], i + 2)
                for n, (g, hf) in enumerate(UNITS):
                    pool.wait_ge(read_ready, per_batch(i, NU, n + 1))
                    ro3 = read_out[n % 2].rearrange("p (j t) -> p j t", j=HS)
                    pool.tensor_tensor(ro3, ro3, r[:, hf, g * P:(g + 1) * P].unsqueeze(1).broadcast_to([P, HS, P]), ALU.mult).then_inc(out_prod_ready, 1)
                pool.wait_ge(gve_ready, i + 1)
                pool.tensor_tensor(grstd[:], gve[:], mhalf[:, 0:G * KT * NH].rearrange("p (a h) -> p a h", h=NH), ALU.pow).then_inc(grstd_ready, 1)
                pool.wait_ge(ve_ready, per_batch(i, 2, 2))
                pool.tensor_tensor(rstd[:], ve[:], mhalf[:, 0:G], ALU.pow).then_inc(rstd_ready, 1)

        @block.scalar
        def _(act):
            for name in ("xt", "ct", "m1", "vp", "kp", "td1", "td2", "rp", "ogt", "xt2", "rr", "kk"):
                act.sem_inc(used[name], 1)
            act.sem_inc(units_done, 2)
            with act.Fori(0, NI) as i:
                def got(name):
                    act.wait_ge(ready[name], i + 1)
                    return at[name]

                first = got("ct")[:, 0:2 * KT * G].rearrange("p (k g r) -> p k g r", k=KT, g=G)
                act.activation(xa[:, :, :, 0], first[:, :, :, 1], ACT.Copy)
                act.activation(state0[:], first[:, :, :, 0], ACT.Copy).then_inc(used["ct"], 1)
                o = got("xt")
                for hf in range(KT):
                    last = act.activation(xa[:, hf, :, 1:P + 1], by_batch(o[:, hf * N:(hf + 1) * N]), ACT.Identity, bias=col("ln1_b")[:, hf:hf + 1], scale=col("ln1_w")[:, hf:hf + 1])
                last.then_inc(used["xt"], 1)
                o = got("m1")
                act.activation(mix_a[:], o[:, 0:N], ACT.Tanh).then_inc(mix_ready, 1)
                act.activation(mix_b[:], o[0:32, N:2 * N], ACT.Tanh).then_inc(mix_ready, 1)
                act.wait_ge(mix_ready, per_batch(i, 2, 2))
                act.sem_inc(used["m1"], 1)
                act.wait_ge(v_stored, per_batch(i, 32, 32))
                act.activation(v[:].rearrange("p k n -> p (k n)"), got("vp")[:], ACT.Copy).then_inc(used["vp"], 1)
                act.activation(k[:].rearrange("p k n -> p (k n)"), got("kp")[:], ACT.Copy).then_inc(used["kp"], 1)
                act.activation(td[:], got("td1")[0:64, 0:N], ACT.Tanh).then_inc(used["td1"], 1)
                act.activation(r[:].rearrange("p k n -> p (k n)"), got("rp")[:], ACT.Copy).then_inc(used["rp"], 1)
                o = got("td2")
                for hf in range(KT):
                    last = act.activation(decay_log[:, hf, :], o[:, hf * N:(hf + 1) * N], ACT.Exp, bias=col("time_decay")[:, hf:hf + 1])
                last.then_inc(used["td2"], 1)
                act.wait_ge(used["td2"], i + 2)
                act.activation(decay[:], decay_log[:], ACT.Exp, scale=-1.0).then_inc(decay_ready, 1)
                act.activation(th[:].rearrange("p k n -> p (k n)"), got("gp")[:], ACT.Tanh, scale=0.5).then_inc(th_ready, 1)
                act.wait_ge(oc_ready, i + 1)
                act.activation(oc_sq[:], oc[:], ACT.Square).then_inc(oc_sq_ready, 1)
                o = got("ogt")
                for hf in range(KT):
                    last = act.activation(og[:, hf, :], o[:, hf * N:(hf + 1) * N], ACT.Identity, bias=col("gn_b")[:, hf:hf + 1], scale=col("gn_w")[:, hf:hf + 1])
                last.then_inc(used["ogt"], 1)
                o = got("xt2")
                act.activation(xc[:, :, :, 0], state0[:], ACT.Copy)
                for hf in range(KT):
                    last = act.activation(xc[:, hf, :, 1:P + 1], by_batch(o[:, hf * N:(hf + 1) * N]), ACT.Identity, bias=col("ln2_b")[:, hf:hf + 1], scale=col("ln2_w")[:, hf:hf + 1])
                last.then_inc(used["xt2"], 1)
                act.activation(relu[:].rearrange("p k n -> p (k n)"), got("kk")[:], ACT.Relu).then_inc(used["kk"], 1)
                act.wait_ge(used["kk"], i + 2)
                act.activation(kk[:], relu[:], ACT.Square).then_inc(kk_ready, 1)
                act.activation(rr[:].rearrange("p g e -> p (g e)"), got("rr")[:], ACT.Tanh, scale=0.5).then_inc(used["rr"], 1)
                act.sem_inc(th_ready, 1)


def deq_attention(nc, NB, w, consts, src, ctx_in, dst, prefetch):
    H, D, L = 16, 64, 256
    M = H * D // P
    ident, ones, mhalf = consts["ident"], consts["ones"], consts["mhalf"]
    Q0, K0, V0, TA0, WO, MEAN, VAR, BCAST, NJ = 0, 4, 8, 12, 16, 17, 18, 19, 20
    HJ = NJ // 2

    with ExitStack() as st:
        sems = st.enter_context(Semaphores(nc))

        def sb(name, shape, dt=F32):
            return st.enter_context(nc.sbuf_tensor("l1_" + name, shape, dt))

        def sem(name):
            return sems.new("l1_" + name)

        z, u, z_res = sb("z", [P, L]), sb("u", [P, L]), sb("z_res", [P, L])
        qT, kT, v = sb("qT", [P, M, L]), sb("kT", [P, M, L]), sb("v", [P, 2, H * D])
        bias8 = sb("bias8", [P, M])
        prob, probT = sb("prob", [P, 2, 2, L]), sb("probT", [P, 2, 2, L])
        negmax, rowsum, rinv = sb("negmax", [P, H, 2]), sb("rowsum", [P, H, 2]), sb("rinv", [P, H, 2])
        att, attT = sb("att", [P, 2, H * D]), sb("attT", [P, M, L])
        x1, mean, xc, sq = sb("x1", [P, L]), sb("mean", [P, L]), sb("xc", [P, L]), sb("sq", [P, L])
        var, rstd, diag, rb, out = sb("var", [P, 2]), sb("rstd", [P, 2]), sb("diag", [P, 2, P]), sb("rb", [P, L]), sb("out", [P, L])
        J = [st.enter_context(nc.psum_tensor(f"l1_J{i}", [P, 512], F32)) for i in range(2)]
        S = [st.enter_context(nc.psum_tensor(f"l1_S{i}", [P, 2, L], F32)) for i in range(2)]
        T = [st.enter_context(nc.psum_tensor(f"l1_T{i}", [P, 2, L], F32)) for i in range(2)]
        A = [st.enter_context(nc.psum_tensor(f"l1_A{i}", [P, 2, 4, D], F32)) for i in range(2)]

        zu_loaded, zres_loaded, stored = sem("zu_loaded"), sem("zres_loaded"), sem("stored")
        bias_scaled = sem("bias_scaled")
        j_ready = sem("j_ready")
        j_used = [sem("j0_used"), sem("j1_used")]
        scores_ready = sem("scores_ready")
        max_ready = sem("max_ready")
        exp_done = sem("exp_done")
        t_ready = sem("t_ready")
        probT_ready = [sem("probT0_ready"), sem("probT1_ready")]
        pv_done = sem("pv_done")
        att_ready = sem("att_ready")
        rinv_ready = sem("rinv_ready")
        xc_ready, sq_ready, x1_ready = sem("xc_ready"), sem("sq_ready"), sem("x1_ready")
        var_ready, rstd_ready, diag_ready, out_ready = sem("var_ready"), sem("rstd_ready"), sem("diag_ready"), sem("out_ready")
        block = st.enter_context(nc.Block())

        @block.sync
        def _(sp):
            with sp.Fori(0, NB) as b:
                sp.wait_ge(j_ready, per_batch(b, NJ, 1))
                sp.dma_start(z[:], src[b]).then_inc(zu_loaded, 16)
                sp.dma_start(u[:], ctx_in[b]).then_inc(zu_loaded, 16)
                sp.wait_ge(x1_ready, b + 1)
                sp.dma_start(z_res[:], src[b]).then_inc(zres_loaded, 16)
                sp.wait_ge(out_ready, b + 1)
                sp.dma_start(dst[b], out[:]).then_inc(stored, 16)
            sp.wait_ge(stored, 16 * NB + 16)
            if prefetch:
                prefetch[1](sp)

        @block.tensor
        def _(pe):
            pe.sem_inc(t_ready, 2)
            pe.sem_inc(pv_done, 2)
            pe.sem_inc(j_ready, 1)

            with pe.Fori(0, NB) as b:
                def j_free(g):
                    pe.wait_ge(j_used[g % 2], per_batch(b, HJ, g // 2 + 1))

                def j_evacuated(g):
                    pe.wait_ge(j_used[g % 2], per_batch(b, HJ, g // 2 + 2))

                pe.wait_ge(zu_loaded, per_batch(b, 32, 32))
                for g in range(TA0):
                    bank = J[g % 2]
                    j_free(g)
                    if g < V0:
                        for mm in range(2):
                            m = 2 * (g % 4) + mm
                            f0 = (0 if g < K0 else H * D) + m * P
                            for s in range(2):
                                o = bank[:, mm * L + s * P:mm * L + (s + 1) * P]
                                pe.matmul(o, w["wq"][s][:, f0:f0 + P], z[:, s * P:(s + 1) * P], start=True, stop=False)
                                last = pe.matmul(o, w["wi"][s][:, f0:f0 + P], u[:, s * P:(s + 1) * P], start=False, stop=True)
                    else:
                        s, c = (g - V0) // 2, (g - V0) % 2
                        f0 = 2 * H * D + c * 512
                        pe.matmul(bank[:], z[:, s * P:(s + 1) * P], w["wq"][s][:, f0:f0 + 512], start=True, stop=False)
                        last = pe.matmul(bank[:], u[:, s * P:(s + 1) * P], w["wi"][s][:, f0:f0 + 512], start=False, stop=True)
                    last.then_inc(j_ready, 1)

                def scores(n):
                    m, r0 = n // 2, D * (n % 2)
                    pe.wait_ge(exp_done, per_batch(b, H, n + 1))
                    for it in range(2):
                        last = pe.matmul(S[n % 2][:, it, :], qT[r0:r0 + D, m, it * P:(it + 1) * P], kT[r0:r0 + D, m, :], start=True, stop=True)
                    last.then_inc(scores_ready, 1)

                def transposes(n):
                    pe.wait_ge(exp_done, per_batch(b, H, n + 3))
                    pe.wait_ge(probT_ready[n % 2], per_batch(b, H // 2, n // 2 + 1))
                    for jt in range(2):
                        for it in range(2):
                            last = pe.transpose(T[n % 2][:, jt, it * P:(it + 1) * P], prob[:, n % 2, it, jt * P:(jt + 1) * P], ident[:])
                    last.then_inc(t_ready, 1)

                def attend(n):
                    a = n // 4
                    pe.wait_ge(probT_ready[n % 2], per_batch(b, H // 2, n // 2 + 2))
                    if n % 4 == 0:
                        pe.wait_ge(att_ready, per_batch(b, 4, a + 1))
                    for it in range(2):
                        for jt in range(2):
                            last = pe.matmul(A[a % 2][:, it, n % 4, :], probT[:, n % 2, jt, it * P:(it + 1) * P],
                                             v[:, jt, n * D:(n + 1) * D], start=(jt == 0), stop=(jt == 1))
                    last.then_inc(pv_done, 1)

                def turn_attended(a):
                    g = TA0 + a
                    j_free(g)
                    pe.wait_ge(att_ready, per_batch(b, 4, a + 3))
                    for c in range(2):
                        for it in range(2):
                            last = pe.transpose(J[g % 2][:, c * L + it * P:c * L + (it + 1) * P],
                                                att[:, it, (2 * a + c) * P:(2 * a + c + 1) * P], ident[:])
                    last.then_inc(j_ready, 1)

                j_evacuated(K0 + 2), j_evacuated(K0 + 3)
                for n in range(H + 3):
                    if n < H:
                        scores(n)
                    if 1 <= n <= H:
                        transposes(n - 1)
                    if n == 2:
                        j_evacuated(V0 + 2), j_evacuated(V0 + 3)
                    if 2 <= n < H + 2:
                        attend(n - 2)
                    if n >= 6 and n % 4 == 2:
                        turn_attended((n - 6) // 4)
                j_evacuated(TA0 + 2), j_evacuated(TA0 + 3)
                for kt in range(M):
                    last = pe.matmul(J[WO % 2][:, :L], w["wo"][:, kt, :], attT[:, kt, :], start=(kt == 0), stop=(kt == M - 1))
                last.then_inc(j_ready, 1)
                j_free(MEAN)
                pe.wait_ge(x1_ready, b + 2)
                pe.matmul(J[MEAN % 2][:, :L], ones[:], x1[:], start=True, stop=True).then_inc(j_ready, 1)
                j_free(VAR)
                pe.wait_ge(sq_ready, b + 1)
                for c in range(2):
                    last = pe.matmul(J[VAR % 2][:, c:c + 1], sq[:, c * P:(c + 1) * P], ones[:, 0:1], start=True, stop=True)
                last.then_inc(j_ready, 1)
                j_free(BCAST)
                pe.wait_ge(diag_ready, b + 1)
                for c in range(2):
                    last = pe.matmul(J[BCAST % 2][:, c * P:(c + 1) * P], consts["full1"][:], diag[:, c, :], start=True, stop=True)
                last.then_inc(j_ready, 1)

        @block.vector
        def _(dve):
            dve.tensor_scalar(bias8[:], w["bias"], 0.125, None, ALU.mult).then_inc(bias_scaled, 1)
            dve.sem_inc(j_used[0], 1)
            dve.sem_inc(probT_ready[0], 1)
            dve.sem_inc(att_ready, 2)
            dve.sem_inc(x1_ready, 1)

            with dve.Fori(0, NB) as b:
                def j_wait(g):
                    dve.wait_ge(j_ready, per_batch(b, NJ, g + 2))

                for g in range(0, TA0, 2):
                    j_wait(g)
                    if g < K0:
                        for mm in range(2):
                            m = 2 * g + mm
                            last = dve.tensor_scalar(qT[:, m, :], J[0][:, mm * L:(mm + 1) * L], w["bias"][:, m:m + 1], 0.125, ALU.add, ALU.mult)
                    elif g < V0:
                        m = 2 * (g - K0)
                        last = dve.tensor_copy(kT[:, m:m + 2, :], J[0][:].rearrange("p (m l) -> p m l", m=2))
                    else:
                        s = (g - V0) // 2
                        last = dve.tensor_copy(v[:, s, 0:512], J[0][:])
                    last.then_inc(j_used[0], 1)

                for n in range(H + 4):
                    if n < H:
                        dve.wait_ge(scores_ready, per_batch(b, H, n + 1))
                        dve.tensor_reduce(negmax[:, n, :], S[n % 2][:], X_AXIS, ALU.max, negate=True).then_inc(max_ready, 1)
                    if 1 <= n <= H and (n - 1) % 2 == 0:
                        h = n - 1
                        dve.wait_ge(t_ready, per_batch(b, H, h + 3))
                        dve.wait_ge(pv_done, per_batch(b, H, h + 1))
                        dve.tensor_copy(probT[:, 0], T[0][:]).then_inc(probT_ready[0], 1)
                    if n >= 6 and (n - 6) % 4 == 0:
                        a = (n - 6) // 4
                        dve.wait_ge(pv_done, per_batch(b, H, 4 * a + 6))
                        dve.reciprocal(rinv[:, 4 * a:4 * a + 4, :], rowsum[:, 4 * a:4 * a + 4, :]).then_inc(rinv_ready, 1)
                        dve.wait_ge(rinv_ready, per_batch(b, 4, a + 1))
                        dve.tensor_tensor(att[:, :, 4 * a * D:(4 * a + 4) * D].rearrange("p i (h d) -> p i h d", h=4), A[a % 2][:],
                                          rinv[:, 4 * a:4 * a + 4, :].rearrange("p h i -> p i h").unsqueeze(3).broadcast_to([P, 2, 4, D]),
                                          ALU.mult).then_inc(att_ready, 1)
                    if n in (8, 16):
                        a = (n - 8) // 4
                        j_wait(TA0 + a)
                        dve.tensor_copy(attT[:, 2 * a:2 * a + 2, :], J[0][:].rearrange("p (c l) -> p c l", c=2)).then_inc(j_used[0], 1)
                j_wait(WO)
                dve.wait_ge(zres_loaded, per_batch(b, 16, 16))
                dve.scalar_tensor_tensor(x1[:], J[0][:, :L], w["bo"], z_res[:], ALU.add, ALU.add).then_inc(x1_ready, 1)
                dve.wait_ge(x1_ready, b + 2)
                dve.sem_inc(j_used[0], 1)
                dve.wait_ge(j_used[1], per_batch(b, HJ, MEAN // 2 + 2))
                dve.tensor_tensor(xc[:], x1[:], mean[:], ALU.subtract).then_inc(xc_ready, 1)
                j_wait(VAR)
                dve.tensor_scalar(var[:], J[0][:, 0:2], 1e-5, None, ALU.add).then_inc(var_ready, 1)
                dve.wait_ge(var_ready, b + 1)
                dve.sem_inc(j_used[0], 1)
                dve.wait_ge(rstd_ready, b + 1)
                for c in range(2):
                    last = dve.tensor_scalar(diag[:, c, :], ident[:], rstd[:, c:c + 1], None, ALU.mult)
                last.then_inc(diag_ready, 1)
                dve.wait_ge(j_used[1], per_batch(b, HJ, BCAST // 2 + 2))
                dve.wait_ge(stored, per_batch(b, 16, 16))
                dve.tensor_tensor(out[:], xc[:], rb[:], ALU.mult).then_inc(out_ready, 1)

        @block.gpsimd
        def _(pool):
            pool.sem_inc(stored, 16)
            if prefetch:
                prefetch[0](pool)
            with pool.Fori(0, NB) as b:
                pool.wait_ge(var_ready, b + 1)
                pool.tensor_tensor(rstd[:], var[:], mhalf[:, 0:2], ALU.pow).then_inc(rstd_ready, 1)

        @block.scalar
        def _(act):
            act.sem_inc(j_used[1], 1)
            act.sem_inc(probT_ready[1], 1)
            act.sem_inc(exp_done, 2)
            act.wait_ge(bias_scaled, 1)

            with act.Fori(0, NB) as b:
                def j_wait(g):
                    act.wait_ge(j_ready, per_batch(b, NJ, g + 2))

                for g in range(1, TA0, 2):
                    j_wait(g)
                    if g < K0:
                        for mm in range(2):
                            m = 2 * g + mm
                            last = act.activation(qT[:, m, :], J[1][:, mm * L:(mm + 1) * L], ACT.Identity, bias=bias8[:, m:m + 1], scale=0.125)
                    elif g < V0:
                        m = 2 * (g - K0)
                        last = act.activation(kT[:, m:m + 2, :], J[1][:].rearrange("p (m l) -> p m l", m=2), ACT.Copy)
                    else:
                        s = (g - V0) // 2
                        last = act.activation(v[:, s, 512:1024], J[1][:], ACT.Copy)
                    last.then_inc(j_used[1], 1)

                for n in range(H + 5):
                    if n < H:
                        act.wait_ge(max_ready, per_batch(b, H, n + 1))
                        act.wait_ge(t_ready, per_batch(b, H, n + 1))
                        for it in range(2):
                            last = act.activation(prob[:, n % 2, it, :], S[n % 2][:, it, :], ACT.Exp, bias=negmax[:, n, it:it + 1],
                                                  accum_out=rowsum[:, n, it:it + 1])
                        last.then_inc(exp_done, 1)
                    if 2 <= n <= H + 1 and (n - 2) % 2 == 1 or n == H + 1:
                        h = n - 2
                        act.wait_ge(t_ready, per_batch(b, H, h + 3))
                        act.wait_ge(pv_done, per_batch(b, H, h + 1))
                        act.activation(probT[:, 1], T[1][:], ACT.Copy).then_inc(probT_ready[1], 1)
                    if n in (12, 20):
                        a = (n - 8) // 4
                        j_wait(TA0 + a)
                        act.activation(attT[:, 2 * a:2 * a + 2, :], J[1][:].rearrange("p (c l) -> p c l", c=2), ACT.Copy).then_inc(j_used[1], 1)
                j_wait(MEAN)
                act.activation(mean[:], J[1][:, :L], ACT.Copy).then_inc(j_used[1], 1)
                act.wait_ge(xc_ready, b + 1)
                act.activation(sq[:], xc[:], ACT.Square).then_inc(sq_ready, 1)
                j_wait(BCAST)
                act.activation(rb[:], J[1][:, :L], ACT.Copy).then_inc(j_used[1], 1)


def perceiver_attention(nc, NB, w, consts, src, kv_in, mask, row16_in, dst, prefetch):
    H, D, NK = 16, 16, 2 * P
    M = H // 4
    ident, mhalf = consts["ident"], consts["mhalf"]
    CTX_T, LAT_T, K0, V, Q, AT_T, OUT, NJ = 0, 1, 2, 4, 5, 6, 7, 8
    HJ = NJ // 2
    NP = H // 2

    def head(n, i):
        m, g = 2 * (n // 4) + i, n % 4
        return m, g, 4 * m + g

    with ExitStack() as st:
        sems = st.enter_context(Semaphores(nc))

        def sb(name, shape, dt=F32):
            return st.enter_context(nc.sbuf_tensor("l2_" + name, shape, dt))

        def sem(name):
            return sems.new("l2_" + name)

        lat, ctx, resid = sb("lat", [P, E]), sb("ctx", [P, E]), sb("resid", [P, E])
        allT = sb("allT", [P, KT, NK])
        qT, kT, v = sb("qT", [P, M, P]), sb("kT", [P, M, NK]), sb("v", [P, 2, E])
        prob, probT = sb("prob", [P, 2, 2, NK]), sb("probT", [P, 2, 2, 2, P])
        negmax, rowsum, rinv = sb("negmax", [P, NP, 2]), sb("rowsum", [P, NP, 2]), sb("rinv", [P, NP, 2])
        att_out = sb("att_out", [P, E])
        att, attT, out = sb("att", [P, E]), sb("attT", [P, KT, P]), sb("out", [P, E])
        J = [st.enter_context(nc.psum_tensor(f"l2_J{i}", [P, 512], F32)) for i in range(2)]
        S = [st.enter_context(nc.psum_tensor(f"l2_S{i}", [P, 2, NK], F32)) for i in range(2)]
        T = [st.enter_context(nc.psum_tensor(f"l2_T{i}", [P, 2, 2, P], F32)) for i in range(2)]
        A = st.enter_context(nc.psum_tensor("l2_A", [P, 512], F32))

        mask_in, mask_bias = sb("mask_in", [1, NB * P], I32), sb("mask_bias", [1, NB * P])
        row16, qb16 = sb("row16", [1, 512]), sb("qb16", [P, M])
        mask_loaded, mask_set, qb16_set = sem("mask_loaded"), sem("mask_set"), sem("qb16_set")
        loaded, stored = sem("loaded"), sem("stored")
        j_ready = sem("j_ready")
        j_used = [sem("j0_used"), sem("j1_used")]
        scores_ready, max_ready, exp_done, t_ready, pv_done = sem("scores_ready"), sem("max_ready"), sem("exp_done"), sem("t_ready"), sem("pv_done")
        probT_ready = [sem("probT0_ready"), sem("probT1_ready")]
        rinv_ready, att_ready, out_ready, resid_ready, att_out_ready = sem("rinv_ready"), sem("att_ready"), sem("out_ready"), sem("resid_ready"), sem("att_out_ready")
        block = st.enter_context(nc.Block())

        @block.sync
        def _(sp):
            sp.dma_start(mask_in[:], mask).then_inc(mask_loaded, 16)
            sp.dma_start(row16[:], row16_in).then_inc(mask_loaded, 16)
            with sp.Fori(0, NB) as b:
                sp.wait_ge(resid_ready, b + 1)
                sp.wait_ge(j_ready, per_batch(b, NJ, 1))
                sp.dma_start(lat[:], src[b]).then_inc(loaded, 16)
                sp.dma_start(ctx[:], kv_in[b]).then_inc(loaded, 16)
                sp.wait_ge(out_ready, b + 1)
                sp.dma_start(dst[b], out[:]).then_inc(stored, 16)
            sp.wait_ge(stored, 16 * NB + 16)
            if prefetch:
                prefetch[1](sp)

        @block.tensor
        def _(pe):
            pe.sem_inc(j_ready, 1)
            pe.sem_inc(t_ready, 2)
            pe.sem_inc(pv_done, 2)
            pe.wait_ge(mask_set, 1)
            with pe.Fori(0, NB) as b:
                def j_free(g):
                    pe.wait_ge(j_used[g % 2], per_batch(b, HJ, g // 2 + 1))

                def j_evacuated(g):
                    pe.wait_ge(j_used[g % 2], per_batch(b, HJ, g // 2 + 2))

                pe.wait_ge(loaded, per_batch(b, 32, 32))
                for g, rows in ((CTX_T, ctx), (LAT_T, lat)):
                    j_free(g)
                    for kt in range(KT):
                        last = pe.transpose(J[g][:, kt * P:(kt + 1) * P], rows[:, kt * P:(kt + 1) * P], ident[:])
                    last.then_inc(j_ready, 1)
                j_evacuated(CTX_T), j_evacuated(LAT_T)
                for g in (K0, K0 + 1):
                    j_free(g)
                    for mm in range(2):
                        m = 2 * (g - K0) + mm
                        o = J[g % 2][:, mm * NK:(mm + 1) * NK]
                        for kt in range(KT):
                            pe.matmul(o, w["kw"][:, kt, m * P:(m + 1) * P], allT[:, kt, :], start=(kt == 0), stop=False)
                        last = pe.matmul(o[:, 0:P], row16[:, m * P:(m + 1) * P], mask_bias[0:1, bass.ds(b * P, P)], start=False, stop=True)
                    last.then_inc(j_ready, 1)
                j_free(V)
                for n in range(2):
                    for kt in range(KT):
                        last = pe.matmul(J[V % 2][:, n * E:(n + 1) * E], allT[:, kt, n * P:(n + 1) * P], w["vw"][:, kt, :], start=(kt == 0), stop=(kt == KT - 1))
                last.then_inc(j_ready, 1)
                j_free(Q)
                for m in range(M):
                    for kt in range(KT):
                        last = pe.matmul(J[Q % 2][:, m * P:(m + 1) * P], w["qw"][:, kt, m * P:(m + 1) * P], allT[:, kt, P:NK], start=(kt == 0), stop=(kt == KT - 1))
                last.then_inc(j_ready, 1)

                def scores(n):
                    pe.wait_ge(exp_done, per_batch(b, NP, n + 1))
                    for i in range(2):
                        m, g, _ = head(n, i)
                        last = pe.matmul(S[n % 2][:, i, :], qT[32 * g:32 * g + 32, m, :], kT[32 * g:32 * g + 32, m, :], start=True, stop=True,
                                         tile_position=(32 * g, 0))
                    last.then_inc(scores_ready, 1)

                def turn(n):
                    pe.wait_ge(exp_done, per_batch(b, NP, n + 3))
                    pe.wait_ge(probT_ready[n % 2], per_batch(b, NP // 2, n // 2 + 1))
                    for i in range(2):
                        for t in range(2):
                            last = pe.transpose(T[n % 2][:, i, t, :], prob[:, n % 2, i, t * P:(t + 1) * P], ident[:])
                    last.then_inc(t_ready, 1)

                def attend(n):
                    pe.wait_ge(probT_ready[n % 2], per_batch(b, NP // 2, n // 2 + 2))
                    for i in range(2):
                        _, _, h = head(n, i)
                        for t in range(2):
                            last = pe.matmul(A[:, h * D:(h + 1) * D], probT[:, n % 2, i, t, :], v[:, t, h * D:(h + 1) * D], start=(t == 0), stop=(t == 1))
                    last.then_inc(pv_done, 1)

                j_evacuated(K0), j_evacuated(K0 + 1), j_evacuated(Q)
                for n in range(NP + 2):
                    if n < NP:
                        scores(n)
                    if 1 <= n <= NP:
                        turn(n - 1)
                    if n == 2:
                        j_evacuated(V)
                        pe.wait_ge(att_ready, b + 1)
                    if n >= 2:
                        attend(n - 2)
                j_free(AT_T)
                pe.wait_ge(att_ready, b + 2)
                for kt in range(KT):
                    last = pe.transpose(J[AT_T % 2][:, kt * P:(kt + 1) * P], att[:, kt * P:(kt + 1) * P], ident[:])
                last.then_inc(j_ready, 1)
                j_free(OUT)
                j_evacuated(AT_T)
                for kt in range(KT):
                    last = pe.matmul(J[OUT % 2][:, 0:E], attT[:, kt, :], w["ow"][:, kt, :], start=(kt == 0), stop=(kt == KT - 1))
                last.then_inc(j_ready, 1)

        @block.vector
        def _(dve):
            dve.wait_ge(mask_loaded, 32)
            dve.tensor_scalar(mask_bias[:], mask_in[:], 0.0, -1e30, ALU.is_equal, ALU.mult).then_inc(mask_set, 1)
            dve.tensor_scalar(qb16[:], w["qb"], 1.0 / D, None, ALU.mult).then_inc(qb16_set, 1)
            dve.sem_inc(j_used[0], 1)
            dve.sem_inc(probT_ready[0], 1)
            dve.sem_inc(att_ready, 1)
            dve.sem_inc(resid_ready, 1)
            with dve.Fori(0, NB) as b:
                def j_wait(g):
                    dve.wait_ge(j_ready, per_batch(b, NJ, g + 2))

                j_wait(CTX_T)
                dve.tensor_copy(allT[:, :, 0:P], J[0][:, 0:E].rearrange("p (k t) -> p k t", k=KT)).then_inc(j_used[0], 1)
                dve.tensor_tensor(resid[:], lat[:], w["ob"], ALU.add).then_inc(resid_ready, 1)
                j_wait(K0)
                dve.tensor_tensor(kT[:, 0:2, :], J[0][:].rearrange("p (m n) -> p m n", m=2), w["kb"][:, 0:2].unsqueeze(2).broadcast_to([P, 2, NK]), ALU.add)\
                    .then_inc(j_used[0], 1)
                j_wait(V)
                dve.tensor_tensor(v[:], J[0][:].rearrange("p (n e) -> p n e", n=2), w["vb"].unsqueeze(1).broadcast_to([P, 2, E]), ALU.add).then_inc(j_used[0], 1)
                for n in range(NP + 3):
                    if n < NP:
                        dve.wait_ge(scores_ready, per_batch(b, NP, n + 1))
                        dve.tensor_reduce(negmax[:, n, :], S[n % 2][:], X_AXIS, ALU.max, negate=True).then_inc(max_ready, 1)
                    if 1 <= n <= NP and (n - 1) % 2 == 0:
                        dve.wait_ge(t_ready, per_batch(b, NP, n + 2))
                        dve.wait_ge(pv_done, per_batch(b, NP, n))
                        dve.tensor_copy(probT[:, 0], T[0][:]).then_inc(probT_ready[0], 1)
                    if n == NP:
                        dve.wait_ge(exp_done, per_batch(b, NP, NP + 2))
                        dve.reciprocal(rinv[:], rowsum[:]).then_inc(rinv_ready, 1)
                dve.wait_ge(pv_done, per_batch(b, NP, NP + 2))
                dve.wait_ge(rinv_ready, b + 1)
                for mp in range(2):
                    cols = slice(mp * P, (mp + 1) * P)
                    last = dve.tensor_tensor(att[:, cols].rearrange("p (i g d) -> p i g d", i=2, g=4), A[:, cols].rearrange("p (i g d) -> p i g d", i=2, g=4),
                                             rinv[:, 4 * mp:4 * mp + 4, :].rearrange("p g i -> p i g").unsqueeze(3).broadcast_to([P, 2, 4, D]), ALU.mult)
                last.then_inc(att_ready, 1)
                j_wait(AT_T)
                dve.tensor_copy(attT[:], J[0][:, 0:E].rearrange("p (k t) -> p k t", k=KT)).then_inc(j_used[0], 1)
                dve.wait_ge(att_out_ready, b + 1)
                dve.wait_ge(stored, per_batch(b, 16, 16))
                dve.tensor_tensor(out[:], att_out[:], resid[:], ALU.add).then_inc(out_ready, 1)

        @block.gpsimd
        def _(pool):
            pool.sem_inc(stored, 16)
            if prefetch:
                prefetch[0](pool)

        @block.scalar
        def _(act):
            act.sem_inc(j_used[1], 1)
            act.sem_inc(probT_ready[1], 1)
            act.sem_inc(exp_done, 2)
            act.wait_ge(qb16_set, 1)
            with act.Fori(0, NB) as b:
                def j_wait(g):
                    act.wait_ge(j_ready, per_batch(b, NJ, g + 2))

                j_wait(LAT_T)
                act.activation(allT[:, :, P:NK], J[1][:, 0:E].rearrange("p (k t) -> p k t", k=KT), ACT.Copy).then_inc(j_used[1], 1)
                j_wait(K0 + 1)
                for mm in range(2):
                    last = act.activation(kT[:, 2 + mm, :], J[1][:, mm * NK:(mm + 1) * NK], ACT.Identity, bias=w["kb"][:, 2 + mm:3 + mm])
                last.then_inc(j_used[1], 1)
                j_wait(Q)
                for m in range(M):
                    last = act.activation(qT[:, m, :], J[1][:, m * P:(m + 1) * P], ACT.Identity, bias=qb16[:, m:m + 1], scale=1.0 / D)
                last.then_inc(j_used[1], 1)
                for n in range(NP + 3):
                    if n < NP:
                        act.wait_ge(max_ready, per_batch(b, NP, n + 1))
                        act.wait_ge(t_ready, per_batch(b, NP, n + 1))
                        for i in range(2):
                            last = act.activation(prob[:, n % 2, i, :], S[n % 2][:, i, :], ACT.Exp, bias=negmax[:, n, i:i + 1], accum_out=rowsum[:, n, i:i + 1])
                        last.then_inc(exp_done, 1)
                    if n >= 3 and (n - 2) % 2 == 1 and n - 2 < NP:
                        h = n - 2
                        act.wait_ge(t_ready, per_batch(b, NP, h + 3))
                        act.wait_ge(pv_done, per_batch(b, NP, h + 1))
                        act.activation(probT[:, 1], T[1][:], ACT.Copy).then_inc(probT_ready[1], 1)
                j_wait(OUT)
                act.activation(att_out[:], J[1][:, 0:E], ACT.Copy).then_inc(att_out_ready, 1)
                act.wait_ge(att_out_ready, b + 1)
                act.sem_inc(j_used[1], 1)


def gelu_mlp(nc, NB, w, consts, src, resid_in, dst, gelu, rms, tag, prefetch):
    G = 4
    F = 1024
    M = F // P
    ident, mhalf = consts["ident"], consts["mhalf"]
    NI = NB // G

    with ExitStack() as st:
        sems = st.enter_context(Semaphores(nc))

        def sb(name, shape, dt=F32):
            return st.enter_context(nc.sbuf_tensor(tag + name, shape, dt))

        def sem(name):
            return sems.new(tag + name)

        x, res, xn, out = sb("x", [P, G, E]), sb("res", [P, G, E]), sb("xn", [P, G, E]), sb("out", [P, G, E])
        resb = sb("resb", [P, G, E])
        stats, mv, ve, rstd, sqm = sb("stats", [P, G, 6]), sb("mv", [P, G, 2]), sb("ve", [P, G]), sb("rstd", [P, G]), sb("sqm", [P, G])
        xnT, hT = sb("xnT", [P, KT, G * P]), sb("hT", [P, M, G * P])
        XT = [st.enter_context(nc.psum_tensor(f"{tag}XT{i}", [P, 512], F32)) for i in range(KT)]
        H = [st.enter_context(nc.psum_tensor(f"{tag}H{i}", [P, 512], F32)) for i in range(4)]
        Y = [st.enter_context(nc.psum_tensor(f"{tag}Y{i}", [P, 2, E], F32)) for i in range(2)]

        x_loaded, res_loaded, stored = sem("x_loaded"), sem("res_loaded"), sem("stored")
        chain_sem, ve_ready, rstd_ready, xn_ready, resb_ready = sem("chain"), sem("ve_ready"), sem("rstd_ready"), sem("xn_ready"), sem("resb_ready")
        xt_ready, xnT_ready = sem("xt_ready"), sem("xnT_ready")
        h_ready, h_done = sem("h_ready"), sem("h_done")
        y_ready, y_done = sem("y_ready"), sem("y_done")
        block = st.enter_context(nc.Block())

        def rows(ap, i):
            return ap.rearrange("(n g) t e -> n t g e", g=G)[i]

        @block.sync
        def _(sp):
            with sp.Fori(0, NI) as i:
                sp.wait_ge(xn_ready, i + 1)
                sp.dma_start(x[:], rows(src, i)).then_inc(x_loaded, 16)
                sp.wait_ge(resb_ready, i + 1)
                sp.dma_start(res[:], rows(resid_in, i)).then_inc(res_loaded, 16)
                sp.wait_ge(y_done, per_batch(i, 2, 4))
                sp.dma_start(rows(dst, i), out[:]).then_inc(stored, 16)
            sp.wait_ge(stored, 16 * NI + 16)
            if prefetch:
                prefetch[1](sp)

        @block.tensor
        def _(pe):
            with pe.Fori(0, NI) as i:
                pe.wait_ge(xn_ready, i + 2)
                for kt in range(KT):
                    for g in range(G):
                        last = pe.transpose(XT[kt][:, g * P:(g + 1) * P], xn[:, g, kt * P:(kt + 1) * P], ident[:])
                    last.then_inc(xt_ready, 1)
                pe.wait_ge(xnT_ready, per_batch(i, KT, KT))
                for m in range(M):
                    pe.wait_ge(h_done, per_batch(i, M, m + 1))
                    for kt in range(KT):
                        last = pe.matmul(H[m % 4][:], w["w1"][:, kt, m * P:(m + 1) * P], xnT[:, kt, :], start=(kt == 0), stop=(kt == KT - 1))
                    last.then_inc(h_ready, 1)
                pe.wait_ge(h_done, per_batch(i, M, M + 4))
                for pair in range(G // 2):
                    pe.wait_ge(y_done, per_batch(i, 2, pair + 1))
                    for k in range(2):
                        g = 2 * pair + k
                        for m in range(M):
                            last = pe.matmul(Y[pair][:, k, :], hT[:, m, g * P:(g + 1) * P], w["w2"][:, m, :], start=(m == 0), stop=(m == M - 1))
                    last.then_inc(y_ready, 1)

        @block.vector
        def _(dve):
            dve.sem_inc(xn_ready, 1)
            dve.sem_inc(resb_ready, 1)
            dve.sem_inc(y_done, 2)
            with dve.Fori(0, NI) as i:
                dve.wait_ge(x_loaded, per_batch(i, 16, 16))
                chain = Chain(dve, chain_sem, 5 if rms else 3, i)
                for g in range(G):
                    last = dve.bn_stats(stats[:, g, :], x[:, g, :])
                chain.link_before_aggregate(last)
                for g in range(G):
                    last = dve.bn_aggr(mv[:, g, :], stats[:, g, :])
                chain.link(last)
                if rms:
                    chain.link(dve.tensor_tensor(sqm[:], mv[:, :, 0], mv[:, :, 0], ALU.mult))
                    chain.link(dve.tensor_tensor(sqm[:], mv[:, :, 1], sqm[:], ALU.add))
                    dve.tensor_scalar(ve[:], sqm[:], 1e-6, None, ALU.add).then_inc(ve_ready, 1)
                else:
                    dve.tensor_scalar(ve[:], mv[:, :, 1], 1e-5, None, ALU.add).then_inc(ve_ready, 1)
                chain.close()
                dve.wait_ge(res_loaded, per_batch(i, 16, 16))
                dve.tensor_tensor(resb[:], res[:], w["b2"].unsqueeze(1).broadcast_to([P, G, E]), ALU.add).then_inc(resb_ready, 1)
                dve.wait_ge(rstd_ready, i + 1)
                for g in range(G):
                    if rms:
                        last = dve.tensor_scalar(xn[:, g, :], x[:, g, :], rstd[:, g:g + 1], None, ALU.mult)
                    else:
                        last = dve.tensor_scalar(xn[:, g, :], x[:, g, :], mv[:, g, 0:1], rstd[:, g:g + 1], ALU.subtract, ALU.mult)
                last.then_inc(xn_ready, 1)
                for kt in range(KT):
                    dve.wait_ge(xt_ready, per_batch(i, KT, kt + 1))
                    dve.tensor_scalar(xnT[:, kt, :], XT[kt][:], w["scale"][:, kt:kt + 1], w["offset"][:, kt:kt + 1], ALU.mult, ALU.add).then_inc(xnT_ready, 1)
                dve.wait_ge(resb_ready, i + 2)
                dve.wait_ge(stored, per_batch(i, 16, 16))
                for pair in range(G // 2):
                    dve.wait_ge(y_ready, per_batch(i, 2, pair + 1))
                    dve.tensor_tensor(out[:, 2 * pair:2 * pair + 2, :], Y[pair][:], resb[:, 2 * pair:2 * pair + 2, :], ALU.add).then_inc(y_done, 1)

        @block.gpsimd
        def _(pool):
            pool.sem_inc(stored, 16)
            if prefetch:
                prefetch[0](pool)
            with pool.Fori(0, NI) as i:
                pool.wait_ge(ve_ready, i + 1)
                pool.tensor_tensor(rstd[:], ve[:], mhalf[:, 0:G], ALU.pow).then_inc(rstd_ready, 1)

        @block.scalar
        def _(act):
            act.sem_inc(h_done, 4)
            with act.Fori(0, NI) as i:
                for m in range(M):
                    act.wait_ge(h_ready, per_batch(i, M, m + 1))
                    act.activation(hT[:, m, :], H[m % 4][:], gelu, bias=w["b1"][:, m:m + 1]).then_inc(h_done, 1)


def cross_attention(nc, NB, w, consts, src, kv_in, dst, tag, prefetch):
    H, D = 16, 128
    scale = float(D) ** -0.5
    ident, mhalf = consts["ident"], consts["mhalf"]
    CTX_T, K0, XN_T, Q0, V0, PB_T, WO, NJ = 0, 1, 5, 6, 10, 14, 15, 16
    HJ = NJ // 2
    HPG = 4
    NG = H // HPG

    with ExitStack() as st:
        sems = st.enter_context(Semaphores(nc))

        def sb(name, shape, dt=F32):
            return st.enter_context(nc.sbuf_tensor(tag + name, shape, dt))

        def sem(name):
            return sems.new(tag + name)

        x, ctx = sb("x", [P, E]), sb("ctx", [P, E])
        stats, mv, ve, rstd = sb("stats", [P, 6]), sb("mv", [P, 2]), sb("ve", [P, 1]), sb("rstd", [P, 1])
        xn, resid, wo_out, out = sb("xn", [P, E]), sb("resid", [P, E]), sb("wo_out", [P, E]), sb("out", [P, E])
        xnT, ctxT = sb("xnT", [P, KT, P]), sb("ctxT", [P, KT, P])
        qT, kT, v = sb("qT", [P, H, P]), sb("kT", [P, H, P + 1]), sb("v", [P, H * D])
        prob, probT, attT = sb("prob", [P, H, P + 1]), sb("probT", [P, H, P]), sb("attT", [P, H, P])
        negmax, rowsum, rinv = sb("negmax", [P, H]), sb("rowsum", [P, H]), sb("rinv", [P, H])
        pbT = sb("pbT", [H, P])
        bqs, bvd = sb("bqs", [P, H]), sb("bvd", [P, H])
        diag_bv, biasv_wo, row_bias = sb("diag_bv", [P, H, H]), sb("biasv_wo", [H, E]), sb("row_bias", [P, E])
        J = [st.enter_context(nc.psum_tensor(f"{tag}J{i}", [P, 512], F32)) for i in range(2)]
        S = [st.enter_context(nc.psum_tensor(f"{tag}S{i}", [P, 512], F32)) for i in range(2)]
        T = [st.enter_context(nc.psum_tensor(f"{tag}T{i}", [P, HPG, P], F32)) for i in range(2)]
        C = [st.enter_context(nc.psum_tensor(f"{tag}C{i}", [P, HPG, P], F32)) for i in range(2)]

        x_loaded, ctx_loaded, stored = sem("x_loaded"), sem("ctx_loaded"), sem("stored")
        setup_v, setup_pe, setup_done = sem("setup_v"), sem("setup_pe"), sem("setup_done")
        ln_chain, ve_ready, rstd_ready = sem("ln_chain"), sem("ve_ready"), sem("rstd_ready")
        xn_ready, resid_ready = sem("xn_ready"), sem("resid_ready")
        j_ready = sem("j_ready")
        j_used = [sem("j0_used"), sem("j1_used")]
        scores_ready, max_ready, exp_done = sem("scores_ready"), sem("max_ready"), sem("exp_done")
        rinv_ready, prob_ready = sem("rinv_ready"), sem("prob_ready")
        t_ready, c_ready = sem("t_ready"), sem("c_ready")
        t_used = [sem("t0_used"), sem("t1_used")]
        c_used = [sem("c0_used"), sem("c1_used")]
        out_ready, wo_copied = sem("out_ready"), sem("wo_copied")
        block = st.enter_context(nc.Block())

        @block.sync
        def _(sp):
            with sp.Fori(0, NB) as b:
                sp.wait_ge(j_ready, per_batch(b, NJ, 1))
                sp.dma_start(ctx[:], kv_in[b]).then_inc(ctx_loaded, 16)
                sp.wait_ge(resid_ready, b + 1)
                sp.wait_ge(xn_ready, b + 1)
                sp.dma_start(x[:], src[b]).then_inc(x_loaded, 16)
                sp.wait_ge(out_ready, b + 1)
                sp.dma_start(dst[b], out[:]).then_inc(stored, 16)
            sp.wait_ge(stored, 16 * NB + 16)
            if prefetch:
                prefetch[1](sp)

        @block.tensor
        def _(pe):
            pe.sem_inc(j_ready, 1)
            pe.wait_ge(setup_v, 3)
            for h in range(H):
                last = pe.matmul(J[0][0:H, 0:E], diag_bv[:, h, :], w["wo"][:, h, :], start=(h == 0), stop=(h == H - 1))
            last.then_inc(setup_pe, 1)
            for h in range(H):
                last = pe.matmul(J[1][:, 0:E], w["bv"][:, h:h + 1].broadcast_to([P, P]), w["wo"][:, h, :], start=(h == 0), stop=(h == H - 1))
            last.then_inc(setup_pe, 1)
            pe.wait_ge(setup_done, 3)

            with pe.Fori(0, NB) as b:
                def j_free(g):
                    pe.wait_ge(j_used[g % 2], per_batch(b, HJ, g // 2 + 1))

                def j_evacuated(g):
                    pe.wait_ge(j_used[g % 2], per_batch(b, HJ, g // 2 + 2))

                def project(g, wt, moving):
                    j_free(g)
                    for i in range(HPG):
                        h = HPG * ((g - (K0 if g < XN_T else Q0))) + i
                        for kt in range(KT):
                            last = pe.matmul(J[g % 2][:, i * P:(i + 1) * P], wt[:, kt, h * D:(h + 1) * D], moving[:, kt, :],
                                             start=(kt == 0), stop=(kt == KT - 1))
                    last.then_inc(j_ready, 1)

                def values(c):
                    g = V0 + c
                    j_free(g)
                    for kt in range(KT):
                        last = pe.matmul(J[g % 2][:], ctxT[:, kt, :], w["wv"][:, kt, c * 512:(c + 1) * 512], start=(kt == 0), stop=(kt == KT - 1))
                    last.then_inc(j_ready, 1)

                def scores(n):
                    pe.wait_ge(exp_done, per_batch(b, H // 2, n + 1))
                    for i in range(2):
                        h = 2 * n + i
                        last = pe.matmul(S[n % 2][:, i * (P + 1):(i + 1) * (P + 1)], qT[:, h, :], kT[:, h, :], start=True, stop=True)
                    last.then_inc(scores_ready, 1)

                def turn(g4):
                    pe.wait_ge(prob_ready, per_batch(b, H // 2, 2 * g4 + 2))
                    pe.wait_ge(t_used[g4 % 2], per_batch(b, NG // 2, g4 // 2 + 1))
                    for i in range(HPG):
                        last = pe.transpose(T[g4 % 2][:, i, :], prob[:, HPG * g4 + i, 0:P], ident[:])
                    last.then_inc(t_ready, 1)

                def attend(g4):
                    pe.wait_ge(t_used[g4 % 2], per_batch(b, NG // 2, g4 // 2 + 2))
                    pe.wait_ge(c_used[g4 % 2], per_batch(b, NG // 2, g4 // 2 + 1))
                    j_evacuated(V0 + g4)
                    for i in range(HPG):
                        h = HPG * g4 + i
                        last = pe.matmul(C[g4 % 2][:, i, :], v[:, h * D:(h + 1) * D], probT[:, h, :], start=True, stop=True)
                    last.then_inc(c_ready, 1)

                def output(g4):
                    pe.wait_ge(c_used[g4 % 2], per_batch(b, NG // 2, g4 // 2 + 2))
                    for h in range(HPG * g4, HPG * g4 + HPG):
                        pe.matmul(J[WO % 2][:, 0:E], attT[:, h, :], w["wo"][:, h, :], start=(h == 0), stop=False)

                j_free(CTX_T)
                pe.wait_ge(ctx_loaded, per_batch(b, 16, 16))
                for kt in range(KT):
                    last = pe.transpose(J[0][:, kt * P:(kt + 1) * P], ctx[:, kt * P:(kt + 1) * P], ident[:])
                last.then_inc(j_ready, 1)
                j_evacuated(CTX_T)
                for g in range(K0, XN_T):
                    project(g, w["wk"], ctxT)
                j_free(XN_T)
                pe.wait_ge(xn_ready, b + 2)
                for kt in range(KT):
                    last = pe.transpose(J[1][:, kt * P:(kt + 1) * P], xn[:, kt * P:(kt + 1) * P], ident[:])
                last.then_inc(j_ready, 1)
                j_evacuated(XN_T)
                for g in range(Q0, V0):
                    project(g, w["wq"], xnT)
                j_evacuated(Q0 + 2)
                for n in range(12):
                    if n == 6:
                        j_evacuated(Q0 + 3)
                    if n < H // 2:
                        scores(n)
                    if n < NG:
                        values(n)
                    if n >= 3 and n % 2 == 1 and n <= 9:
                        turn((n - 3) // 2)
                    if n >= 4 and n % 2 == 0 and n <= 10:
                        attend((n - 4) // 2)
                    if n >= 5 and n % 2 == 1:
                        if n == 5:
                            j_free(WO)
                        output((n - 5) // 2)
                    if n == 9:
                        j_free(PB_T)
                        pe.transpose(J[0][0:H, 0:P], prob[:, :, P], ident[:]).then_inc(j_ready, 1)
                j_evacuated(PB_T)
                pe.matmul(J[WO % 2][:, 0:E], pbT[:], biasv_wo[:], start=False, stop=True).then_inc(j_ready, 1)

        @block.vector
        def _(dve):
            dve.tensor_scalar(bqs[:], w["bq"], scale, None, ALU.mult).then_inc(setup_v, 1)
            dve.memset(diag_bv[:], 0.0).then_inc(setup_v, 1)
            dve.wait_ge(setup_v, 2)
            dve.tensor_tensor(diag_bv[:].rearrange("p a c -> p (a c)")[:, 0:H * H:H + 1], w["bias_v"], w["bv"], ALU.subtract).then_inc(setup_v, 1)
            dve.tensor_copy(kT[:, :, P], w["bias_k"]).then_inc(setup_done, 1)
            dve.wait_ge(setup_pe, 1)
            dve.tensor_copy(biasv_wo[:], J[0][0:H, 0:E]).then_inc(setup_done, 1)
            dve.wait_ge(setup_pe, 2)
            dve.tensor_tensor(row_bias[:], J[1][:, 0:E], w["bo"], ALU.add).then_inc(setup_done, 1)
            dve.sem_inc(j_used[0], 1)
            dve.sem_inc(t_used[0], 1)
            dve.sem_inc(c_used[0], 1)
            dve.sem_inc(xn_ready, 1)
            dve.sem_inc(resid_ready, 1)
            dve.wait_ge(setup_done, 3)

            with dve.Fori(0, NB) as b:
                def j_wait(g):
                    dve.wait_ge(j_ready, per_batch(b, NJ, g + 2))

                j_wait(CTX_T)
                dve.tensor_copy(ctxT[:], J[0][:, 0:E].rearrange("p (k t) -> p k t", k=KT)).then_inc(j_used[0], 1)
                dve.wait_ge(x_loaded, per_batch(b, 16, 16))
                chain = Chain(dve, ln_chain, 3, b)
                chain.link_before_aggregate(dve.bn_stats(stats[:], x[:]))
                chain.link(dve.bn_aggr(mv[:], stats[:]))
                chain.close()
                dve.tensor_scalar(ve[:], mv[:, 1:2], 1e-5, None, ALU.add).then_inc(ve_ready, 1)
                dve.tensor_tensor(resid[:], x[:], row_bias[:], ALU.add).then_inc(resid_ready, 1)
                dve.wait_ge(rstd_ready, b + 1)
                dve.tensor_scalar(xn[:], x[:], mv[:, 0:1], rstd[:], ALU.subtract, ALU.mult).then_inc(xn_ready, 1)
                for g in (K0 + 1, K0 + 3):
                    j_wait(g)
                    h = HPG * (g - K0)
                    dve.tensor_tensor(kT[:, h:h + HPG, 0:P], J[0][:].rearrange("p (h t) -> p h t", h=HPG),
                                      w["bk"][:, h:h + HPG].unsqueeze(2).broadcast_to([P, HPG, P]), ALU.add).then_inc(j_used[0], 1)
                for g in (Q0, Q0 + 2):
                    j_wait(g)
                    h = HPG * (g - Q0)
                    dve.scalar_tensor_tensor(qT[:, h:h + HPG, :], J[0][:].rearrange("p (h t) -> p h t", h=HPG), scale,
                                             bqs[:, h:h + HPG].unsqueeze(2).broadcast_to([P, HPG, P]), ALU.mult, ALU.add).then_inc(j_used[0], 1)
                for n in range(12):
                    if n < H // 2:
                        dve.wait_ge(scores_ready, per_batch(b, H // 2, n + 1))
                        dve.tensor_reduce(negmax[:, 2 * n:2 * n + 2], S[n % 2][:, 0:2 * (P + 1)].rearrange("p (h t) -> p h t", h=2),
                                          X_AXIS, ALU.max, negate=True).then_inc(max_ready, 1)
                    if n in (0, 2):
                        j_wait(V0 + n)
                        dve.tensor_copy(v[:, n * 512:(n + 1) * 512], J[0][:]).then_inc(j_used[0], 1)
                    if 1 <= n <= H // 2:
                        dve.wait_ge(exp_done, per_batch(b, H // 2, n + 2))
                        dve.reciprocal(rinv[:, 2 * n - 2:2 * n], rowsum[:, 2 * n - 2:2 * n]).then_inc(rinv_ready, 1)
                    if n in (3, 7):
                        g4 = (n - 3) // 2
                        dve.wait_ge(t_ready, per_batch(b, NG, g4 + 1))
                        dve.tensor_copy(probT[:, HPG * g4:HPG * g4 + HPG, :], T[0][:]).then_inc(t_used[0], 1)
                    if n in (5, 9):
                        g4 = (n - 5) // 2
                        dve.wait_ge(c_ready, per_batch(b, NG, g4 + 1))
                        dve.tensor_copy(attT[:, HPG * g4:HPG * g4 + HPG, :], C[0][:]).then_inc(c_used[0], 1)
                j_wait(PB_T)
                dve.tensor_copy(pbT[:], J[0][0:H, 0:P]).then_inc(j_used[0], 1)
                dve.wait_ge(wo_copied, b + 1)
                dve.wait_ge(stored, per_batch(b, 16, 16))
                dve.tensor_tensor(out[:], wo_out[:], resid[:], ALU.add).then_inc(out_ready, 1)

        @block.gpsimd
        def _(pool):
            pool.sem_inc(stored, 16)
            if prefetch:
                prefetch[0](pool)
            with pool.Fori(0, NB) as b:
                pool.wait_ge(ve_ready, b + 1)
                pool.tensor_tensor(rstd[:], ve[:], mhalf[:, 0:1], ALU.pow).then_inc(rstd_ready, 1)
                for n in range(H // 2):
                    pool.wait_ge(rinv_ready, per_batch(b, H // 2, n + 1))
                    pr = prob[:, 2 * n:2 * n + 2, :]
                    pool.tensor_tensor(pr, pr, rinv[:, 2 * n:2 * n + 2].unsqueeze(2).broadcast_to([P, 2, P + 1]), ALU.mult).then_inc(prob_ready, 1)

        @block.scalar
        def _(act):
            act.sem_inc(j_used[1], 1)
            act.sem_inc(t_used[1], 1)
            act.sem_inc(c_used[1], 1)
            act.sem_inc(exp_done, 2)
            act.wait_ge(setup_v, 1)
            act.wait_ge(setup_done, 3)

            with act.Fori(0, NB) as b:
                def j_wait(g):
                    act.wait_ge(j_ready, per_batch(b, NJ, g + 2))

                for g in (K0, K0 + 2):
                    j_wait(g)
                    for i in range(HPG):
                        h = HPG * (g - K0) + i
                        last = act.activation(kT[:, h, 0:P], J[1][:, i * P:(i + 1) * P], ACT.Identity, bias=w["bk"][:, h:h + 1])
                    last.then_inc(j_used[1], 1)
                j_wait(XN_T)
                for kt in range(KT):
                    last = act.activation(xnT[:, kt, :], J[1][:, kt * P:(kt + 1) * P], ACT.Identity, bias=w["offset"][:, kt:kt + 1], scale=w["scale"][:, kt:kt + 1])
                last.then_inc(j_used[1], 1)
                for g in (Q0 + 1, Q0 + 3):
                    j_wait(g)
                    for i in range(HPG):
                        h = HPG * (g - Q0) + i
                        last = act.activation(qT[:, h, :], J[1][:, i * P:(i + 1) * P], ACT.Identity, bias=bqs[:, h:h + 1], scale=scale)
                    last.then_inc(j_used[1], 1)
                for n in range(13):
                    if n < H // 2:
                        act.wait_ge(max_ready, per_batch(b, H // 2, n + 1))
                        for i in range(2):
                            h = 2 * n + i
                            last = act.activation(prob[:, h, :], S[n % 2][:, i * (P + 1):(i + 1) * (P + 1)], ACT.Exp,
                                                  bias=negmax[:, h:h + 1], accum_out=rowsum[:, h:h + 1])
                        last.then_inc(exp_done, 1)
                    if n in (1, 3):
                        j_wait(V0 + n)
                        act.activation(v[:, n * 512:(n + 1) * 512], J[1][:], ACT.Copy).then_inc(j_used[1], 1)
                    if n in (5, 9):
                        g4 = (n - 3) // 2
                        act.wait_ge(t_ready, per_batch(b, NG, g4 + 1))
                        act.activation(probT[:, HPG * g4:HPG * g4 + HPG, :], T[1][:], ACT.Copy).then_inc(t_used[1], 1)
                    if n in (7, 11):
                        g4 = (n - 5) // 2
                        act.wait_ge(c_ready, per_batch(b, NG, g4 + 1))
                        act.activation(attT[:, HPG * g4:HPG * g4 + HPG, :], C[1][:], ACT.Copy).then_inc(c_used[1], 1)
                j_wait(WO)
                act.activation(wo_out[:], J[1][:, 0:E], ACT.Copy).then_inc(wo_copied, 1)
                act.wait_ge(wo_copied, b + 1)
                act.sem_inc(j_used[1], 1)


L0_COLS = ["ln1_w", "ln1_b", "ln2_w", "ln2_b", "maa_x", "time_decay", "u", "gn_w", "gn_b", "ffn_k", "ffn_r",
           "stack0", "stack1", "stack2", "stack3", "stack4"]
HEAD_COLS = ["bq", "bk", "bv", "bias_k", "bias_v"]
COLUMNS = ([("l0_" + n, 2) for n in L0_COLS] + [("l1_bias", 8), ("l1_bo", 1)]
           + [("l2_qb", 4), ("l2_kb", 4), ("l2m_b1", 8), ("l2m_scale", 2), ("l2m_offset", 2)]
           + [(f"l3{s}_{n}", 16) for s in "ab" for n in HEAD_COLS]
           + [(f"l3{s}_{n}", 2) for s in "ab" for n in ("scale", "offset")]
           + [("l3m_b1", 8), ("l3m_scale", 2), ("l3m_offset", 2)])
ROWS = ["l2_vb", "l2_ob", "l2m_b2", "l3a_bo", "l3b_bo", "l3m_b2"]
N_COLS = sum(n for _, n in COLUMNS)


def col_at(name):
    at = 0
    for n, width in COLUMNS:
        if n == name:
            return at, width
        at += width
    raise KeyError(name)


L0_W = [("l0_maa_w1", 2 * 160, P), ("l0_maa_w2a", 256, P), ("l0_maa_w2b", 256, 32), ("l0_wv", 512, P), ("l0_wk", 512, P), ("l0_td_w1", 128, P),
        ("l0_td_w2", 256, 64), ("l0_wr", 512, P), ("l0_wg", 512, P), ("l0_wo", 512, P), ("l0_wfk", 512, P), ("l0_wfr", 512, P), ("l0_wfv", 512, P)]
L1_W = [("l1_wq0", 3072, P), ("l1_wi0", 3072, P), ("l1_wq1", 3072, P), ("l1_wi1", 3072, P), ("l1_wo", 1024, P)]
L2_W = [("l2_kw", 1024, P), ("l2_vw", 512, P), ("l2_qw", 1024, P), ("l2_ow", 512, P), ("l2m_w1", 2048, P), ("l2m_w2", 2048, P)]
L3A_W = [("l3a_wk", 4096, P), ("l3a_wq", 4096, P), ("l3a_wv", 4096, P), ("l3a_wo", 4096, P)]
L3B_W = [("l3b" + n[3:], c, p) for n, c, p in L3A_W]
L3M_W = [("l3m_w1", 2048, P), ("l3m_w2", 2048, P)]


def program(nc, dram, out):
    NB = dram["x"].shape[0]
    hidden = [nc.dram_tensor(f"hidden{n}", [NB, P, E], F32, kind="Internal").ap() for n in range(6)]
    v_dram = nc.dram_tensor("v_dram", [2, E, P], F32, kind="Internal").ap()

    with ExitStack() as st:
        def sb(name, shape, dt=F32):
            return st.enter_context(nc.sbuf_tensor(name, shape, dt))

        region = [sb("region0", [P, REGION]), sb("region1", [P, REGION])]
        columns, rows = sb("columns", [P, N_COLS]), sb("rows", [P, len(ROWS), E])
        ident, pick = sb("ident", [P, P]), sb("pick", [P, 16])
        mean_of, full1, mhalf = sb("mean_of", [P, P]), sb("full1", [P, P]), sb("mhalf", [P, 64])
        loaded = {name: st.enter_context(nc.semaphore("loaded_" + name)) for name in ("small", "l0", "l1", "l2", "l3a", "l3b", "l3m")}
        constants_set = st.enter_context(nc.semaphore("constants_set"))
        consts = dict(ident=ident, pick=pick, ones=mean_of, full1=full1, mhalf=mhalf)

        def col(name):
            at, width = col_at(name)
            return columns[:, at:at + width]

        def row(name):
            return rows[:, ROWS.index(name), :]

        def places(weights, reg):
            at, out_ = 0, {}
            for name, words, parts in weights:
                out_[name] = region[reg][0:parts, at:at + words]
                at += words
            return out_

        place = {}
        for weights, reg in ((L0_W, 0), (L1_W, 1), (L2_W, 0), (L3A_W, 1), (L3B_W, 0), (L3M_W, 1)):
            place.update(places(weights, reg))

        def loader(name, weights):
            def start(eng):
                for n, _, _ in weights:
                    eng.dma_start(place[n], dram[n]).then_inc(loaded[name], 16)

            def wait(eng):
                eng.wait_ge(loaded[name], 16 * len(weights))
            return start, wait

        def tiles(name, k):
            return place[name].rearrange("p (k n) -> p k n", k=k)

        start_l0, wait_l0 = loader("l0", L0_W)
        with nc.Block() as block:
            @block.sync
            def _(sp):
                for to, name in ((columns, "columns"), (ident, "ident"), (pick, "pick")):
                    sp.dma_start(to[:], dram[name]).then_inc(loaded["small"], 16)
                sp.dma_start(rows[:].rearrange("p r e -> p (r e)"), dram["rows"].partition_broadcast(P)).then_inc(loaded["small"], 16)
                start_l0(sp)
                sp.wait_ge(loaded["small"], 64)
                wait_l0(sp)

            @block.vector
            def _(dve):
                dve.memset(mean_of[:], 1.0 / P).then_inc(constants_set, 1)
                dve.memset(full1[:], 1.0).then_inc(constants_set, 1)
                dve.memset(mhalf[:], -0.5).then_inc(constants_set, 1)
                dve.wait_ge(constants_set, 3)

        w0 = {n[3:]: place[n] for n, _, _ in L0_W}
        for n in ("maa_w1", "td_w1", "wr", "wk", "wv", "wg", "wo", "wfk", "wfr", "wfv"):
            w0[n] = tiles("l0_" + n, 2)
        w0["col"] = lambda name: col("l0_" + name)
        rwkv_block(nc, NB, w0, dict(region=region[0], at=REGION), consts, dram["x"], dram["ctx"], v_dram, hidden[0], loader("l1", L1_W))

        w1 = dict(wq=[place["l1_wq0"], place["l1_wq1"]], wi=[place["l1_wi0"], place["l1_wi1"]], wo=tiles("l1_wo", 8), bias=col("l1_bias"), bo=col("l1_bo"))
        deq_attention(nc, NB, w1, consts, hidden[0], dram["ctx"], hidden[1], loader("l2", L2_W))

        w2 = dict(kw=tiles("l2_kw", 2), vw=tiles("l2_vw", 2), qw=tiles("l2_qw", 2), ow=tiles("l2_ow", 2), qb=col("l2_qb"), kb=col("l2_kb"),
                  vb=row("l2_vb"), ob=row("l2_ob"))
        perceiver_attention(nc, NB, w2, consts, hidden[1], dram["ctx"], dram["mask"], dram["row16"], hidden[2], loader("l3a", L3A_W))

        def mlp_weights(tag):
            return dict(w1=tiles(tag + "_w1", 2), w2=tiles(tag + "_w2", 8), b1=col(tag + "_b1"), b2=row(tag + "_b2"), scale=col(tag + "_scale"), offset=col(tag + "_offset"))

        gelu_mlp(nc, NB, mlp_weights("l2m"), consts, hidden[2], hidden[1], hidden[3], ACT.Gelu_apprx_tanh, True, "l2m_", None)

        def attention_weights(tag):
            w = {n: col(f"{tag}_{n}") for n in HEAD_COLS + ["scale", "offset"]}
            w.update({n: tiles(f"{tag}_{n}", 2) for n in ("wq", "wk", "wv")})
            w.update(wo=tiles(tag + "_wo", 16), bo=row(tag + "_bo"))
            return w

        cross_attention(nc, NB, attention_weights("l3a"), consts, hidden[3], dram["ctx"], hidden[4], "l3a_", loader("l3b", L3B_W))
        cross_attention(nc, NB, attention_weights("l3b"), consts, hidden[4], dram["ctx"], hidden[5], "l3b_", loader("l3m", L3M_W))
        gelu_mlp(nc, NB, mlp_weights("l3m"), consts, hidden[5], hidden[5], out, ACT.Gelu, False, "l3m_", None)


def layout(inputs, np):
    def c(a):
        return np.ascontiguousarray(a)

    def tiled(a):
        return c(a.reshape(-1, P, a.shape[1]).transpose(1, 0, 2)).reshape(P, -1)

    def columns_of(a):
        return a.reshape(-1, P).T

    def slots(a):
        o = np.zeros(a.shape[:-1] + (32,), a.dtype)
        o[..., :16] = a
        return o.reshape(a.shape[:-2] + (512,))

    l0 = {k[9:]: v for k, v in inputs.items() if k.startswith("L0_xattn_")}
    l1 = {k[9:]: v for k, v in inputs.items() if k.startswith("L1_xattn_")}
    l2 = {k[9:]: v for k, v in inputs.items() if k.startswith("L2_xattn_")}
    l3 = {k[9:]: v for k, v in inputs.items() if k.startswith("L3_xattn_")}
    a = dict(x=inputs["x"], ctx=inputs["ctx_2048"], mask=inputs["mask_BxS2_ik0"].reshape(1, -1))
    a["l0_maa_w1"], a["l0_maa_w2a"], a["l0_maa_w2b"] = tiled(l0["maa_w1"]), l0["maa_w2"][:4].reshape(P, E), l0["maa_w2"][4]
    a["l0_td_w1"], a["l0_td_w2"] = tiled(l0["td_w1"]), l0["td_w2"]
    for n in ("r", "k", "v", "g", "o", "fk", "fr", "fv"):
        a["l0_w" + n] = tiled(l0["W" + n].T)
    for s in "01":
        a["l1_wq" + s], a["l1_wi" + s] = l1["Wqkv" + s].T, l1["Winj" + s].T
    a["l1_wo"] = tiled(l1["Wo"].T)
    kv = l2["kv_w"].reshape(E, 16, 16, 2)
    a["l2_qw"], a["l2_kw"] = tiled(slots(l2["q_w"].reshape(E, 16, 16))), tiled(slots(kv[..., 0]))
    a["l2_vw"], a["l2_ow"] = tiled(kv[..., 1].reshape(E, E)), tiled(l2["out_w"])
    a["l2m_w1"], a["l2m_w2"] = tiled(l2["mlp_w1"]), tiled(l2["mlp_w2"])
    for s, n in (("a", "1"), ("b", "2")):
        for m in ("wq", "wk", "wv", "wo"):
            a[f"l3{s}_{m}"] = tiled(l3[m + n])
    a["l3m_w1"], a["l3m_w2"] = tiled(l3["w_fc1"]), tiled(l3["w_fc2"])

    kv_b = l2["kv_b"].reshape(16, 16, 2)
    one16 = np.zeros((16, 32), np.float32)
    one16[:, 16] = 1.0
    q_b = slots(l2["q_b"].reshape(16, 16)).reshape(16, 32)
    q_b[:, 16] = 1.0
    v = {"l1_bias": l1["r_w_bias"], "l1_bo": l1["bo"], "l2_qb": q_b, "l2_kb": slots(kv_b[..., 0]), "l2m_b1": l2["mlp_b1"],
         "l2m_scale": l2["postnorm_w"], "l2m_offset": np.zeros(E, np.float32),
         "l3m_b1": l3["b_fc1"], "l3m_scale": l3["ln_mlp_scale"], "l3m_offset": l3["ln_mlp_offset"]}
    for n in L0_COLS:
        v["l0_" + n] = l0["maa_stack"][0, int(n[5:])] if n.startswith("stack") else l0[n.replace("ffn_", "ffn_maa_")]
    for s, n in (("a", "1"), ("b", "2")):
        for m in HEAD_COLS:
            v[f"l3{s}_{m}"] = l3[m + n]
        v[f"l3{s}_scale"], v[f"l3{s}_offset"] = l3[f"ln{n}_scale"], l3[f"ln{n}_offset"]
    a["columns"] = np.concatenate([columns_of(v[n]) for n, _ in COLUMNS], axis=1)
    r = {"l2_vb": kv_b[..., 1].reshape(E), "l2_ob": l2["out_b"], "l2m_b2": l2["mlp_b2"], "l3a_bo": l3["bo1"], "l3b_bo": l3["bo2"], "l3m_b2": l3["b_fc2"]}
    a["rows"] = np.concatenate([r[n] for n in ROWS])
    a["ident"] = np.eye(P, dtype=np.float32)
    a["pick"] = (np.arange(P)[:, None] // 8 == np.arange(16)).astype(np.float32)
    a["row16"] = one16.reshape(1, 512)
    return {k: c(x) for k, x in a.items()}


def kernel(**inputs):
    import numpy as _np
    import concourse.bacc as _bacc
    from concourse import mybir as _mybir
    from concourse.bass_utils import run_bass_kernel_spmd as _run

    nc = _bacc.Bacc("TRN2", target_bir_lowering=False, num_devices=1)
    arrays = layout({k: _np.asarray(v) for k, v in inputs.items()}, _np)
    dram = {n: nc.dram_tensor(n + "_dram", a.shape, _mybir.dt.from_np(a.dtype), kind="ExternalInput").ap() for n, a in arrays.items()}
    out = nc.dram_tensor("out_dram", arrays["x"].shape, _mybir.dt.float32, kind="ExternalOutput").ap()
    program(nc, dram, out)
    r = _run(nc, [{n + "_dram": a for n, a in arrays.items()}], core_ids=[0])
    return r.results[0]["out_dram"]
```

```python
from contextlib import ExitStack

import numpy as np

import concourse.bass as bass
from concourse import mybir

F32 = mybir.dt.float32
I32 = mybir.dt.int32
ALU = mybir.AluOpType
ACT = mybir.ActivationFunctionType
X_AXIS = mybir.AxisListType.X

P = 128
E = 256
KT = E // P
REGION = 16384


class Batch:

    def __init__(self, reg, plus=0, times=1):
        self.reg, self.plus, self.times = reg, plus, times

    def shifted(self, by):
        return Batch(self.reg, self.plus + by, self.times)


def per_batch(b, count, done):
    if isinstance(b, Batch):
        b, count, done = b.reg, count * b.times, done + b.plus * count
    return b * count + done if done else b * count


def index(b):
    return per_batch(b, 1, 0)


def parity(b):
    return b.plus % 2 if isinstance(b, Batch) else b % 2


def rotate(eng, NB, step):
    assert NB % 2 == 0 and NB >= 4
    step(None, None, 0)
    step(None, 0, 1)
    with eng.Fori(0, NB // 2 - 1) as reg:
        for b in (Batch(reg, 1, 2), Batch(reg, 2, 2)):
            step(b.shifted(-1), b, b.shifted(1))
    step(NB - 2, NB - 1, None)
    step(NB - 1, None, None)


class Semaphores:

    def __init__(self, nc):
        self.nc, self.all = nc, []

    def new(self, name):
        self.all.append(self.nc.alloc_semaphore(name=name))
        return self.all[-1]

    def __enter__(self):
        return self

    def __exit__(self, *_):
        self.nc.clear_and_free_semaphores(self.all)
        self.nc.all_engine_barrier()


class Chain:

    def __init__(self, eng, sem, per, b):
        self.eng, self.sem, self.per, self.b, self.n = eng, sem, per, b, 0

    def link(self, ins):
        self.n += 1
        ins.then_inc(self.sem, 1)
        self.eng.wait_ge(self.sem, per_batch(self.b, self.per, self.n))

    def link_before_aggregate(self, ins):
        self.link(ins)
        self.n += 1
        self.eng.sem_inc(self.sem, 1)

    def close(self):
        assert self.n == self.per, (self.n, self.per)


def rwkv_block(nc, NB, w, work, consts, src, state, v_dram, dst, prefetch):
    G, HS, NH = 2, 8, 16
    NI, N = NB // G, G * P
    MIX = dict(k=0, w=1, v=2, r=3, g=4)
    ORDER = "vkwrg"
    ident, mhalf, pick = consts["ident"], consts["mhalf"], consts["pick"]
    col = w["col"]

    with ExitStack() as st:
        sems = st.enter_context(Semaphores(nc))

        def sb(name, shape, dt=F32):
            return st.enter_context(nc.sbuf_tensor("l0_" + name, shape, dt))

        def sem(name):
            return sems.new("l0_" + name)

        def carve(size):
            work["at"] -= size
            return work["region"][:, work["at"]:work["at"] + size]

        x, xn, x1, out = sb("x", [P, G, E]), sb("xn", [P, G, E]), sb("x1", [P, G, E]), sb("out", [P, G, E])
        first_rows, s0 = sb("first_rows", [2, G, E]), sb("s0", [P, KT, G, HS])
        stats, mv, ve, rstd = sb("stats", [P, G, 6]), sb("mv", [P, G, 2]), sb("ve", [P, G]), sb("rstd", [P, G])
        xa, sx, xx = sb("xa", [P, KT, G, P + 1]), sb("sx", [P, KT, N]), sb("xx", [P, KT, N])
        mix_a, mix_b, mix_tmp = sb("mix_a", [P, N]), sb("mix_b", [32, N]), sb("mix_tmp", [P, 2, KT, N])
        xm = sb("xm", [P, 5, KT, N])
        td, decay_log, decay = sb("td", [64, N]), sb("decay_log", [P, KT, N]), sb("decay", [P, KT, N])
        r, k, v, th, sg = sb("r", [P, KT, N]), sb("k", [P, KT, N]), sb("v", [P, KT, N]), sb("th", [P, KT, N]), sb("sg", [P, KT, N])
        v_rep = [carve(HS * P) for _ in range(2)]
        kv = [carve(HS * P) for _ in range(2)]
        swept = [carve(HS * (P + 1)) for _ in range(2)]
        read_out = [carve(HS * P) for _ in range(2)]
        sums, nmean, sq_sums, gve, grstd = (sb(n, [P, G * KT, NH]) for n in ("sums", "nmean", "sq_sums", "gve", "grstd"))
        state0 = sb("state0", [P, KT, G])
        oc, oc_sq = sb("oc", [P, G, E]), sb("oc_sq", [P, G, E])
        og = sb("og", [P, KT, N])
        xc, sx2, xk2, xr2 = xa, sx, xx, sb("xr2", [P, KT, N])
        relu, kk, rr = sb("relu", [P, KT, N]), sb("kk", [P, KT, N]), sb("rr", [P, G, E])
        bank = [st.enter_context(nc.psum_tensor(f"l0_B{i}", [P, 512], F32)) for i in range(8)]

        USES = [("xt", "vp", "wo"), ("ct", "kp", "xt2"), ("m1", "td1", "rr"), ("m2v", "td2", "kk"), ("m2k", "rp", "kvp"),
                ("m2w", "gp"), ("m2r", "wkv"), ("m2g", "ogt")]
        at = {name: bank[n] for n, names in enumerate(USES) for name in names}
        ready = {name: sem(name + "_ready") for names in USES for name in names}
        used = {name: sem(name + "_used") for names in USES for name in names}
        loaded, s0_loaded, stored = sem("loaded"), sem("s0_loaded"), sem("stored")
        v_stored, v_rep_loaded = sem("v_stored"), [sem(f"v_rep{n}_loaded") for n in range(2)]
        chain_sem, ve_ready, rstd_ready = sem("chain"), sem("ve_ready"), sem("rstd_ready")
        xn_ready, sx_ready, xx_ready = sem("xn_ready"), sem("sx_ready"), sem("xx_ready")
        mix_ready, xm_ready, tmp_ready = sem("mix_ready"), sem("xm_ready"), sem("tmp_ready")
        dlog_ready, decay_ready, th_ready, sg_ready = sem("dlog_ready"), sem("decay_ready"), sem("th_ready"), sem("sg_ready")
        kv_ready, col0_ready, swept_ready, read_ready, out_prod_ready = (sem(n) for n in ("kv_ready", "col0_ready", "swept_ready", "read_ready", "out_prod_ready"))
        units_done = sem("units_done")
        oc_ready, oc_sq_ready, gve_ready, grstd_ready, ocn_ready = (sem(n) for n in ("oc_ready", "oc_sq_ready", "gve_ready", "grstd_ready", "ocn_ready"))
        og1_ready, og_ready, x1_ready = sem("og1_ready"), sem("og_ready"), sem("x1_ready")
        xk2_ready, kk_ready, out_ready = (sem(n) for n in ("xk2_ready", "relu_squared", "out_ready"))
        block = st.enter_context(nc.Block())
        UNITS = [(g, hf) for g in range(G) for hf in range(KT)]
        NU = len(UNITS)

        def by_batch(ap):
            return ap.rearrange("p (g t) -> p g t", g=G)

        @block.sync
        def _(sp):
            with sp.Fori(0, NI) as i:
                sp.wait_ge(x1_ready, i + 1)
                sp.dma_start(x[:], src.rearrange("(n g) t e -> n t g e", g=G)[i]).then_inc(loaded, 16)
                sp.wait_ge(used["ct"], i + 1)
                sp.dma_start(first_rows[:], state.rearrange("(n g) t e -> n t g e", g=G)[i, 0:2]).then_inc(loaded, 16)
                sp.wait_ge(units_done, i + 1)
                for g in range(G):
                    rows = state.rearrange("(n g) t e -> n g (t e)", g=G)[i, g, 2 * E:(2 + HS) * E]
                    sp.dma_start(s0[:, :, g, :], rows.rearrange("(h p j) -> p h j", h=KT, j=HS)).then_inc(s0_loaded, 16)
                sp.wait_ge(used["vp"], i + 2)
                for hf in range(KT):
                    sp.dma_start(v_dram[:, hf * P:(hf + 1) * P, :].rearrange("g c t -> c g t"), by_batch(v[:, hf, :])).then_inc(v_stored, 16)
                sp.wait_ge(v_stored, per_batch(i, 32, 64))
                for n, (g, hf) in enumerate(UNITS):
                    sp.wait_ge(kv_ready, per_batch(i, NU, n + 1))
                    rows = v_dram[g, hf * P:(hf + 1) * P, :].rearrange("(h j) t -> h (j t)", j=HS)
                    sp.dma_start(v_rep[n % 2], rows.unsqueeze(1).broadcast_to([NH, HS, HS * P])).then_inc(v_rep_loaded[n % 2], 16)
                sp.wait_ge(out_ready, i + 1)
                sp.dma_start(dst.rearrange("(n g) t e -> n t g e", g=G)[i], out[:]).then_inc(stored, 16)
            sp.wait_ge(stored, 16 * NI + 16)
            if prefetch:
                prefetch[1](sp)

        @block.tensor
        def _(pe):
            with pe.Fori(0, NI) as i:
                def take(name):
                    names = next(n for n in USES if name in n)
                    k = names.index(name)
                    pe.wait_ge(used[names[k - 1]], i + (2 if k else 1))
                    return at[name]

                def by_channel(name, wt, moving):
                    o = take(name)
                    for ho in range(KT):
                        for kt in range(KT):
                            last = pe.matmul(o[:, ho * N:(ho + 1) * N], wt[:, kt, ho * P:(ho + 1) * P], moving[:, kt, :], start=(kt == 0), stop=(kt == KT - 1))
                    last.then_inc(ready[name], 1)

                def by_token(name, lhs, wt):
                    o = take(name)
                    for g in range(G):
                        for kt in range(KT):
                            last = pe.matmul(o[:, g * E:(g + 1) * E], lhs[:, kt, g * P:(g + 1) * P], wt[:, kt, :], start=(kt == 0), stop=(kt == KT - 1))
                    last.then_inc(ready[name], 1)

                def turn(name, rows):
                    o = take(name)
                    for kt in range(KT):
                        for g in range(G):
                            last = pe.transpose(o[:, kt * N + g * P:kt * N + (g + 1) * P], rows[:, g, kt * P:(kt + 1) * P], ident[:])
                    last.then_inc(ready[name], 1)

                pe.wait_ge(loaded, per_batch(i, 32, 32))
                o = take("ct")
                for kt in range(KT):
                    for g in range(G):
                        c = 2 * (kt * G + g)
                        last = pe.matmul(o[:, c:c + 2], first_rows[:, g, kt * P:(kt + 1) * P], ident[0:2, 0:2], start=True, stop=True)
                last.then_inc(ready["ct"], 1)
                pe.wait_ge(xn_ready, per_batch(i, 2, 1))
                turn("xt", xn)
                pe.wait_ge(xx_ready, i + 1)
                o = take("m1")
                for kt in range(KT):
                    pe.matmul(o[:, 0:N], w["maa_w1"][:, kt, 0:P], xx[:, kt, :], start=(kt == 0), stop=(kt == KT - 1))
                for kt in range(KT):
                    last = pe.matmul(o[0:32, N:2 * N], w["maa_w1"][:, kt, P:P + 32], xx[:, kt, :], start=(kt == 0), stop=(kt == KT - 1))
                last.then_inc(ready["m1"], 1)
                pe.wait_ge(mix_ready, per_batch(i, 2, 2))
                for name in ORDER:
                    f = MIX[name]
                    o = take("m2" + name)
                    wt, mv_, r0 = (w["maa_w2a"], mix_a, 32 * f) if f < 4 else (w["maa_w2b"], mix_b, 0)
                    for ho in range(KT):
                        last = pe.matmul(o[:, ho * N:(ho + 1) * N], wt[r0:r0 + 32, ho * P:(ho + 1) * P], mv_[r0:r0 + 32, :], start=True, stop=True,
                                         tile_position=(r0, 0))
                    last.then_inc(ready["m2" + name], 1)

                def xm_wait(name):
                    pe.wait_ge(xm_ready, per_batch(i, 5, ORDER.index(name) + 1))
                    return xm[:, MIX[name]]

                by_channel("vp", w["wv"], xm_wait("v"))
                by_channel("kp", w["wk"], xm_wait("k"))
                mixed = xm_wait("w")
                o = take("td1")
                for kt in range(KT):
                    last = pe.matmul(o[0:64, 0:N], w["td_w1"][:, kt, :], mixed[:, kt, :], start=(kt == 0), stop=(kt == KT - 1))
                last.then_inc(ready["td1"], 1)
                by_channel("rp", w["wr"], xm_wait("r"))
                pe.wait_ge(used["td1"], i + 2)
                o = take("td2")
                for ho in range(KT):
                    last = pe.matmul(o[:, ho * N:(ho + 1) * N], w["td_w2"][:, ho * P:(ho + 1) * P], td[:], start=True, stop=True)
                last.then_inc(ready["td2"], 1)
                by_channel("gp", w["wg"], xm_wait("g"))
                o = take("wkv")
                for n, (g, hf) in enumerate(UNITS):
                    pe.wait_ge(out_prod_ready, per_batch(i, NU, n + 1))
                    for j in range(HS):
                        c = ((g * KT + hf) * HS + j) * NH
                        last = pe.matmul(o[:, c:c + NH], read_out[n % 2][:, j * P:(j + 1) * P], pick[:], start=True, stop=True)
                    last.then_inc(units_done, 1)
                last = pe.wait_ge(units_done, per_batch(i, NU, NU + 2))
                pe.sem_inc(ready["wkv"], 1)
                pe.wait_ge(ocn_ready, i + 1)
                turn("ogt", oc)
                pe.wait_ge(og_ready, i + 1)
                by_token("wo", og, w["wo"])
                pe.wait_ge(xn_ready, per_batch(i, 2, 2))
                turn("xt2", xn)
                pe.wait_ge(xk2_ready, per_batch(i, 2, 1))
                by_channel("kk", w["wfk"], xk2)
                pe.wait_ge(xk2_ready, per_batch(i, 2, 2))
                by_token("rr", xr2, w["wfr"])
                pe.wait_ge(kk_ready, i + 1)
                by_token("kvp", kk, w["wfv"])

        @block.vector
        def _(dve):
            for name in ("m2v", "m2k", "m2w", "m2r", "m2g", "wkv", "wo", "kvp", "gp"):
                dve.sem_inc(used[name], 1)
            dve.sem_inc(x1_ready, 1)
            dve.sem_inc(kv_ready, 2)
            with dve.Fori(0, NI) as i:
                chain = Chain(dve, chain_sem, 6 + 3 + 2, i)

                def normalise(rows, turn):
                    for g in range(G):
                        last = dve.bn_stats(stats[:, g, :], rows[:, g, :])
                    chain.link_before_aggregate(last)
                    for g in range(G):
                        last = dve.bn_aggr(mv[:, g, :], stats[:, g, :])
                    chain.link(last)
                    dve.tensor_scalar(ve[:], mv[:, :, 1], 1e-5, None, ALU.add).then_inc(ve_ready, 1)
                    dve.wait_ge(rstd_ready, per_batch(i, 2, turn + 1))
                    for g in range(G):
                        last = dve.tensor_scalar(xn[:, g, :], rows[:, g, :], mv[:, g, 0:1], rstd[:, g:g + 1], ALU.subtract, ALU.mult)
                    last.then_inc(xn_ready, 1)

                dve.wait_ge(loaded, per_batch(i, 32, 32))
                normalise(x, 0)
                dve.wait_ge(used["xt"], i + 2)
                dve.wait_ge(used["ct"], i + 2)
                sx4, xx4 = (t[:].rearrange("p k (g t) -> p k g t", g=G) for t in (sx, xx))
                xa_now = xa[:, :, :, 1:P + 1]
                dve.tensor_tensor(sx4, xa[:, :, :, 0:P], xa_now, ALU.subtract).then_inc(sx_ready, 1)
                dve.wait_ge(sx_ready, per_batch(i, 2, 1))
                for hf in range(KT):
                    last = dve.scalar_tensor_tensor(xx4[:, hf], sx4[:, hf], col("maa_x")[:, hf:hf + 1], xa_now[:, hf], ALU.mult, ALU.add)
                last.then_inc(xx_ready, 1)
                for n, name in enumerate(ORDER):
                    f = MIX[name]
                    dve.wait_ge(ready["m2" + name], i + 1)
                    for hf in range(KT):
                        last = dve.scalar_tensor_tensor(mix_tmp[:, n % 2, hf, :], at["m2" + name][:, hf * N:(hf + 1) * N], col(f"stack{f}")[:, hf:hf + 1],
                                                        sx[:, hf, :], ALU.add, ALU.mult)
                    last.then_inc(used["m2" + name], 1)
                    dve.wait_ge(used["m2" + name], i + 2)
                    dve.tensor_tensor(xm[:, f].rearrange("p k (g t) -> p k g t", g=G), mix_tmp[:, n % 2].rearrange("p k (g t) -> p k g t", g=G), xa_now, ALU.add)\
                        .then_inc(xm_ready, 1)
                dve.wait_ge(used["kp"], i + 2)
                dve.wait_ge(s0_loaded, per_batch(i, 32, 32))
                for n, (g, hf) in enumerate(UNITS):
                    p = n % 2
                    sw = swept[p].rearrange("p (j t) -> p j t", j=HS)
                    kv3, vr3, ro3 = (t[p].rearrange("p (j t) -> p j t", j=HS) for t in (kv, v_rep, read_out))
                    now = slice(g * P, (g + 1) * P)
                    dve.wait_ge(v_rep_loaded[p], per_batch(i, 32, 16 * (n // 2) + 16))
                    dve.tensor_tensor(kv3, vr3, k[:, hf, now].unsqueeze(1).broadcast_to([P, HS, P]), ALU.mult).then_inc(kv_ready, 1)
                    dve.tensor_copy(sw[:, :, 0], s0[:, hf, g, :]).then_inc(col0_ready, 1)
                    dve.wait_ge(kv_ready, per_batch(i, NU, n + 3))
                    dve.wait_ge(col0_ready, per_batch(i, NU, n + 1))
                    if n == 0:
                        dve.wait_ge(decay_ready, i + 1)
                    for j in range(HS):
                        last = dve.tensor_tensor_scan(sw[:, j, 1:P + 1], decay[:, hf, now], kv3[:, j, :], sw[:, j, 0:1], ALU.mult, ALU.add)
                    last.then_inc(swept_ready, 1)
                    dve.wait_ge(swept_ready, per_batch(i, NU, n + 1))
                    dve.wait_ge(units_done, per_batch(i, NU, n + 1))
                    dve.scalar_tensor_tensor(ro3, kv3, col("u")[:, hf:hf + 1], sw[:, :, 0:P], ALU.mult, ALU.add).then_inc(read_ready, 1)
                dve.wait_ge(th_ready, per_batch(i, 2, 1))
                dve.scalar_tensor_tensor(sg[:].rearrange("p k n -> p (k n)"), th[:].rearrange("p k n -> p (k n)"), 1.0, at["gp"][:], ALU.add, ALU.mult)\
                    .then_inc(used["gp"], 1)
                dve.wait_ge(ready["wkv"], i + 1)
                heads = at["wkv"][:].rearrange("p (a j h) -> p a h j", a=G * KT, j=HS)
                oc4 = oc[:].rearrange("p g (k h j) -> p (g k) h j", k=KT, j=HS)
                chain.link(dve.tensor_reduce(sums[:], heads, X_AXIS, ALU.add))
                chain.link(dve.tensor_scalar(nmean[:], sums[:], -1.0 / HS, None, ALU.mult))
                dve.tensor_tensor(oc4, heads, nmean[:].unsqueeze(3).broadcast_to([P, G * KT, NH, HS]), ALU.add).then_inc(oc_ready, 1)
                dve.wait_ge(oc_sq_ready, i + 1)
                dve.sem_inc(used["wkv"], 1)
                chain.link(dve.tensor_reduce(sq_sums[:], oc_sq[:].rearrange("p g (k h j) -> p (g k) h j", k=KT, j=HS), X_AXIS, ALU.add))
                dve.tensor_scalar(gve[:], sq_sums[:], 1.0 / HS, 1e-5, ALU.mult, ALU.add).then_inc(gve_ready, 1)
                dve.wait_ge(grstd_ready, i + 1)
                dve.tensor_tensor(oc4, oc4, grstd[:].unsqueeze(3).broadcast_to([P, G * KT, NH, HS]), ALU.mult).then_inc(ocn_ready, 1)
                dve.wait_ge(used["ogt"], i + 2)
                dve.wait_ge(used["gp"], i + 2)
                dve.scalar_tensor_tensor(og[:], og[:], 0.5, sg[:], ALU.mult, ALU.mult).then_inc(og_ready, 1)
                dve.wait_ge(ready["wo"], i + 1)
                dve.tensor_tensor(x1[:], at["wo"][:].rearrange("p (g e) -> p g e", g=G), x[:], ALU.add).then_inc(used["wo"], 1)
                dve.wait_ge(used["wo"], i + 2)
                dve.sem_inc(x1_ready, 1)
                normalise(x1, 1)
                dve.wait_ge(used["xt2"], i + 2)
                dve.tensor_tensor(sx4, xc[:, :, :, 0:P], xa_now, ALU.subtract).then_inc(sx_ready, 1)
                dve.wait_ge(sx_ready, per_batch(i, 2, 2))
                for name, to in (("ffn_k", xk2), ("ffn_r", xr2)):
                    to4 = to[:].rearrange("p k (g t) -> p k g t", g=G)
                    for hf in range(KT):
                        last = dve.scalar_tensor_tensor(to4[:, hf], sx4[:, hf], col(name)[:, hf:hf + 1], xa_now[:, hf], ALU.mult, ALU.add)
                    last.then_inc(xk2_ready, 1)
                dve.wait_ge(used["rr"], i + 2)
                chain.link(dve.tensor_scalar(rr[:], rr[:], 0.5, 0.5, ALU.mult, ALU.add))
                dve.wait_ge(ready["kvp"], i + 1)
                chain.link(dve.tensor_tensor(rr[:], at["kvp"][:].rearrange("p (g e) -> p g e", g=G), rr[:], ALU.mult))
                dve.sem_inc(used["kvp"], 1)
                dve.wait_ge(stored, per_batch(i, 16, 16))
                dve.tensor_tensor(out[:], rr[:], x1[:], ALU.add).then_inc(out_ready, 1)
                chain.close()

        @block.gpsimd
        def _(pool):
            pool.sem_inc(stored, 16)
            pool.sem_inc(v_stored, 32)
            if prefetch:
                prefetch[0](pool)
            with pool.Fori(0, NI) as i:
                pool.wait_ge(ve_ready, per_batch(i, 2, 1))
                pool.tensor_tensor(rstd[:], ve[:], mhalf[:, 0:G], ALU.pow).then_inc(rstd_ready, 1)
                pool.wait_ge(used["rp"], i + 2)
                for n, (g, hf) in enumerate(UNITS):
                    pool.wait_ge(read_ready, per_batch(i, NU, n + 1))
                    ro3 = read_out[n % 2].rearrange("p (j t) -> p j t", j=HS)
                    pool.tensor_tensor(ro3, ro3, r[:, hf, g * P:(g + 1) * P].unsqueeze(1).broadcast_to([P, HS, P]), ALU.mult).then_inc(out_prod_ready, 1)
                pool.wait_ge(gve_ready, i + 1)
                pool.tensor_tensor(grstd[:], gve[:], mhalf[:, 0:G * KT * NH].rearrange("p (a h) -> p a h", h=NH), ALU.pow).then_inc(grstd_ready, 1)
                pool.wait_ge(ve_ready, per_batch(i, 2, 2))
                pool.tensor_tensor(rstd[:], ve[:], mhalf[:, 0:G], ALU.pow).then_inc(rstd_ready, 1)

        @block.scalar
        def _(act):
            for name in ("xt", "ct", "m1", "vp", "kp", "td1", "td2", "rp", "ogt", "xt2", "rr", "kk"):
                act.sem_inc(used[name], 1)
            act.sem_inc(units_done, 2)
            with act.Fori(0, NI) as i:
                def got(name):
                    act.wait_ge(ready[name], i + 1)
                    return at[name]

                first = got("ct")[:, 0:2 * KT * G].rearrange("p (k g r) -> p k g r", k=KT, g=G)
                act.activation(xa[:, :, :, 0], first[:, :, :, 1], ACT.Copy)
                act.activation(state0[:], first[:, :, :, 0], ACT.Copy).then_inc(used["ct"], 1)
                o = got("xt")
                for hf in range(KT):
                    last = act.activation(xa[:, hf, :, 1:P + 1], by_batch(o[:, hf * N:(hf + 1) * N]), ACT.Identity, bias=col("ln1_b")[:, hf:hf + 1], scale=col("ln1_w")[:, hf:hf + 1])
                last.then_inc(used["xt"], 1)
                o = got("m1")
                act.activation(mix_a[:], o[:, 0:N], ACT.Tanh).then_inc(mix_ready, 1)
                act.activation(mix_b[:], o[0:32, N:2 * N], ACT.Tanh).then_inc(mix_ready, 1)
                act.wait_ge(mix_ready, per_batch(i, 2, 2))
                act.sem_inc(used["m1"], 1)
                act.wait_ge(v_stored, per_batch(i, 32, 32))
                act.activation(v[:].rearrange("p k n -> p (k n)"), got("vp")[:], ACT.Copy).then_inc(used["vp"], 1)
                act.activation(k[:].rearrange("p k n -> p (k n)"), got("kp")[:], ACT.Copy).then_inc(used["kp"], 1)
                act.activation(td[:], got("td1")[0:64, 0:N], ACT.Tanh).then_inc(used["td1"], 1)
                act.activation(r[:].rearrange("p k n -> p (k n)"), got("rp")[:], ACT.Copy).then_inc(used["rp"], 1)
                o = got("td2")
                for hf in range(KT):
                    last = act.activation(decay_log[:, hf, :], o[:, hf * N:(hf + 1) * N], ACT.Exp, bias=col("time_decay")[:, hf:hf + 1])
                last.then_inc(used["td2"], 1)
                act.wait_ge(used["td2"], i + 2)
                act.activation(decay[:], decay_log[:], ACT.Exp, scale=-1.0).then_inc(decay_ready, 1)
                act.activation(th[:].rearrange("p k n -> p (k n)"), got("gp")[:], ACT.Tanh, scale=0.5).then_inc(th_ready, 1)
                act.wait_ge(oc_ready, i + 1)
                act.activation(oc_sq[:], oc[:], ACT.Square).then_inc(oc_sq_ready, 1)
                o = got("ogt")
                for hf in range(KT):
                    last = act.activation(og[:, hf, :], o[:, hf * N:(hf + 1) * N], ACT.Identity, bias=col("gn_b")[:, hf:hf + 1], scale=col("gn_w")[:, hf:hf + 1])
                last.then_inc(used["ogt"], 1)
                o = got("xt2")
                act.activation(xc[:, :, :, 0], state0[:], ACT.Copy)
                for hf in range(KT):
                    last = act.activation(xc[:, hf, :, 1:P + 1], by_batch(o[:, hf * N:(hf + 1) * N]), ACT.Identity, bias=col("ln2_b")[:, hf:hf + 1], scale=col("ln2_w")[:, hf:hf + 1])
                last.then_inc(used["xt2"], 1)
                act.activation(relu[:].rearrange("p k n -> p (k n)"), got("kk")[:], ACT.Relu).then_inc(used["kk"], 1)
                act.wait_ge(used["kk"], i + 2)
                act.activation(kk[:], relu[:], ACT.Square).then_inc(kk_ready, 1)
                act.activation(rr[:].rearrange("p g e -> p (g e)"), got("rr")[:], ACT.Tanh, scale=0.5).then_inc(used["rr"], 1)
                act.sem_inc(th_ready, 1)


def deq_attention(nc, NB, w, consts, src, ctx_in, dst, prefetch):
    H, D, L = 16, 64, 256
    M = H * D // P
    ident, ones, mhalf = consts["ident"], consts["ones"], consts["mhalf"]

    J_GROUPS = [("q", 0), ("k", 0), ("v", 0, 0), ("v", 1, 0), ("q", 1), ("k", 1), ("q", 2), ("k", 2), ("v", 0, 1), ("v", 1, 1), ("q", 3), ("k", 3)]
    J_SLOT = {4: 0, 5: 1, 6: 4, 7: 5, 8: 6, 9: 7, 10: 9, 11: 10}
    NJ = len(J_GROUPS)
    TA0, WO, MEAN, VAR, BCAST, NL = 0, 4, 5, 6, 7, 8
    TA_SLOT = {0: 8, 1: 12, 2: 16}
    TAIL_SLOT = {1: 3, 2: WO, 3: MEAN, 4: VAR, 5: BCAST}

    with ExitStack() as st:
        sems = st.enter_context(Semaphores(nc))

        def sb(name, shape, dt=F32):
            return st.enter_context(nc.sbuf_tensor("l1_" + name, shape, dt))

        def sem(name):
            return sems.new("l1_" + name)

        z, u, z_res = sb("z", [P, L]), sb("u", [P, L]), sb("z_res", [P, L])
        qT, kT, v = sb("qT", [P, M, L]), sb("kT", [P, M, L]), sb("v", [P, 2, H * D])
        prob, probT = sb("prob", [P, 2, 2, L]), sb("probT", [P, 2, 2, L])
        negmax, rowsum, rinv = sb("negmax", [P, H, 2]), sb("rowsum", [P, H, 2]), sb("rinv", [P, H, 2])
        att, attT = sb("att", [P, 2, H * D]), sb("attT", [P, M, L])
        x1, xc, sq, out = sb("x1", [P, L]), sb("xc", [P, L]), sb("sq", [P, L]), sb("out", [P, L])
        var, rstd, diag = sb("var", [P, 2]), sb("rstd", [P, 2]), sb("diag", [P, 2, P])
        J = [st.enter_context(nc.psum_tensor(f"l1_J{i}", [P, 512], F32)) for i in range(2)]
        S = [st.enter_context(nc.psum_tensor(f"l1_S{i}", [P, 2, L], F32)) for i in range(2)]
        T = [st.enter_context(nc.psum_tensor(f"l1_T{i}", [P, 2, L], F32)) for i in range(2)]
        A = st.enter_context(nc.psum_tensor("l1_A", [P, 2, 4, D], F32))
        LB = st.enter_context(nc.psum_tensor("l1_L", [P, 512], F32))

        zu_loaded, zres_loaded, stored = sem("zu_loaded"), sem("zres_loaded"), sem("stored")
        j_ready, j_used = sem("j_ready"), [sem("j0_used"), sem("j1_used")]
        l_ready, l_used = sem("l_ready"), sem("l_used")
        scores_ready, max_ready = sem("scores_ready"), sem("max_ready")
        exp_done, t_ready, pv_done = sem("exp_done"), sem("t_ready"), sem("pv_done")
        probT_ready = [sem("probT0_ready"), sem("probT1_ready")]
        rinv_ready, att_ready = sem("rinv_ready"), sem("att_ready")
        x1_ready, xc_ready, sq_ready = sem("x1_ready"), sem("xc_ready"), sem("sq_ready")
        var_ready, rstd_ready, diag_ready, out_ready = sem("var_ready"), sem("rstd_ready"), sem("diag_ready"), sem("out_ready")
        block = st.enter_context(nc.Block())

        def batches(eng, boundary, main):
            boundary(None, 0)
            main(0, None)
            if NB > 1:
                with eng.Fori(1, NB) as b:
                    boundary(Batch(b, -1), b)
                    main(b, Batch(b, -1))
            boundary(NB - 1, None)
            main(None, NB - 1)

        @block.sync
        def _(sp):
            sp.sem_inc(stored, 16)

            def load(b, done):
                if done is not None:
                    sp.wait_ge(j_ready, per_batch(done, NJ, NJ + 1))
                sp.dma_start(z[:], src[b]).then_inc(zu_loaded, 16)
                sp.dma_start(u[:], ctx_in[b]).then_inc(zu_loaded, 16)
                if done is not None:
                    sp.wait_ge(x1_ready, per_batch(done, 1, 2))
                sp.dma_start(z_res[:], src[b]).then_inc(zres_loaded, 16)

            load(0, None)
            if NB > 1:
                with sp.Fori(0, NB - 1) as b:
                    load(b + 1, b)
                    sp.wait_ge(out_ready, b + 1)
                    sp.dma_start(dst[b], out[:]).then_inc(stored, 16)
            sp.wait_ge(out_ready, NB)
            sp.dma_start(dst[NB - 1], out[:]).then_inc(stored, 16)
            sp.wait_ge(stored, 16 * NB + 16)
            if prefetch:
                prefetch[1](sp)

        @block.tensor
        def _(pe):
            pe.sem_inc(t_ready, 2)
            pe.sem_inc(pv_done, 2)
            pe.sem_inc(j_ready, 1)

            def project(b, g):
                kind = J_GROUPS[g]
                bank = J[g % 2]
                pe.wait_ge(j_used[g % 2], per_batch(b, NJ // 2, g // 2 + 1))
                if kind[0] == "v":
                    _, s, c = kind
                    f0 = 2 * H * D + c * 512
                    pe.matmul(bank[:], z[:, s * P:(s + 1) * P], w["wq"][s][:, f0:f0 + 512], start=True, stop=False)
                    last = pe.matmul(bank[:], u[:, s * P:(s + 1) * P], w["wi"][s][:, f0:f0 + 512], start=False, stop=True)
                else:
                    for mm in range(2):
                        f0 = (0 if kind[0] == "q" else H * D) + (2 * kind[1] + mm) * P
                        for s in range(2):
                            o = bank[:, mm * L + s * P:mm * L + (s + 1) * P]
                            pe.matmul(o, w["wq"][s][:, f0:f0 + P], z[:, s * P:(s + 1) * P], start=True, stop=False)
                            last = pe.matmul(o, w["wi"][s][:, f0:f0 + P], u[:, s * P:(s + 1) * P], start=False, stop=True)
                last.then_inc(j_ready, 1)

            def j_evacuated(b, g):
                pe.wait_ge(j_used[g % 2], per_batch(b, NJ // 2, g // 2 + 2))

            def scores(b, n):
                m, r0 = n // 2, D * (n % 2)
                if n % 4 == 0:
                    q = J_GROUPS.index(("q", n // 4))
                    j_evacuated(b, q), j_evacuated(b, q + 1)
                pe.wait_ge(exp_done, per_batch(b, H, n + 1))
                for it in range(2):
                    last = pe.matmul(S[n % 2][:, it, :], qT[r0:r0 + D, m, it * P:(it + 1) * P], kT[r0:r0 + D, m, :], start=True, stop=True)
                last.then_inc(scores_ready, 1)

            def transposes(b, n):
                pe.wait_ge(exp_done, per_batch(b, H, n + 3))
                pe.wait_ge(probT_ready[n % 2], per_batch(b, H // 2, n // 2 + 1))
                for jt in range(2):
                    for it in range(2):
                        last = pe.transpose(T[n % 2][:, jt, it * P:(it + 1) * P], prob[:, n % 2, it, jt * P:(jt + 1) * P], ident[:])
                last.then_inc(t_ready, 1)

            def attend(b, n):
                if n % 8 == 0:
                    g = J_GROUPS.index(("v", 0, n // 8))
                    j_evacuated(b, g), j_evacuated(b, g + 1)
                pe.wait_ge(probT_ready[n % 2], per_batch(b, H // 2, n // 2 + 2))
                if n % 4 == 0:
                    pe.wait_ge(att_ready, per_batch(b, 4, n // 4 + 1))
                for it in range(2):
                    for jt in range(2):
                        last = pe.matmul(A[:, it, n % 4, :], probT[:, n % 2, jt, it * P:(it + 1) * P],
                                         v[:, jt, n * D:(n + 1) * D], start=(jt == 0), stop=(jt == 1))
                last.then_inc(pv_done, 1)

            def into_l(b, g):
                pe.wait_ge(l_used, per_batch(b, NL, g + 1))
                if g < WO:
                    pe.wait_ge(att_ready, per_batch(b, 4, g + 2))
                    for c in range(2):
                        for it in range(2):
                            last = pe.transpose(LB[:, c * L + it * P:c * L + (it + 1) * P], att[:, it, (2 * g + c) * P:(2 * g + c + 1) * P], ident[:])
                elif g == WO:
                    for kt in range(M):
                        last = pe.matmul(LB[:, :L], w["wo"][:, kt, :], attT[:, kt, :], start=(kt == 0), stop=(kt == M - 1))
                elif g == MEAN:
                    last = pe.matmul(LB[:, :L], ones[:], x1[:], start=True, stop=True)
                elif g == VAR:
                    pe.wait_ge(sq_ready, per_batch(b, 1, 1))
                    for c in range(2):
                        last = pe.matmul(LB[:, c:c + 1], sq[:, c * P:(c + 1) * P], ones[:, 0:1], start=True, stop=True)
                else:
                    pe.wait_ge(diag_ready, per_batch(b, 1, 1))
                    for c in range(2):
                        last = pe.matmul(LB[:, c * P:(c + 1) * P], consts["full1"][:], diag[:, c, :], start=True, stop=True)
                last.then_inc(l_ready, 1)

            def boundary(old, new):
                if new is not None:
                    pe.wait_ge(zu_loaded, per_batch(new, 32, 32))
                for i in range(3):
                    if old is not None and i < 2:
                        transposes(old, H - 2 + i)
                    if new is not None:
                        project(new, i)
                    if old is not None:
                        attend(old, H - 3 + i)
                        if H + i in TA_SLOT.values():
                            into_l(old, 2)
                if new is not None:
                    project(new, 3)

            def main(b, old):
                for n in range(H):
                    if b is not None:
                        scores(b, n)
                        for g, slot in J_SLOT.items():
                            if slot == n:
                                project(b, g)
                        if n >= 2:
                            transposes(b, n - 2)
                        if n >= 3:
                            attend(b, n - 3)
                        for a, slot in TA_SLOT.items():
                            if slot == n:
                                into_l(b, TA0 + a)
                    if old is not None and n in TAIL_SLOT:
                        into_l(old, TAIL_SLOT[n])

            batches(pe, boundary, main)

        @block.vector
        def _(dve):
            dve.sem_inc(j_used[0], 1)
            dve.sem_inc(l_used, 1)
            dve.sem_inc(probT_ready[0], 1)
            dve.sem_inc(att_ready, 1)
            dve.sem_inc(x1_ready, 1)

            def evacuate(b, g):
                kind = J_GROUPS[g]
                dve.wait_ge(j_ready, per_batch(b, NJ, g + 2))
                if kind[0] == "q":
                    for mm in range(2):
                        m = 2 * kind[1] + mm
                        last = dve.tensor_scalar(qT[:, m, :], J[0][:, mm * L:(mm + 1) * L], w["bias"][:, m:m + 1], 0.125, ALU.add, ALU.mult)
                else:
                    last = dve.tensor_copy(v[:, kind[1], kind[2] * 512:(kind[2] + 1) * 512], J[0][:])
                last.then_inc(j_used[0], 1)

            def head_max(b, n):
                dve.wait_ge(scores_ready, per_batch(b, H, n + 1))
                dve.tensor_reduce(negmax[:, n, :], S[n % 2][:], X_AXIS, ALU.max, negate=True).then_inc(max_ready, 1)

            def take_turned(b, n):
                dve.wait_ge(t_ready, per_batch(b, H, n + 3))
                dve.wait_ge(pv_done, per_batch(b, H, n + 1))
                dve.tensor_copy(probT[:, 0], T[0][:]).then_inc(probT_ready[0], 1)

            def divide(b, a):
                dve.wait_ge(pv_done, per_batch(b, H, 4 * a + 6))
                dve.reciprocal(rinv[:, 4 * a:4 * a + 4, :], rowsum[:, 4 * a:4 * a + 4, :]).then_inc(rinv_ready, 1)
                dve.wait_ge(rinv_ready, per_batch(b, 4, a + 1))
                dve.tensor_tensor(att[:, :, 4 * a * D:(4 * a + 4) * D].rearrange("p i (h d) -> p i h d", h=4), A[:],
                                  rinv[:, 4 * a:4 * a + 4, :].rearrange("p h i -> p i h").unsqueeze(3).broadcast_to([P, 2, 4, D]),
                                  ALU.mult).then_inc(att_ready, 1)

            def from_l(b, g):
                if g < WO and g % 2:
                    return
                dve.wait_ge(l_ready, per_batch(b, NL, g + 1))
                if g < WO:
                    dve.tensor_copy(attT[:, 2 * g:2 * g + 2, :], LB[:].rearrange("p (c l) -> p c l", c=2)).then_inc(l_used, 1)
                elif g == WO:
                    dve.wait_ge(zres_loaded, per_batch(b, 16, 16))
                    dve.scalar_tensor_tensor(x1[:], LB[:, :L], w["bo"], z_res[:], ALU.add, ALU.add).then_inc(l_used, 1)
                    dve.wait_ge(l_used, per_batch(b, NL, WO + 2))
                    dve.sem_inc(x1_ready, 1)
                elif g == MEAN:
                    dve.tensor_tensor(xc[:], x1[:], LB[:, :L], ALU.subtract).then_inc(l_used, 1)
                    dve.wait_ge(l_used, per_batch(b, NL, MEAN + 2))
                    dve.sem_inc(xc_ready, 1)
                elif g == VAR:
                    dve.tensor_scalar(var[:], LB[:, 0:2], 1e-5, None, ALU.add).then_inc(l_used, 1)
                    dve.wait_ge(l_used, per_batch(b, NL, VAR + 2))
                    dve.sem_inc(var_ready, 1)
                    dve.wait_ge(rstd_ready, per_batch(b, 1, 1))
                    for c in range(2):
                        last = dve.tensor_scalar(diag[:, c, :], ident[:], rstd[:, c:c + 1], None, ALU.mult)
                    last.then_inc(diag_ready, 1)
                else:
                    dve.wait_ge(stored, per_batch(b, 16, 16))
                    dve.tensor_tensor(out[:], xc[:], LB[:, :L], ALU.mult).then_inc(l_used, 1)
                    dve.wait_ge(l_used, per_batch(b, NL, BCAST + 2))
                    dve.sem_inc(out_ready, 1)

            def boundary(old, new):
                for i in range(3):
                    if old is not None and i == 0:
                        take_turned(old, H - 2)
                    if new is not None and i % 2 == 0:
                        evacuate(new, i)
                    if old is not None and i == 0:
                        from_l(old, 2)
                if old is not None:
                    divide(old, 3)

            def main(b, old):
                for n in range(H):
                    if b is not None:
                        head_max(b, n)
                        for g, slot in J_SLOT.items():
                            if slot == n and g % 2 == 0:
                                evacuate(b, g)
                        if n >= 2 and n % 2 == 0:
                            take_turned(b, n - 2)
                        if n >= 6 and n % 4 == 2:
                            divide(b, n // 4 - 1)
                        for a, slot in TA_SLOT.items():
                            if slot == n:
                                from_l(b, TA0 + a)
                    if old is not None and n in TAIL_SLOT:
                        from_l(old, TAIL_SLOT[n])

            batches(dve, boundary, main)

        @block.gpsimd
        def _(pool):
            if prefetch:
                prefetch[0](pool)
            with pool.Fori(0, NB) as b:
                pool.wait_ge(var_ready, b + 1)
                pool.tensor_tensor(rstd[:], var[:], mhalf[:, 0:2], ALU.pow).then_inc(rstd_ready, 1)

        @block.scalar
        def _(act):
            act.sem_inc(j_used[1], 1)
            act.sem_inc(probT_ready[1], 1)
            act.sem_inc(exp_done, 2)

            def evacuate(b, g):
                kind = J_GROUPS[g]
                act.wait_ge(j_ready, per_batch(b, NJ, g + 2))
                if kind[0] == "k":
                    o = kT[:, 2 * kind[1]:2 * kind[1] + 2, :].rearrange("p m l -> p (m l)")
                else:
                    o = v[:, kind[1], kind[2] * 512:(kind[2] + 1) * 512]
                act.activation(o, J[1][:], ACT.Copy).then_inc(j_used[1], 1)

            def exponentials(b, n):
                act.wait_ge(max_ready, per_batch(b, H, n + 1))
                act.wait_ge(t_ready, per_batch(b, H, n + 1))
                for it in range(2):
                    last = act.activation(prob[:, n % 2, it, :], S[n % 2][:, it, :], ACT.Exp, bias=negmax[:, n, it:it + 1],
                                          accum_out=rowsum[:, n, it:it + 1])
                last.then_inc(exp_done, 1)

            def take_turned(b, n):
                act.wait_ge(t_ready, per_batch(b, H, n + 3))
                act.wait_ge(pv_done, per_batch(b, H, n + 1))
                act.activation(probT[:, 1], T[1][:], ACT.Copy).then_inc(probT_ready[1], 1)

            def from_l(b, g):
                if g < WO and g % 2:
                    act.wait_ge(l_ready, per_batch(b, NL, g + 1))
                    act.activation(attT[:, 2 * g:2 * g + 2, :], LB[:].rearrange("p (c l) -> p c l", c=2), ACT.Copy).then_inc(l_used, 1)
                elif g == MEAN:
                    act.wait_ge(xc_ready, per_batch(b, 1, 1))
                    act.activation(sq[:], xc[:], ACT.Square).then_inc(sq_ready, 1)

            def boundary(old, new):
                if new is not None:
                    evacuate(new, 1)
                if old is not None:
                    take_turned(old, H - 1)
                if new is not None:
                    evacuate(new, 3)

            def main(b, old):
                for n in range(H):
                    if b is not None:
                        exponentials(b, n)
                        for g, slot in J_SLOT.items():
                            if slot == n and g % 2:
                                evacuate(b, g)
                        if n >= 3 and n % 2:
                            take_turned(b, n - 2)
                        for a, slot in TA_SLOT.items():
                            if slot == n:
                                from_l(b, TA0 + a)
                    if old is not None and n in TAIL_SLOT:
                        from_l(old, TAIL_SLOT[n])

            batches(act, boundary, main)


def perceiver_attention(nc, NB, w, consts, src, kv_in, mask, row16_in, dst, prefetch):
    H, D, NK = 16, 16, 2 * P
    M = H // 4
    ident, mhalf = consts["ident"], consts["mhalf"]
    CTX_T, LAT_T, K0, Q, V, NJ = 0, 1, 2, 4, 5, 6
    HJ = NJ // 2
    HALVES = {1: [(K0, 0)], 2: [(K0, 1)], 3: [(K0 + 1, 0)], 4: [(K0 + 1, 1)], 5: [(Q, 0)], 6: [(Q, 1)], 7: [(V, 0), (V, 1)]}
    AT_T, OUT, NL = 0, 1, 2
    L_SLOT = {3: AT_T, 4: OUT}
    NP = H // 2

    def head(n, i):
        m, g = 2 * (n // 4) + i, n % 4
        return m, g, 4 * m + g

    with ExitStack() as st:
        sems = st.enter_context(Semaphores(nc))

        def sb(name, shape, dt=F32):
            return st.enter_context(nc.sbuf_tensor("l2_" + name, shape, dt))

        def sem(name):
            return sems.new("l2_" + name)

        lat, ctx, resid = sb("lat", [P, E]), sb("ctx", [P, E]), sb("resid", [P, 2, E])
        allT = sb("allT", [P, KT, NK])
        qT, kT, v = sb("qT", [P, 2, M, P]), sb("kT", [P, 2, M, NK]), sb("v", [P, 2, 2, E])
        prob, probT = sb("prob", [P, 2, 2, NK]), sb("probT", [P, 2, 2, 2, P])
        negmax, rowsum, rinv = sb("negmax", [P, NP, 2]), sb("rowsum", [P, 2, NP, 2]), sb("rinv", [P, NP, 2])
        att, attT, out = sb("att", [P, E]), sb("attT", [P, KT, P]), sb("out", [P, E])
        J = [st.enter_context(nc.psum_tensor(f"l2_J{i}", [P, 512], F32)) for i in range(2)]
        S = [st.enter_context(nc.psum_tensor(f"l2_S{i}", [P, 2, NK], F32)) for i in range(2)]
        T = [st.enter_context(nc.psum_tensor(f"l2_T{i}", [P, 2, 2, P], F32)) for i in range(2)]
        A = st.enter_context(nc.psum_tensor("l2_A", [P, 512], F32))
        LB = st.enter_context(nc.psum_tensor("l2_L", [P, 512], F32))

        mask_in, mask_bias = sb("mask_in", [1, NB * P], I32), sb("mask_bias", [1, NB * P])
        row16, qb16 = sb("row16", [1, 512]), sb("qb16", [P, M])
        mask_loaded, mask_set, qb16_set = sem("mask_loaded"), sem("mask_set"), sem("qb16_set")
        loaded, stored = sem("loaded"), sem("stored")
        j_ready = sem("j_ready")
        j_used = [sem("j0_used"), sem("j1_used")]
        l_ready, l_used = sem("l_ready"), sem("l_used")
        scores_ready, max_ready = sem("scores_ready"), sem("max_ready")
        exp_done, t_ready, pv_done = sem("exp_done"), sem("t_ready"), sem("pv_done")
        probT_ready = [sem("probT0_ready"), sem("probT1_ready")]
        rinv_ready, att_ready, out_ready, resid_ready = sem("rinv_ready"), sem("att_ready"), sem("out_ready"), sem("resid_ready")
        block = st.enter_context(nc.Block())

        @block.sync
        def _(sp):
            sp.sem_inc(stored, 16)
            sp.dma_start(mask_in[:], mask).then_inc(mask_loaded, 16)
            sp.dma_start(row16[:], row16_in).then_inc(mask_loaded, 16)

            def load(b, before):
                if before is not None:
                    sp.wait_ge(resid_ready, per_batch(before, 1, 1))
                    sp.wait_ge(j_ready, per_batch(before, NJ, LAT_T + 1))
                sp.dma_start(lat[:], src[index(b)]).then_inc(loaded, 16)
                sp.dma_start(ctx[:], kv_in[index(b)]).then_inc(loaded, 16)

            def store(b):
                sp.wait_ge(out_ready, per_batch(b, 1, 1))
                sp.dma_start(dst[index(b)], out[:]).then_inc(stored, 16)

            load(0, None)
            load(1, 0)
            with sp.Fori(0, NB - 2) as b:
                load(Batch(b, 2), Batch(b, 1))
                store(b)
            store(NB - 2)
            store(NB - 1)
            sp.wait_ge(stored, 16 * NB + 16)
            if prefetch:
                prefetch[1](sp)

        @block.tensor
        def _(pe):
            pe.sem_inc(t_ready, 2)
            pe.sem_inc(pv_done, 2)
            pe.wait_ge(mask_set, 1)

            def j_free(b, g):
                pe.wait_ge(j_used[g % 2], per_batch(b, HJ, g // 2 + 1))

            def j_evacuated(b, g):
                pe.wait_ge(j_used[g % 2], per_batch(b, HJ, g // 2 + 2))

            def turn_inputs(b):
                pe.wait_ge(loaded, per_batch(b, 32, 32))
                for g, rows in ((CTX_T, ctx), (LAT_T, lat)):
                    j_free(b, g)
                    for kt in range(KT):
                        last = pe.transpose(J[g][:, kt * P:(kt + 1) * P], rows[:, kt * P:(kt + 1) * P], ident[:])
                    last.then_inc(j_ready, 1)

            def project(b, g, half):
                if half == 0:
                    j_free(b, g)
                if g == K0 and half == 0:
                    j_evacuated(b, CTX_T), j_evacuated(b, LAT_T)
                bank = J[g % 2]
                if g < Q:
                    m = 2 * (g - K0) + half
                    o = bank[:, half * NK:(half + 1) * NK]
                    for kt in range(KT):
                        pe.matmul(o, w["kw"][:, kt, m * P:(m + 1) * P], allT[:, kt, :], start=(kt == 0), stop=False)
                    last = pe.matmul(o[:, 0:P], row16[:, m * P:(m + 1) * P], mask_bias[0:1, bass.ds(per_batch(b, P, 0), P)], start=False, stop=True)
                elif g == Q:
                    for m in (2 * half, 2 * half + 1):
                        for kt in range(KT):
                            last = pe.matmul(bank[:, m * P:(m + 1) * P], w["qw"][:, kt, m * P:(m + 1) * P], allT[:, kt, P:NK], start=(kt == 0), stop=(kt == KT - 1))
                else:
                    for kt in range(KT):
                        last = pe.matmul(bank[:, half * E:(half + 1) * E], allT[:, kt, half * P:(half + 1) * P], w["vw"][:, kt, :], start=(kt == 0), stop=(kt == KT - 1))
                if half == 1:
                    last.then_inc(j_ready, 1)

            def scores(b, n):
                if n == 0:
                    j_evacuated(b, K0), j_evacuated(b, K0 + 1), j_evacuated(b, Q)
                pe.wait_ge(exp_done, per_batch(b, NP, n + 1))
                for i in range(2):
                    m, g, _ = head(n, i)
                    rows = slice(32 * g, 32 * g + 32)
                    last = pe.matmul(S[n % 2][:, i, :], qT[rows, parity(b), m, :], kT[rows, parity(b), m, :], start=True, stop=True, tile_position=(32 * g, 0))
                last.then_inc(scores_ready, 1)

            def turn(b, n):
                pe.wait_ge(exp_done, per_batch(b, NP, n + 3))
                pe.wait_ge(probT_ready[n % 2], per_batch(b, NP // 2, n // 2 + 1))
                for i in range(2):
                    for t in range(2):
                        last = pe.transpose(T[n % 2][:, i, t, :], prob[:, n % 2, i, t * P:(t + 1) * P], ident[:])
                last.then_inc(t_ready, 1)

            def attend(b, n):
                if n == 0:
                    j_evacuated(b, V)
                    pe.wait_ge(att_ready, per_batch(b, 1, 1))
                pe.wait_ge(probT_ready[n % 2], per_batch(b, NP // 2, n // 2 + 2))
                for i in range(2):
                    _, _, h = head(n, i)
                    for t in range(2):
                        last = pe.matmul(A[:, h * D:(h + 1) * D], probT[:, n % 2, i, t, :], v[:, parity(b), t, h * D:(h + 1) * D], start=(t == 0), stop=(t == 1))
                last.then_inc(pv_done, 1)

            def into_l(b, g):
                pe.wait_ge(l_used, per_batch(b, NL, g + 1))
                if g == AT_T:
                    pe.wait_ge(att_ready, per_batch(b, 1, 2))
                for kt in range(KT):
                    if g == AT_T:
                        last = pe.transpose(LB[:, kt * P:(kt + 1) * P], att[:, kt * P:(kt + 1) * P], ident[:])
                    else:
                        last = pe.matmul(LB[:, 0:E], attT[:, kt, :], w["ow"][:, kt, :], start=(kt == 0), stop=(kt == KT - 1))
                last.then_inc(l_ready, 1)

            def step(old, b, new):
                for n in range(NP):
                    if b is not None:
                        scores(b, n)
                    if new is not None:
                        if n == 0:
                            turn_inputs(new)
                        for g, half in HALVES.get(n, []):
                            project(new, g, half)
                    if old is not None and n in L_SLOT:
                        into_l(old, L_SLOT[n])
                    if n < 2 and old is not None:
                        attend(old, NP - 2 + n)
                    if n >= 2 and b is not None:
                        attend(b, n - 2)
                    if n == 0 and old is not None:
                        turn(old, NP - 1)
                    if n >= 1 and b is not None:
                        turn(b, n - 1)

            rotate(pe, NB, step)

        @block.vector
        def _(dve):
            dve.wait_ge(mask_loaded, 32)
            dve.tensor_scalar(mask_bias[:], mask_in[:], 0.0, -1e30, ALU.is_equal, ALU.mult).then_inc(mask_set, 1)
            dve.tensor_scalar(qb16[:], w["qb"], 1.0 / D, None, ALU.mult).then_inc(qb16_set, 1)
            dve.sem_inc(j_used[0], 1)
            dve.sem_inc(l_used, 1)
            dve.sem_inc(probT_ready[0], 1)
            dve.sem_inc(att_ready, 1)
            dve.wait_ge(qb16_set, 1)

            def evacuate(b, g):
                dve.wait_ge(j_ready, per_batch(b, NJ, g + 1))
                bank, p = J[g % 2], parity(b)
                if g == CTX_T:
                    last = dve.tensor_copy(allT[:, :, 0:P], bank[:, 0:E].rearrange("p (k t) -> p k t", k=KT))
                elif g == K0:
                    last = dve.tensor_tensor(kT[:, p, 0:2, :], bank[:].rearrange("p (m n) -> p m n", m=2), w["kb"][:, 0:2].unsqueeze(2).broadcast_to([P, 2, NK]), ALU.add)
                elif g == Q:
                    last = dve.scalar_tensor_tensor(qT[:, p], bank[:].rearrange("p (m t) -> p m t", m=M), 1.0 / D, qb16[:].unsqueeze(2).broadcast_to([P, M, P]),
                                                    ALU.mult, ALU.add)
                else:
                    last = dve.tensor_tensor(v[:, p], bank[:].rearrange("p (n e) -> p n e", n=2), w["vb"].unsqueeze(1).broadcast_to([P, 2, E]), ALU.add)
                last.then_inc(j_used[g % 2], 1)

            def take_turned(b, n):
                dve.wait_ge(t_ready, per_batch(b, NP, n + 3))
                dve.wait_ge(pv_done, per_batch(b, NP, n + 1))
                dve.tensor_copy(probT[:, 0], T[0][:]).then_inc(probT_ready[0], 1)

            def divide(b):
                dve.wait_ge(pv_done, per_batch(b, NP, NP + 2))
                dve.wait_ge(rinv_ready, per_batch(b, 1, 1))
                for mp in range(2):
                    cols = slice(mp * P, (mp + 1) * P)
                    last = dve.tensor_tensor(att[:, cols].rearrange("p (i g d) -> p i g d", i=2, g=4), A[:, cols].rearrange("p (i g d) -> p i g d", i=2, g=4),
                                             rinv[:, 4 * mp:4 * mp + 4, :].rearrange("p g i -> p i g").unsqueeze(3).broadcast_to([P, 2, 4, D]), ALU.mult)
                last.then_inc(att_ready, 1)

            def from_l(b, g):
                dve.wait_ge(l_ready, per_batch(b, NL, g + 1))
                if g == AT_T:
                    dve.tensor_copy(attT[:], LB[:, 0:E].rearrange("p (k t) -> p k t", k=KT)).then_inc(l_used, 1)
                else:
                    dve.wait_ge(resid_ready, per_batch(b, 1, 1))
                    dve.wait_ge(stored, per_batch(b, 16, 16))
                    dve.tensor_tensor(out[:], LB[:, 0:E], resid[:, parity(b), :], ALU.add).then_inc(l_used, 1)
                    dve.wait_ge(l_used, per_batch(b, NL, NL + 1))
                    dve.sem_inc(out_ready, 1)

            def step(old, b, new):
                for n in range(NP):
                    if n == 2 and old is not None:
                        divide(old)
                    if n >= 2 and n % 2 == 0 and b is not None:
                        take_turned(b, n - 2)
                    if n == 0 and old is not None:
                        take_turned(old, NP - 2)
                    if b is not None:
                        dve.wait_ge(scores_ready, per_batch(b, NP, n + 1))
                        dve.tensor_reduce(negmax[:, n, :], S[n % 2][:], X_AXIS, ALU.max, negate=True).then_inc(max_ready, 1)
                    if n == 1 and old is not None:
                        dve.wait_ge(exp_done, per_batch(old, NP, NP + 2))
                        dve.reciprocal(rinv[:], rowsum[:, parity(old)]).then_inc(rinv_ready, 1)
                    if new is not None:
                        for g, slot in ((CTX_T, 0), (K0, 2), (Q, 6), (V, 7)):
                            if slot == n:
                                evacuate(new, g)
                    if old is not None and n in L_SLOT:
                        from_l(old, L_SLOT[n])
                    if n == 6 and new is not None:
                        dve.wait_ge(loaded, per_batch(new, 32, 32))
                        dve.tensor_tensor(resid[:, parity(new), :], lat[:], w["ob"], ALU.add).then_inc(resid_ready, 1)

            rotate(dve, NB, step)

        @block.gpsimd
        def _(pool):
            if prefetch:
                prefetch[0](pool)

        @block.scalar
        def _(act):
            act.sem_inc(j_used[1], 1)
            act.sem_inc(probT_ready[1], 1)
            act.sem_inc(exp_done, 2)

            def evacuate(b, g):
                act.wait_ge(j_ready, per_batch(b, NJ, g + 1))
                if g == LAT_T:
                    last = act.activation(allT[:, :, P:NK], J[1][:, 0:E].rearrange("p (k t) -> p k t", k=KT), ACT.Copy)
                else:
                    for mm in range(2):
                        last = act.activation(kT[:, parity(b), 2 + mm, :], J[1][:, mm * NK:(mm + 1) * NK], ACT.Identity, bias=w["kb"][:, 2 + mm:3 + mm])
                last.then_inc(j_used[1], 1)

            def take_turned(b, n):
                act.wait_ge(t_ready, per_batch(b, NP, n + 3))
                act.wait_ge(pv_done, per_batch(b, NP, n + 1))
                act.activation(probT[:, 1], T[1][:], ACT.Copy).then_inc(probT_ready[1], 1)

            def exponentials(b, n):
                act.wait_ge(max_ready, per_batch(b, NP, n + 1))
                act.wait_ge(t_ready, per_batch(b, NP, n + 1))
                for i in range(2):
                    last = act.activation(prob[:, n % 2, i, :], S[n % 2][:, i, :], ACT.Exp, bias=negmax[:, n, i:i + 1], accum_out=rowsum[:, parity(b), n, i:i + 1])
                last.then_inc(exp_done, 1)

            def step(old, b, new):
                for n in range(NP):
                    if n >= 2 and n % 2 == 1 and b is not None:
                        take_turned(b, n - 2)
                    if n == 1 and old is not None:
                        take_turned(old, NP - 1)
                    if n == 0 and new is not None:
                        evacuate(new, LAT_T)
                    if b is not None:
                        exponentials(b, n)
                    if n == 4 and new is not None:
                        evacuate(new, K0 + 1)

            rotate(act, NB, step)


def gelu_mlp(nc, NB, w, consts, src, resid_in, dst, gelu, rms, tag, prefetch):
    G = 4
    F = 1024
    M = F // P
    ident, mhalf = consts["ident"], consts["mhalf"]
    NI = NB // G

    with ExitStack() as st:
        sems = st.enter_context(Semaphores(nc))

        def sb(name, shape, dt=F32):
            return st.enter_context(nc.sbuf_tensor(tag + name, shape, dt))

        def sem(name):
            return sems.new(tag + name)

        x, res, xn, out = sb("x", [P, G, E]), sb("res", [P, G, E]), sb("xn", [P, G, E]), sb("out", [P, G, E])
        resb = sb("resb", [P, G, E])
        stats, mv, ve, rstd, sqm = sb("stats", [P, G, 6]), sb("mv", [P, G, 2]), sb("ve", [P, G]), sb("rstd", [P, G]), sb("sqm", [P, G])
        xnT, hT = sb("xnT", [P, KT, G * P]), sb("hT", [P, M, G * P])
        XT = [st.enter_context(nc.psum_tensor(f"{tag}XT{i}", [P, 512], F32)) for i in range(KT)]
        H = [st.enter_context(nc.psum_tensor(f"{tag}H{i}", [P, 512], F32)) for i in range(4)]
        Y = [st.enter_context(nc.psum_tensor(f"{tag}Y{i}", [P, 2, E], F32)) for i in range(2)]

        x_loaded, res_loaded, stored = sem("x_loaded"), sem("res_loaded"), sem("stored")
        chain_sem, ve_ready, rstd_ready, xn_ready, resb_ready = sem("chain"), sem("ve_ready"), sem("rstd_ready"), sem("xn_ready"), sem("resb_ready")
        xt_ready, xnT_ready = sem("xt_ready"), sem("xnT_ready")
        h_ready, h_done = sem("h_ready"), sem("h_done")
        y_ready, y_done = sem("y_ready"), sem("y_done")
        block = st.enter_context(nc.Block())

        def rows(ap, i):
            return ap.rearrange("(n g) t e -> n t g e", g=G)[i]

        @block.sync
        def _(sp):
            with sp.Fori(0, NI) as i:
                sp.wait_ge(xn_ready, i + 1)
                sp.dma_start(x[:], rows(src, i)).then_inc(x_loaded, 16)
                sp.wait_ge(resb_ready, i + 1)
                sp.dma_start(res[:], rows(resid_in, i)).then_inc(res_loaded, 16)
                sp.wait_ge(y_done, per_batch(i, 2, 4))
                sp.dma_start(rows(dst, i), out[:]).then_inc(stored, 16)
            sp.wait_ge(stored, 16 * NI + 16)
            if prefetch:
                prefetch[1](sp)

        @block.tensor
        def _(pe):
            with pe.Fori(0, NI) as i:
                pe.wait_ge(xn_ready, i + 2)
                for kt in range(KT):
                    for g in range(G):
                        last = pe.transpose(XT[kt][:, g * P:(g + 1) * P], xn[:, g, kt * P:(kt + 1) * P], ident[:])
                    last.then_inc(xt_ready, 1)
                pe.wait_ge(xnT_ready, per_batch(i, KT, KT))
                for m in range(M):
                    pe.wait_ge(h_done, per_batch(i, M, m + 1))
                    for kt in range(KT):
                        last = pe.matmul(H[m % 4][:], w["w1"][:, kt, m * P:(m + 1) * P], xnT[:, kt, :], start=(kt == 0), stop=(kt == KT - 1))
                    last.then_inc(h_ready, 1)
                pe.wait_ge(h_done, per_batch(i, M, M + 4))
                for pair in range(G // 2):
                    pe.wait_ge(y_done, per_batch(i, 2, pair + 1))
                    for k in range(2):
                        g = 2 * pair + k
                        for m in range(M):
                            last = pe.matmul(Y[pair][:, k, :], hT[:, m, g * P:(g + 1) * P], w["w2"][:, m, :], start=(m == 0), stop=(m == M - 1))
                    last.then_inc(y_ready, 1)

        @block.vector
        def _(dve):
            dve.sem_inc(xn_ready, 1)
            dve.sem_inc(resb_ready, 1)
            dve.sem_inc(y_done, 2)
            with dve.Fori(0, NI) as i:
                dve.wait_ge(x_loaded, per_batch(i, 16, 16))
                chain = Chain(dve, chain_sem, 5 if rms else 3, i)
                for g in range(G):
                    last = dve.bn_stats(stats[:, g, :], x[:, g, :])
                chain.link_before_aggregate(last)
                for g in range(G):
                    last = dve.bn_aggr(mv[:, g, :], stats[:, g, :])
                chain.link(last)
                if rms:
                    chain.link(dve.tensor_tensor(sqm[:], mv[:, :, 0], mv[:, :, 0], ALU.mult))
                    chain.link(dve.tensor_tensor(sqm[:], mv[:, :, 1], sqm[:], ALU.add))
                    dve.tensor_scalar(ve[:], sqm[:], 1e-6, None, ALU.add).then_inc(ve_ready, 1)
                else:
                    dve.tensor_scalar(ve[:], mv[:, :, 1], 1e-5, None, ALU.add).then_inc(ve_ready, 1)
                chain.close()
                dve.wait_ge(res_loaded, per_batch(i, 16, 16))
                dve.tensor_tensor(resb[:], res[:], w["b2"].unsqueeze(1).broadcast_to([P, G, E]), ALU.add).then_inc(resb_ready, 1)
                dve.wait_ge(rstd_ready, i + 1)
                for g in range(G):
                    if rms:
                        last = dve.tensor_scalar(xn[:, g, :], x[:, g, :], rstd[:, g:g + 1], None, ALU.mult)
                    else:
                        last = dve.tensor_scalar(xn[:, g, :], x[:, g, :], mv[:, g, 0:1], rstd[:, g:g + 1], ALU.subtract, ALU.mult)
                last.then_inc(xn_ready, 1)
                for kt in range(KT):
                    dve.wait_ge(xt_ready, per_batch(i, KT, kt + 1))
                    dve.tensor_scalar(xnT[:, kt, :], XT[kt][:], w["scale"][:, kt:kt + 1], w["offset"][:, kt:kt + 1], ALU.mult, ALU.add).then_inc(xnT_ready, 1)
                dve.wait_ge(resb_ready, i + 2)
                dve.wait_ge(stored, per_batch(i, 16, 16))
                for pair in range(G // 2):
                    dve.wait_ge(y_ready, per_batch(i, 2, pair + 1))
                    dve.tensor_tensor(out[:, 2 * pair:2 * pair + 2, :], Y[pair][:], resb[:, 2 * pair:2 * pair + 2, :], ALU.add).then_inc(y_done, 1)

        @block.gpsimd
        def _(pool):
            pool.sem_inc(stored, 16)
            if prefetch:
                prefetch[0](pool)
            with pool.Fori(0, NI) as i:
                pool.wait_ge(ve_ready, i + 1)
                pool.tensor_tensor(rstd[:], ve[:], mhalf[:, 0:G], ALU.pow).then_inc(rstd_ready, 1)

        @block.scalar
        def _(act):
            act.sem_inc(h_done, 4)
            with act.Fori(0, NI) as i:
                for m in range(M):
                    act.wait_ge(h_ready, per_batch(i, M, m + 1))
                    act.activation(hT[:, m, :], H[m % 4][:], gelu, bias=w["b1"][:, m:m + 1]).then_inc(h_done, 1)


def cross_attention(nc, NB, w, consts, src, kv_in, dst, tag, prefetch):
    H, D = 16, 128
    scale = float(D) ** -0.5
    ident, mhalf = consts["ident"], consts["mhalf"]
    HPG = 4
    NG, NP = H // HPG, H // 2
    JS = ["ctx_T", "xn_T", "k0", "q0", "k1", "q1", "v0", "k2", "q2", "v1", "k3", "q3", "v2", "v3"]
    NJ = len(JS)
    HJ = NJ // 2
    BY_SCALAR = ("xn_T", "v0", "v1", "v2", "v3")

    with ExitStack() as st:
        sems = st.enter_context(Semaphores(nc))

        def sb(name, shape, dt=F32):
            return st.enter_context(nc.sbuf_tensor(tag + name, shape, dt))

        def sem(name):
            return sems.new(tag + name)

        x, ctx = sb("x", [P, E]), sb("ctx", [P, E])
        stats, mv, ve, rstd = sb("stats", [P, 6]), sb("mv", [P, 2]), sb("ve", [P, 1]), sb("rstd", [P, 1])
        xn, resid, out = sb("xn", [P, E]), sb("resid", [P, 2, E]), sb("out", [P, E])
        xnT, ctxT = sb("xnT", [P, KT, P]), sb("ctxT", [P, 2, KT, P])
        qT, kT, v = sb("qT", [P, H, P]), sb("kT", [P, H, P + 1]), sb("v", [P, H * D])
        prob, probT, attT = sb("prob", [P, H, P + 1]), sb("probT", [P, H, P]), sb("attT", [P, H, P])
        negmax, rowsum, rinv = sb("negmax", [P, H]), sb("rowsum", [P, H]), sb("rinv", [P, H])
        learned, learnedT = sb("learned", [P, 2, H]), sb("learnedT", [H, P])
        bqs = sb("bqs", [P, H])
        diag_bv, biasv_wo, row_bias = sb("diag_bv", [P, H, H]), sb("biasv_wo", [H, E]), sb("row_bias", [P, E])
        J = [st.enter_context(nc.psum_tensor(f"{tag}J{i}", [P, 512], F32)) for i in range(2)]
        S = [st.enter_context(nc.psum_tensor(f"{tag}S{i}", [P, 512], F32)) for i in range(2)]
        T = st.enter_context(nc.psum_tensor(tag + "T", [P, HPG, P], F32))
        C = st.enter_context(nc.psum_tensor(tag + "C", [P, HPG, P], F32))
        LT = st.enter_context(nc.psum_tensor(tag + "LT", [P, 512], F32))
        Y = st.enter_context(nc.psum_tensor(tag + "Y", [P, 512], F32))

        x_loaded, ctx_loaded, stored = sem("x_loaded"), sem("ctx_loaded"), sem("stored")
        setup_v, setup_pe, setup_done = sem("setup_v"), sem("setup_pe"), sem("setup_done")
        ln_chain, ve_ready, rstd_ready = sem("ln_chain"), sem("ve_ready"), sem("rstd_ready")
        xn_ready, resid_ready = sem("xn_ready"), sem("resid_ready")
        j_ready = sem("j_ready")
        j_used = [sem("j0_used"), sem("j1_used")]
        scores_ready, max_ready, exp_done = sem("scores_ready"), sem("max_ready"), sem("exp_done")
        rinv_ready, prob_ready = sem("rinv_ready"), sem("prob_ready")
        t_ready, t_used = sem("t_ready"), sem("t_used")
        c_ready, c_used = sem("c_ready"), sem("c_used")
        lt_ready, lt_used, y_ready, y_used = sem("lt_ready"), sem("lt_used"), sem("y_ready"), sem("y_used")
        out_ready = sem("out_ready")
        block = st.enter_context(nc.Block())

        @block.sync
        def _(sp):
            sp.sem_inc(stored, 16)

            def load(b, before):
                if before is not None:
                    sp.wait_ge(resid_ready, per_batch(before, 1, 1))
                    sp.wait_ge(j_ready, per_batch(before, NJ, 1))
                sp.dma_start(x[:], src[index(b)]).then_inc(x_loaded, 16)
                sp.dma_start(ctx[:], kv_in[index(b)]).then_inc(ctx_loaded, 16)

            def store(b):
                sp.wait_ge(out_ready, per_batch(b, 1, 1))
                sp.dma_start(dst[index(b)], out[:]).then_inc(stored, 16)

            load(0, None)
            load(1, 0)
            with sp.Fori(0, NB - 2) as b:
                load(Batch(b, 2), Batch(b, 1))
                store(b)
            store(NB - 2)
            store(NB - 1)
            sp.wait_ge(stored, 16 * NB + 16)
            if prefetch:
                prefetch[1](sp)

        @block.tensor
        def _(pe):
            pe.wait_ge(setup_v, 3)
            for h in range(H):
                last = pe.matmul(J[0][0:H, 0:E], diag_bv[:, h, :], w["wo"][:, h, :], start=(h == 0), stop=(h == H - 1))
            last.then_inc(setup_pe, 1)
            for h in range(H):
                last = pe.matmul(J[1][:, 0:E], w["bv"][:, h:h + 1].broadcast_to([P, P]), w["wo"][:, h, :], start=(h == 0), stop=(h == H - 1))
            last.then_inc(setup_pe, 1)
            pe.wait_ge(setup_done, 3)

            def j_free(b, name):
                g = JS.index(name)
                pe.wait_ge(j_used[g % 2], per_batch(b, HJ, g // 2 + 1))
                return J[g % 2]

            def j_evacuated(b, name):
                g = JS.index(name)
                pe.wait_ge(j_used[g % 2], per_batch(b, HJ, g // 2 + 2))

            def turn_inputs(b):
                bank = j_free(b, "ctx_T")
                pe.wait_ge(ctx_loaded, per_batch(b, 16, 16))
                for kt in range(KT):
                    last = pe.transpose(bank[:, kt * P:(kt + 1) * P], ctx[:, kt * P:(kt + 1) * P], ident[:])
                last.then_inc(j_ready, 1)
                bank = j_free(b, "xn_T")
                pe.wait_ge(xn_ready, per_batch(b, 1, 1))
                for kt in range(KT):
                    last = pe.transpose(bank[:, kt * P:(kt + 1) * P], xn[:, kt * P:(kt + 1) * P], ident[:])
                last.then_inc(j_ready, 1)

            def project(b, name):
                bank = j_free(b, name)
                kind, c = name[0], int(name[1])
                if name in ("k0", "q0"):
                    j_evacuated(b, "ctx_T" if kind == "k" else "xn_T")
                if kind == "v":
                    for kt in range(KT):
                        last = pe.matmul(bank[:], ctxT[:, parity(b), kt, :], w["wv"][:, kt, c * 512:(c + 1) * 512], start=(kt == 0), stop=(kt == KT - 1))
                else:
                    wt = w["wk"] if kind == "k" else w["wq"]
                    for i in range(HPG):
                        h = HPG * c + i
                        for kt in range(KT):
                            moving = ctxT[:, parity(b), kt, :] if kind == "k" else xnT[:, kt, :]
                            last = pe.matmul(bank[:, i * P:(i + 1) * P], wt[:, kt, h * D:(h + 1) * D], moving, start=(kt == 0), stop=(kt == KT - 1))
                last.then_inc(j_ready, 1)

            def scores(b, n):
                if n % 2 == 0:
                    j_evacuated(b, f"k{n // 2}"), j_evacuated(b, f"q{n // 2}")
                pe.wait_ge(exp_done, per_batch(b, NP, n + 1))
                for i in range(2):
                    h = 2 * n + i
                    last = pe.matmul(S[n % 2][:, i * (P + 1):(i + 1) * (P + 1)], qT[:, h, :], kT[:, h, :], start=True, stop=True)
                last.then_inc(scores_ready, 1)

            def turn(b, g):
                pe.wait_ge(prob_ready, per_batch(b, NP, 2 * g + 2))
                pe.wait_ge(t_used, per_batch(b, NG, g + 1))
                for i in range(HPG):
                    last = pe.transpose(T[:, i, :], prob[:, HPG * g + i, 0:P], ident[:])
                last.then_inc(t_ready, 1)

            def attend(b, g):
                j_evacuated(b, f"v{g}")
                pe.wait_ge(t_used, per_batch(b, NG, g + 2))
                pe.wait_ge(c_used, per_batch(b, NG, g + 1))
                for i in range(HPG):
                    h = HPG * g + i
                    last = pe.matmul(C[:, i, :], v[:, h * D:(h + 1) * D], probT[:, h, :], start=True, stop=True)
                last.then_inc(c_ready, 1)

            def output(b, g):
                pe.wait_ge(c_used, per_batch(b, NG, g + 2))
                if g == 0:
                    pe.wait_ge(y_used, per_batch(b, 1, 1))
                for h in range(HPG * g, HPG * g + HPG):
                    pe.matmul(Y[:, 0:E], attT[:, h, :], w["wo"][:, h, :], start=(h == 0), stop=False)

            def step(old, b, new):
                for g in range(NG):
                    done, last_group = (old, NG - 1) if g == 0 else (b, g - 1)
                    if b is not None:
                        scores(b, 2 * g)
                    if done is not None:
                        turn(done, last_group)
                    if b is not None:
                        scores(b, 2 * g + 1)
                    if g == 0:
                        if old is not None:
                            pe.transpose(LT[0:H, 0:P], learned[:, parity(old), :], ident[:]).then_inc(lt_ready, 1)
                            attend(old, NG - 1)
                        if b is not None:
                            project(b, "v3")
                        if new is not None:
                            turn_inputs(new)
                        if old is not None:
                            output(old, NG - 1)
                            pe.wait_ge(lt_used, per_batch(old, 1, 1))
                            pe.matmul(Y[:, 0:E], learnedT[:], biasv_wo[:], start=False, stop=True).then_inc(y_ready, 1)
                        if new is not None:
                            project(new, "k0")
                            project(new, "q0")
                    else:
                        if new is not None:
                            project(new, f"k{g}")
                        if b is not None:
                            attend(b, g - 1)
                        if new is not None:
                            project(new, f"q{g}")
                            project(new, f"v{g - 1}")
                        if b is not None:
                            output(b, g - 1)

            rotate(pe, NB, step)

        @block.vector
        def _(dve):
            dve.tensor_scalar(bqs[:], w["bq"], scale, None, ALU.mult).then_inc(setup_v, 1)
            dve.memset(diag_bv[:], 0.0).then_inc(setup_v, 1)
            dve.wait_ge(setup_v, 2)
            dve.tensor_tensor(diag_bv[:].rearrange("p a c -> p (a c)")[:, 0:H * H:H + 1], w["bias_v"], w["bv"], ALU.subtract).then_inc(setup_v, 1)
            dve.tensor_copy(kT[:, :, P], w["bias_k"]).then_inc(setup_done, 1)
            dve.wait_ge(setup_pe, 1)
            dve.tensor_copy(biasv_wo[:], J[0][0:H, 0:E]).then_inc(setup_done, 1)
            dve.wait_ge(setup_pe, 2)
            dve.tensor_tensor(row_bias[:], J[1][:, 0:E], w["bo"], ALU.add).then_inc(setup_done, 1)
            dve.wait_ge(setup_done, 3)
            dve.sem_inc(t_used, 1)
            dve.sem_inc(y_used, 1)
            for j in range(2):
                dve.sem_inc(j_used[j], 1)

            def evacuate(b, name):
                i = JS.index(name)
                dve.wait_ge(j_ready, per_batch(b, NJ, i + 1))
                bank = J[i % 2]
                if name == "ctx_T":
                    last = dve.tensor_copy(ctxT[:, parity(b)], bank[:, 0:E].rearrange("p (k t) -> p k t", k=KT))
                else:
                    h = HPG * int(name[1])
                    heads = bank[:].rearrange("p (h t) -> p h t", h=HPG)
                    if name[0] == "k":
                        last = dve.tensor_tensor(kT[:, h:h + HPG, 0:P], heads, w["bk"][:, h:h + HPG].unsqueeze(2).broadcast_to([P, HPG, P]), ALU.add)
                    else:
                        last = dve.scalar_tensor_tensor(qT[:, h:h + HPG, :], heads, scale, bqs[:, h:h + HPG].unsqueeze(2).broadcast_to([P, HPG, P]), ALU.mult, ALU.add)
                last.then_inc(j_used[i % 2], 1)

            def pair_max(b, n):
                dve.wait_ge(scores_ready, per_batch(b, NP, n + 1))
                dve.tensor_reduce(negmax[:, 2 * n:2 * n + 2], S[n % 2][:, 0:2 * (P + 1)].rearrange("p (h t) -> p h t", h=2),
                                  X_AXIS, ALU.max, negate=True).then_inc(max_ready, 1)

            def invert_sums(b, n):
                dve.wait_ge(exp_done, per_batch(b, NP, n + 3))
                dve.reciprocal(rinv[:, 2 * n:2 * n + 2], rowsum[:, 2 * n:2 * n + 2]).then_inc(rinv_ready, 1)

            def normalise_input(b):
                dve.wait_ge(x_loaded, per_batch(b, 16, 16))
                chain = Chain(dve, ln_chain, 3, b)
                chain.link_before_aggregate(dve.bn_stats(stats[:], x[:]))
                chain.link(dve.bn_aggr(mv[:], stats[:]))
                chain.close()
                dve.tensor_scalar(ve[:], mv[:, 1:2], 1e-5, None, ALU.add).then_inc(ve_ready, 1)
                dve.wait_ge(rstd_ready, per_batch(b, 1, 1))
                dve.tensor_scalar(xn[:], x[:], mv[:, 0:1], rstd[:], ALU.subtract, ALU.mult).then_inc(xn_ready, 1)

            def step(old, b, new):
                for g in range(NG):
                    done, last_group = (old, NG - 1) if g == 0 else (b, g - 1)
                    if b is not None:
                        pair_max(b, 2 * g)
                    if done is not None:
                        dve.wait_ge(t_ready, per_batch(done, NG, last_group + 1))
                        h = HPG * last_group
                        dve.tensor_copy(probT[:, h:h + HPG, :], T[:]).then_inc(t_used, 1)
                    if b is not None:
                        pair_max(b, 2 * g + 1)
                        invert_sums(b, 2 * g)
                    if g == 0:
                        if new is not None:
                            normalise_input(new)
                        if old is not None:
                            dve.wait_ge(lt_ready, per_batch(old, 1, 1))
                            dve.tensor_copy(learnedT[:], LT[0:H, 0:P]).then_inc(lt_used, 1)
                        if new is not None:
                            evacuate(new, "ctx_T")
                    if b is not None:
                        invert_sums(b, 2 * g + 1)
                    if g == 0 and old is not None:
                        dve.wait_ge(y_ready, per_batch(old, 1, 1))
                        dve.wait_ge(resid_ready, per_batch(old, 1, 1))
                        dve.wait_ge(stored, per_batch(old, 16, 16))
                        dve.tensor_tensor(out[:], Y[:, 0:E], resid[:, parity(old), :], ALU.add).then_inc(y_used, 1)
                        dve.wait_ge(y_used, per_batch(old, 1, 2))
                        dve.sem_inc(out_ready, 1)
                    if new is not None:
                        evacuate(new, f"k{g}")
                        evacuate(new, f"q{g}")
                        if g == 1:
                            dve.tensor_tensor(resid[:, parity(new), :], x[:], row_bias[:], ALU.add).then_inc(resid_ready, 1)

            rotate(dve, NB, step)

        @block.gpsimd
        def _(pool):
            if prefetch:
                prefetch[0](pool)

            def probabilities(b, n):
                pool.wait_ge(rinv_ready, per_batch(b, NP, n + 1))
                pr, ri = prob[:, 2 * n:2 * n + 2, 0:P], rinv[:, 2 * n:2 * n + 2]
                pool.tensor_tensor(learned[:, parity(b), 2 * n:2 * n + 2], prob[:, 2 * n:2 * n + 2, P], ri, ALU.mult)
                pool.tensor_tensor(pr, pr, ri.unsqueeze(2).broadcast_to([P, 2, P]), ALU.mult).then_inc(prob_ready, 1)

            def step(old, b, new):
                for g in range(NG):
                    if b is not None:
                        probabilities(b, 2 * g)
                    if g == 0 and new is not None:
                        pool.wait_ge(ve_ready, per_batch(new, 1, 1))
                        pool.tensor_tensor(rstd[:], ve[:], mhalf[:, 0:1], ALU.pow).then_inc(rstd_ready, 1)
                    if b is not None:
                        probabilities(b, 2 * g + 1)

            rotate(pool, NB, step)

        @block.scalar
        def _(act):
            act.sem_inc(c_used, 1)
            act.sem_inc(exp_done, 2)

            def evacuate(b, name):
                i = JS.index(name)
                act.wait_ge(j_ready, per_batch(b, NJ, i + 1))
                bank = J[i % 2]
                if name == "xn_T":
                    for kt in range(KT):
                        last = act.activation(xnT[:, kt, :], bank[:, kt * P:(kt + 1) * P], ACT.Identity, bias=w["offset"][:, kt:kt + 1], scale=w["scale"][:, kt:kt + 1])
                else:
                    c = int(name[1])
                    last = act.activation(v[:, c * 512:(c + 1) * 512], bank[:], ACT.Copy)
                last.then_inc(j_used[i % 2], 1)

            def exponentials(b, n):
                act.wait_ge(max_ready, per_batch(b, NP, n + 1))
                for i in range(2):
                    h = 2 * n + i
                    last = act.activation(prob[:, h, :], S[n % 2][:, i * (P + 1):(i + 1) * (P + 1)], ACT.Exp, bias=negmax[:, h:h + 1], accum_out=rowsum[:, h:h + 1])
                last.then_inc(exp_done, 1)

            def take_attended(b, g):
                act.wait_ge(c_ready, per_batch(b, NG, g + 1))
                act.activation(attT[:, HPG * g:HPG * g + HPG, :], C[:], ACT.Copy).then_inc(c_used, 1)

            def step(old, b, new):
                for g in range(NG):
                    if b is not None:
                        exponentials(b, 2 * g)
                        exponentials(b, 2 * g + 1)
                    if g == 0:
                        if old is not None:
                            take_attended(old, NG - 1)
                        if b is not None:
                            evacuate(b, "v3")
                        if new is not None:
                            evacuate(new, "xn_T")
                    else:
                        if b is not None:
                            take_attended(b, g - 1)
                        if new is not None:
                            evacuate(new, f"v{g - 1}")

            rotate(act, NB, step)


L0_COLS = ["ln1_w", "ln1_b", "ln2_w", "ln2_b", "maa_x", "time_decay", "u", "gn_w", "gn_b", "ffn_k", "ffn_r",
           "stack0", "stack1", "stack2", "stack3", "stack4"]
HEAD_COLS = ["bq", "bk", "bv", "bias_k", "bias_v"]
COLUMNS = ([("l0_" + n, 2) for n in L0_COLS] + [("l1_bias", 8), ("l1_bo", 1)]
           + [("l2_qb", 4), ("l2_kb", 4), ("l2m_b1", 8), ("l2m_scale", 2), ("l2m_offset", 2)]
           + [(f"l3{s}_{n}", 16) for s in "ab" for n in HEAD_COLS]
           + [(f"l3{s}_{n}", 2) for s in "ab" for n in ("scale", "offset")]
           + [("l3m_b1", 8), ("l3m_scale", 2), ("l3m_offset", 2)])
ROWS = ["l2_vb", "l2_ob", "l2m_b2", "l3a_bo", "l3b_bo", "l3m_b2"]
N_COLS = sum(n for _, n in COLUMNS)


def col_at(name):
    at = 0
    for n, width in COLUMNS:
        if n == name:
            return at, width
        at += width
    raise KeyError(name)


L0_W = [("l0_maa_w1", 2 * 160, P), ("l0_maa_w2a", 256, P), ("l0_maa_w2b", 256, 32), ("l0_wv", 512, P), ("l0_wk", 512, P), ("l0_td_w1", 128, P),
        ("l0_td_w2", 256, 64), ("l0_wr", 512, P), ("l0_wg", 512, P), ("l0_wo", 512, P), ("l0_wfk", 512, P), ("l0_wfr", 512, P), ("l0_wfv", 512, P)]
L1_W = [("l1_wq0", 3072, P), ("l1_wi0", 3072, P), ("l1_wq1", 3072, P), ("l1_wi1", 3072, P), ("l1_wo", 1024, P)]
L2_W = [("l2_kw", 1024, P), ("l2_vw", 512, P), ("l2_qw", 1024, P), ("l2_ow", 512, P), ("l2m_w1", 2048, P), ("l2m_w2", 2048, P)]
L3A_W = [("l3a_wk", 4096, P), ("l3a_wq", 4096, P), ("l3a_wv", 4096, P), ("l3a_wo", 4096, P)]
L3B_W = [("l3b" + n[3:], c, p) for n, c, p in L3A_W]
L3M_W = [("l3m_w1", 2048, P), ("l3m_w2", 2048, P)]


def program(nc, dram, out):
    NB = dram["x"].shape[0]
    hidden = [nc.dram_tensor(f"hidden{n}", [NB, P, E], F32, kind="Internal").ap() for n in range(6)]
    v_dram = nc.dram_tensor("v_dram", [2, E, P], F32, kind="Internal").ap()

    with ExitStack() as st:
        def sb(name, shape, dt=F32):
            return st.enter_context(nc.sbuf_tensor(name, shape, dt))

        region = [sb("region0", [P, REGION]), sb("region1", [P, REGION])]
        columns, rows = sb("columns", [P, N_COLS]), sb("rows", [P, len(ROWS), E])
        ident, pick = sb("ident", [P, P]), sb("pick", [P, 16])
        mean_of, full1, mhalf = sb("mean_of", [P, P]), sb("full1", [P, P]), sb("mhalf", [P, 64])
        loaded = {name: st.enter_context(nc.semaphore("loaded_" + name)) for name in ("small", "l0", "l1", "l2", "l3a", "l3b", "l3m")}
        constants_set = st.enter_context(nc.semaphore("constants_set"))
        consts = dict(ident=ident, pick=pick, ones=mean_of, full1=full1, mhalf=mhalf)

        def col(name):
            at, width = col_at(name)
            return columns[:, at:at + width]

        def row(name):
            return rows[:, ROWS.index(name), :]

        def places(weights, reg):
            at, out_ = 0, {}
            for name, words, parts in weights:
                out_[name] = region[reg][0:parts, at:at + words]
                at += words
            return out_

        place = {}
        for weights, reg in ((L0_W, 0), (L1_W, 1), (L2_W, 0), (L3A_W, 1), (L3B_W, 0), (L3M_W, 1)):
            place.update(places(weights, reg))

        def loader(name, weights):
            def start(eng):
                for n, _, _ in weights:
                    eng.dma_start(place[n], dram[n]).then_inc(loaded[name], 16)

            def wait(eng):
                eng.wait_ge(loaded[name], 16 * len(weights))
            return start, wait

        def tiles(name, k):
            return place[name].rearrange("p (k n) -> p k n", k=k)

        start_l0, wait_l0 = loader("l0", L0_W)
        with nc.Block() as block:
            @block.sync
            def _(sp):
                for to, name in ((columns, "columns"), (ident, "ident"), (pick, "pick")):
                    sp.dma_start(to[:], dram[name]).then_inc(loaded["small"], 16)
                sp.dma_start(rows[:].rearrange("p r e -> p (r e)"), dram["rows"].partition_broadcast(P)).then_inc(loaded["small"], 16)
                start_l0(sp)
                sp.wait_ge(loaded["small"], 64)
                wait_l0(sp)

            @block.vector
            def _(dve):
                dve.memset(mean_of[:], 1.0 / P).then_inc(constants_set, 1)
                dve.memset(full1[:], 1.0).then_inc(constants_set, 1)
                dve.memset(mhalf[:], -0.5).then_inc(constants_set, 1)
                dve.wait_ge(constants_set, 3)

        w0 = {n[3:]: place[n] for n, _, _ in L0_W}
        for n in ("maa_w1", "td_w1", "wr", "wk", "wv", "wg", "wo", "wfk", "wfr", "wfv"):
            w0[n] = tiles("l0_" + n, 2)
        w0["col"] = lambda name: col("l0_" + name)
        rwkv_block(nc, NB, w0, dict(region=region[0], at=REGION), consts, dram["x"], dram["ctx"], v_dram, hidden[0], loader("l1", L1_W))

        w1 = dict(wq=[place["l1_wq0"], place["l1_wq1"]], wi=[place["l1_wi0"], place["l1_wi1"]], wo=tiles("l1_wo", 8), bias=col("l1_bias"), bo=col("l1_bo"))
        deq_attention(nc, NB, w1, consts, hidden[0], dram["ctx"], hidden[1], loader("l2", L2_W))

        w2 = dict(kw=tiles("l2_kw", 2), vw=tiles("l2_vw", 2), qw=tiles("l2_qw", 2), ow=tiles("l2_ow", 2), qb=col("l2_qb"), kb=col("l2_kb"),
                  vb=row("l2_vb"), ob=row("l2_ob"))
        perceiver_attention(nc, NB, w2, consts, hidden[1], dram["ctx"], dram["mask"], dram["row16"], hidden[2], loader("l3a", L3A_W))

        def mlp_weights(tag):
            return dict(w1=tiles(tag + "_w1", 2), w2=tiles(tag + "_w2", 8), b1=col(tag + "_b1"), b2=row(tag + "_b2"), scale=col(tag + "_scale"), offset=col(tag + "_offset"))

        gelu_mlp(nc, NB, mlp_weights("l2m"), consts, hidden[2], hidden[1], hidden[3], ACT.Gelu_apprx_tanh, True, "l2m_", None)

        def attention_weights(tag):
            w = {n: col(f"{tag}_{n}") for n in HEAD_COLS + ["scale", "offset"]}
            w.update({n: tiles(f"{tag}_{n}", 2) for n in ("wq", "wk", "wv")})
            w.update(wo=tiles(tag + "_wo", 16), bo=row(tag + "_bo"))
            return w

        cross_attention(nc, NB, attention_weights("l3a"), consts, hidden[3], dram["ctx"], hidden[4], "l3a_", loader("l3b", L3B_W))
        cross_attention(nc, NB, attention_weights("l3b"), consts, hidden[4], dram["ctx"], hidden[5], "l3b_", loader("l3m", L3M_W))
        gelu_mlp(nc, NB, mlp_weights("l3m"), consts, hidden[5], hidden[5], out, ACT.Gelu, False, "l3m_", None)


def layout(inputs, np):
    def c(a):
        return np.ascontiguousarray(a)

    def tiled(a):
        return c(a.reshape(-1, P, a.shape[1]).transpose(1, 0, 2)).reshape(P, -1)

    def columns_of(a):
        return a.reshape(-1, P).T

    def slots(a):
        o = np.zeros(a.shape[:-1] + (32,), a.dtype)
        o[..., :16] = a
        return o.reshape(a.shape[:-2] + (512,))

    l0 = {k[9:]: v for k, v in inputs.items() if k.startswith("L0_xattn_")}
    l1 = {k[9:]: v for k, v in inputs.items() if k.startswith("L1_xattn_")}
    l2 = {k[9:]: v for k, v in inputs.items() if k.startswith("L2_xattn_")}
    l3 = {k[9:]: v for k, v in inputs.items() if k.startswith("L3_xattn_")}
    a = dict(x=inputs["x"], ctx=inputs["ctx_2048"], mask=inputs["mask_BxS2_ik0"].reshape(1, -1))
    a["l0_maa_w1"], a["l0_maa_w2a"], a["l0_maa_w2b"] = tiled(l0["maa_w1"]), l0["maa_w2"][:4].reshape(P, E), l0["maa_w2"][4]
    a["l0_td_w1"], a["l0_td_w2"] = tiled(l0["td_w1"]), l0["td_w2"]
    for n in ("r", "k", "v", "g", "o", "fk", "fr", "fv"):
        a["l0_w" + n] = tiled(l0["W" + n].T)
    for s in "01":
        a["l1_wq" + s], a["l1_wi" + s] = l1["Wqkv" + s].T, l1["Winj" + s].T
    a["l1_wo"] = tiled(l1["Wo"].T)
    kv = l2["kv_w"].reshape(E, 16, 16, 2)
    a["l2_qw"], a["l2_kw"] = tiled(slots(l2["q_w"].reshape(E, 16, 16))), tiled(slots(kv[..., 0]))
    a["l2_vw"], a["l2_ow"] = tiled(kv[..., 1].reshape(E, E)), tiled(l2["out_w"])
    a["l2m_w1"], a["l2m_w2"] = tiled(l2["mlp_w1"]), tiled(l2["mlp_w2"])
    for s, n in (("a", "1"), ("b", "2")):
        for m in ("wq", "wk", "wv", "wo"):
            a[f"l3{s}_{m}"] = tiled(l3[m + n])
    a["l3m_w1"], a["l3m_w2"] = tiled(l3["w_fc1"]), tiled(l3["w_fc2"])

    kv_b = l2["kv_b"].reshape(16, 16, 2)
    one16 = np.zeros((16, 32), np.float32)
    one16[:, 16] = 1.0
    q_b = slots(l2["q_b"].reshape(16, 16)).reshape(16, 32)
    q_b[:, 16] = 1.0
    v = {"l1_bias": l1["r_w_bias"], "l1_bo": l1["bo"], "l2_qb": q_b, "l2_kb": slots(kv_b[..., 0]), "l2m_b1": l2["mlp_b1"],
         "l2m_scale": l2["postnorm_w"], "l2m_offset": np.zeros(E, np.float32),
         "l3m_b1": l3["b_fc1"], "l3m_scale": l3["ln_mlp_scale"], "l3m_offset": l3["ln_mlp_offset"]}
    for n in L0_COLS:
        v["l0_" + n] = l0["maa_stack"][0, int(n[5:])] if n.startswith("stack") else l0[n.replace("ffn_", "ffn_maa_")]
    for s, n in (("a", "1"), ("b", "2")):
        for m in HEAD_COLS:
            v[f"l3{s}_{m}"] = l3[m + n]
        v[f"l3{s}_scale"], v[f"l3{s}_offset"] = l3[f"ln{n}_scale"], l3[f"ln{n}_offset"]
    a["columns"] = np.concatenate([columns_of(v[n]) for n, _ in COLUMNS], axis=1)
    r = {"l2_vb": kv_b[..., 1].reshape(E), "l2_ob": l2["out_b"], "l2m_b2": l2["mlp_b2"], "l3a_bo": l3["bo1"], "l3b_bo": l3["bo2"], "l3m_b2": l3["b_fc2"]}
    a["rows"] = np.concatenate([r[n] for n in ROWS])
    a["ident"] = np.eye(P, dtype=np.float32)
    a["pick"] = (np.arange(P)[:, None] // 8 == np.arange(16)).astype(np.float32)
    a["row16"] = one16.reshape(1, 512)
    return {k: c(x) for k, x in a.items()}


def kernel(**inputs):
    import numpy as _np
    import concourse.bacc as _bacc
    from concourse import mybir as _mybir
    from concourse.bass_utils import run_bass_kernel_spmd as _run

    nc = _bacc.Bacc("TRN2", target_bir_lowering=False, num_devices=1)
    arrays = layout({k: _np.asarray(v) for k, v in inputs.items()}, _np)
    dram = {n: nc.dram_tensor(n + "_dram", a.shape, _mybir.dt.from_np(a.dtype), kind="ExternalInput").ap() for n, a in arrays.items()}
    out = nc.dram_tensor("out_dram", arrays["x"].shape, _mybir.dt.float32, kind="ExternalOutput").ap()
    program(nc, dram, out)
    r = _run(nc, [{n + "_dram": a for n, a in arrays.items()}], core_ids=[0])
    return r.results[0]["out_dram"]
```

```python
from contextlib import ExitStack

import numpy as np

import concourse.bass as bass
from concourse import mybir

F32 = mybir.dt.float32
F32R = mybir.dt.float32r
I32 = mybir.dt.int32
ALU = mybir.AluOpType
ACT = mybir.ActivationFunctionType
X_AXIS = mybir.AxisListType.X

P = 128
E = 256
KT = E // P
REGION = 16384


def split_matmul(pe, out, stationary, moving, start=True, stop=True):
    (s_hi, s_lo), (m_hi, m_lo) = stationary, moving
    pe.matmul(out, s_hi, m_hi, start=start, stop=False)
    pe.matmul(out, s_hi, m_lo, start=False, stop=False)
    return pe.matmul(out, s_lo, m_hi, start=False, stop=stop)


class Batch:

    def __init__(self, reg, plus=0, times=1):
        self.reg, self.plus, self.times = reg, plus, times

    def shifted(self, by):
        return Batch(self.reg, self.plus + by, self.times)


def per_batch(b, count, done):
    if isinstance(b, Batch):
        b, count, done = b.reg, count * b.times, done + b.plus * count
    return b * count + done if done else b * count


def index(b):
    return per_batch(b, 1, 0)


def parity(b):
    return b.plus % 2 if isinstance(b, Batch) else b % 2


def rotate(eng, NB, step, peeled=1):
    assert NB % 2 == 0 and NB // 2 > peeled
    step(None, None, 0)
    step(None, 0, 1)
    with eng.Fori(0, NB // 2 - peeled) as reg:
        for b in (Batch(reg, 1, 2), Batch(reg, 2, 2)):
            step(b.shifted(-1), b, b.shifted(1))
    for b in range(NB + 1 - 2 * peeled, NB - 1):
        step(b - 1, b, b + 1)
    step(NB - 2, NB - 1, None)
    step(NB - 1, None, None)


class Semaphores:

    def __init__(self, nc):
        self.nc, self.all = nc, []

    def new(self, name):
        self.all.append(self.nc.alloc_semaphore(name=name))
        return self.all[-1]

    def __enter__(self):
        return self

    def __exit__(self, *_):
        self.nc.clear_and_free_semaphores(self.all)
        self.nc.all_engine_barrier()


class Chain:

    def __init__(self, eng, sem, per, b):
        self.eng, self.sem, self.per, self.b, self.n = eng, sem, per, b, 0

    def add(self, ins):
        self.n += 1
        ins.then_inc(self.sem, 1)

    def settle(self):
        self.eng.wait_ge(self.sem, per_batch(self.b, self.per, self.n))

    def link(self, ins):
        self.add(ins)
        self.settle()

    def link_before_aggregate(self, ins):
        self.add(ins)
        self.settle_before_aggregate()

    def settle_before_aggregate(self):
        self.settle()
        self.n += 1
        self.eng.sem_inc(self.sem, 1)

    def close(self):
        assert self.n == self.per, (self.n, self.per)


def rwkv_block(nc, NB, w, work, consts, src, state, v_dram, dst, prefetch):
    G, HS, NH = 2, 8, 16
    NI, N = NB // G, G * P
    MIX = dict(k=0, w=1, v=2, r=3, g=4)
    ORDER = "vkwrg"
    ident, mhalf = consts["ident"], consts["mhalf"]
    col = w["col"]

    with ExitStack() as st:
        sems = st.enter_context(Semaphores(nc))

        def sb(name, shape, dt=F32):
            return st.enter_context(nc.sbuf_tensor("l0_" + name, shape, dt))

        def sem(name):
            return sems.new("l0_" + name)

        def carve(size):
            work["at"] -= size
            return work["region"][:, work["at"]:work["at"] + size]

        tanh_table = sb("tanh_table", [P, 1])
        x, xn, xa = sb("x", [P, G, E]), sb("xn", [P, G, E]), sb("xa", [P, KT, G, P + 1])
        first_rows, s0 = sb("first_rows", [2, G, E]), sb("s0", [P, 2, KT, G, HS])
        stats, mv, ve, rstd = sb("stats", [P, G, 6]), sb("mv", [P, G, 2]), sb("ve", [P, G]), sb("rstd", [P, G])
        sx, xx = sb("sx", [P, KT, N]), sb("xx", [P, KT, N])
        mix_a, mix_b, mix_tmp = sb("mix_a", [P, N]), sb("mix_b", [32, N]), sb("mix_tmp", [P, KT, N])
        xm = sb("xm", [P, 5, KT, N])
        td, decay_log, v = sb("td", [64, N]), sb("decay_log", [P, KT, N]), sb("v", [P, KT, N])
        th = decay_log
        r, k, decay, sg = (sb(n, [P, 2, KT, N]) for n in ("r", "k", "decay", "sg"))
        v_rep = [carve(HS * P) for _ in range(2)]
        kv = [carve(HS * P) for _ in range(2)]
        swept = [carve(HS * (P + 1)) for _ in range(2)]
        read_out = [carve(HS * P) for _ in range(2)]
        eps = sb("eps", [P, 1])
        oc, oc_sq, og = (sb(n, [P, KT, N]) for n in ("oc", "oc_sq", "og"))
        gstd, grstd = sb("gstd", [P, KT * G, NH]), sb("grstd", [P, KT * G, NH])
        grstd8 = oc_sq
        x_again, x1, xn2, out, rr = (sb(n, [P, G, E]) for n in ("x_again", "x1", "xn2", "out", "rr"))
        first_row0, stats2, mv2, ve2, rstd2 = sb("first_row0", [1, G, E]), sb("stats2", [P, G, 6]), sb("mv2", [P, G, 2]), sb("ve2", [P, G]), sb("rstd2", [P, G])
        xc, xk2 = sb("xc", [P, KT, G, P + 1]), sb("xk2", [P, KT, N])
        xr2, kk = x_again[:].rearrange("p g e -> p (g e)").rearrange("p (k n) -> p k n", k=KT), xk2
        sx2, relu = oc_sq, oc
        bank = [st.enter_context(nc.psum_tensor(f"l0_B{i}", [P, 512], F32)) for i in range(8)]

        USES = [("ct", "m2w", "td1"), ("xt", "m2r", "rp"), ("m1", "m2g", "td2"), ("m2v", "vp", "gp"), ("m2k", "kp"),
                ("wkv",),
                ("gm", "gv", "gr", "ct2", "xt2", "rr"), ("wo", "kk", "kvp")]
        at = {name: bank[n] for n, names in enumerate(USES) for name in names}
        ready = {name: sem(name + "_ready") for names in USES for name in names}
        used = {name: sem(name + "_used") for names in USES for name in names}
        a_loaded, c_loaded, s0_loaded, stored = sem("a_loaded"), sem("c_loaded"), sem("s0_loaded"), sem("stored")
        v_stored, v_rep_loaded = sem("v_stored"), [sem(f"v_rep{n}_loaded") for n in range(2)]
        a_chain, ve_ready, rstd_ready, xn_ready = sem("a_chain"), sem("ve_ready"), sem("rstd_ready"), sem("xn_ready")
        c_chain, ve2_ready, rstd2_ready, xn2_ready = sem("c_chain"), sem("ve2_ready"), sem("rstd2_ready"), sem("xn2_ready")
        sx_ready, xx_ready, sx2_ready = sem("sx_ready"), sem("xx_ready"), sem("sx2_ready")
        mix_ready, xm_ready = sem("mix_ready"), sem("xm_ready")
        decay_ready, th_ready, sg_ready = sem("decay_ready"), sem("th_ready"), sem("sg_ready")
        kv_ready, col0_ready, swept_ready, read_ready, out_prod_ready = (sem(n) for n in ("kv_ready", "col0_ready", "swept_ready", "read_ready", "out_prod_ready"))
        waits_passed = sem("waits_passed")
        units_done = sem("units_done")
        oc_ready, oc_sq_ready, gstd_ready, grstd_ready, halved, eps_set = (sem(n) for n in ("oc_ready", "oc_sq_ready", "gstd_ready", "grstd_ready", "halved", "eps_set"))
        og_ready, x1_ready, xk2_ready, kk_ready, out_ready = (sem(n) for n in ("og_ready", "x1_ready", "xk2_ready", "relu_squared", "out_ready"))
        block = st.enter_context(nc.Block())
        UNITS = [(g, hf) for g in range(G) for hf in range(KT)]
        NU = len(UNITS)

        def by_batch(ap):
            return ap.rearrange("p (g t) -> p g t", g=G)

        def flat(ap):
            return ap.rearrange("p k n -> p (k n)")

        def once(i, ahead=0):
            return per_batch(i, 1, 1 + ahead)

        def of(ap, i):
            return ap.rearrange("(n g) t e -> n t g e", g=G)[index(i)]

        @block.sync
        def _(sp):
            sp.sem_inc(stored, 16)
            sp.sem_inc(v_stored, 32)

            def stand():
                sp.sem_inc(waits_passed, 1)

            def load_a(i, before):
                if before is not None:
                    sp.wait_ge(xn_ready, once(before))
                    stand()
                    sp.wait_ge(used["ct"], once(before, 1))
                    stand()
                sp.dma_start(x[:], of(src, i)).then_inc(a_loaded, 16)
                sp.dma_start(first_rows[:], state.rearrange("(n g) t e -> n t g e", g=G)[index(i), 0:2]).then_inc(a_loaded, 16)

            def load_c(i, before):
                if before is not None:
                    sp.wait_ge(used["rr"], once(before, 1))
                    stand()
                sp.dma_start(x_again[:], of(src, i)).then_inc(c_loaded, 16)
                sp.dma_start(first_row0[:], state.rearrange("(n g) t e -> n t g e", g=G)[index(i), 0:1]).then_inc(c_loaded, 16)

            def load_s0(i, old):
                if old is not None:
                    sp.wait_ge(col0_ready, per_batch(old, NU, NU))
                for g in range(G):
                    rows = state.rearrange("(n g) t e -> n g (t e)", g=G)[index(i), g, 2 * E:(2 + HS) * E]
                    sp.dma_start(s0[:, parity(i), :, g, :], rows.rearrange("(h p j) -> p h j", h=KT, j=HS)).then_inc(s0_loaded, 16)

            def store_v(i):
                sp.wait_ge(used["vp"], once(i, 1))
                stand()
                for hf in range(KT):
                    sp.dma_start(v_dram[index(i), :, hf * P:(hf + 1) * P, :].rearrange("g c t -> c g t"), by_batch(v[:, hf, :])).then_inc(v_stored, 16)

            def load_v(i, n):
                if n == 0:
                    sp.wait_ge(v_stored, per_batch(i, 32, 64))
                    stand()
                g, hf = UNITS[n]
                sp.wait_ge(kv_ready, per_batch(i, NU, n + 1))
                rows = v_dram[index(i), g, hf * P:(hf + 1) * P, :].rearrange("(h j) t -> h (j t)", j=HS)
                sp.dma_start(v_rep[n % 2], rows.unsqueeze(1).broadcast_to([NH, HS, HS * P])).then_inc(v_rep_loaded[n % 2], 16)

            def step(old, b, new):
                if b is None and new is not None:
                    load_a(new, None)
                if new is not None and (not isinstance(new, int) or new + 1 < NI):
                    load_a(new + 1 if isinstance(new, int) else new.shifted(1), new)
                if b is not None:
                    load_v(b, 2)
                    load_v(b, 3)
                    load_c(b, old)
                if new is not None:
                    load_s0(new, old)
                    store_v(new)
                    load_v(new, 0)
                    load_v(new, 1)
                if old is not None:
                    sp.wait_ge(out_ready, once(old))
                    sp.dma_start(of(dst, old), out[:]).then_inc(stored, 16)

            rotate(sp, NI, step, peeled=2)
            sp.wait_ge(stored, 16 * NI + 16)
            if prefetch:
                prefetch[1](sp)

        @block.tensor
        def _(pe):
            pe.sem_inc(units_done, 2)

            def take(name, i):
                names = next(n for n in USES if name in n)
                j = names.index(name)
                pe.wait_ge(used[names[j - 1]], once(i, 1 if j else 0))
                return at[name]

            def by_channel(i, name, wt, moving):
                o = take(name, i)
                for ho in range(KT):
                    for kt in range(KT):
                        last = pe.matmul(o[:, ho * N:(ho + 1) * N], wt[:, kt, ho * P:(ho + 1) * P], moving[:, kt, :], start=(kt == 0), stop=(kt == KT - 1))
                last.then_inc(ready[name], 1)

            def by_token(i, name, lhs, wt):
                o = take(name, i)
                for g in range(G):
                    for kt in range(KT):
                        last = pe.matmul(o[:, g * E:(g + 1) * E], lhs[:, kt, g * P:(g + 1) * P], wt[:, kt, :], start=(kt == 0), stop=(kt == KT - 1))
                last.then_inc(ready[name], 1)

            def turn(i, name, rows, rows_ready):
                pe.wait_ge(rows_ready, once(i))
                o = take(name, i)
                for kt in range(KT):
                    for g in range(G):
                        last = pe.transpose(o[:, kt * N + g * P:kt * N + (g + 1) * P], rows[:, g, kt * P:(kt + 1) * P], ident[:])
                last.then_inc(ready[name], 1)

            def turn_first(i, name, rows, n, rows_loaded):
                pe.wait_ge(rows_loaded, per_batch(i, 32, 32))
                o = take(name, i)
                for kt in range(KT):
                    for g in range(G):
                        c = n * (kt * G + g)
                        last = pe.matmul(o[:, c:c + n], rows[:, g, kt * P:(kt + 1) * P], ident[0:n, 0:n], start=True, stop=True)
                last.then_inc(ready[name], 1)

            def mix_product(i):
                pe.wait_ge(xx_ready, once(i))
                o = take("m1", i)
                for kt in range(KT):
                    pe.matmul(o[:, 0:N], w["maa_w1"][:, kt, 0:P], xx[:, kt, :], start=(kt == 0), stop=(kt == KT - 1))
                for kt in range(KT):
                    last = pe.matmul(o[0:32, N:2 * N], w["maa_w1"][:, kt, P:P + 32], xx[:, kt, :], start=(kt == 0), stop=(kt == KT - 1))
                last.then_inc(ready["m1"], 1)

            def mixes(i):
                pe.wait_ge(mix_ready, per_batch(i, 2, 2))
                for name in ORDER:
                    f = MIX[name]
                    o = take("m2" + name, i)
                    for ho in range(KT):
                        last = pe.matmul(o[:, ho * N:(ho + 1) * N], w["maa_w2"][:, f, ho * P:(ho + 1) * P] if f < 4 else w["maa_w2b"][:, ho * P:(ho + 1) * P],
                                         mix_a[:] if f < 4 else mix_b[:], start=True, stop=True)
                    last.then_inc(ready["m2" + name], 1)

            def mixed(i, name):
                pe.wait_ge(xm_ready, per_batch(i, 5, ORDER.index(name) + 1))
                return xm[:, MIX[name]]

            def decay_1(i):
                moving = mixed(i, "w")
                o = take("td1", i)
                for kt in range(KT):
                    last = pe.matmul(o[0:64, 0:N], w["td_w1"][:, kt, :], moving[:, kt, :], start=(kt == 0), stop=(kt == KT - 1))
                last.then_inc(ready["td1"], 1)

            def decay_2(i):
                pe.wait_ge(used["td1"], once(i, 1))
                o = take("td2", i)
                for ho in range(KT):
                    last = pe.matmul(o[:, ho * N:(ho + 1) * N], w["td_w2"][:, ho * P:(ho + 1) * P], td[:], start=True, stop=True)
                last.then_inc(ready["td2"], 1)

            def head_sums(i, n):
                o = take("wkv", i) if n == 0 else at["wkv"]
                pe.wait_ge(out_prod_ready, per_batch(i, NU, n + 1))
                g, hf = UNITS[n]
                c = hf * N + g * P
                for j in range(HS):
                    last = pe.matmul(o[:, c:c + P], w["spread"][:, j, :], read_out[n % 2][:, j * P:(j + 1) * P], start=(j == 0), stop=(j == HS - 1))
                last.then_inc(units_done, 1)

            def group_mean(i):
                pe.wait_ge(used["wkv"], once(i, 1))
                pe.matmul(take("gm", i)[:], w["head_mean"], flat(oc[:]), start=True, stop=True).then_inc(ready["gm"], 1)

            def group_variance(i):
                pe.wait_ge(oc_sq_ready, once(i))
                o = take("gv", i)
                for a in range(KT * G):
                    last = pe.matmul(o[:, a * NH:(a + 1) * NH], oc_sq[:, a // G, (a % G) * P:(a % G + 1) * P], w["head_mean"][:, 0:P:HS], start=True, stop=True)
                last.then_inc(ready["gv"], 1)

            def group_inverse_std(i):
                pe.wait_ge(grstd_ready, once(i))
                o = take("gr", i)
                for a in range(KT * G):
                    last = pe.matmul(o[:, a * P:(a + 1) * P], grstd8[:, a // G, (a % G) * P:(a % G + 1) * P], ident[:], start=True, stop=True)
                last.then_inc(ready["gr"], 1)

            def step(old, b, new):
                if old is not None:
                    group_mean(old)
                if new is not None:
                    turn_first(new, "ct", first_rows, 2, a_loaded)
                    turn(new, "xt", xn, xn_ready)
                if old is not None:
                    group_variance(old)
                    group_inverse_std(old)
                if new is not None:
                    mix_product(new)
                if old is not None:
                    pe.wait_ge(og_ready, once(old))
                    by_token(old, "wo", og, w["wo"])
                    turn_first(old, "ct2", first_row0, 1, c_loaded)
                if new is not None:
                    mixes(new)
                if b is not None:
                    head_sums(b, 0)
                if new is not None:
                    by_channel(new, "vp", w["wv"], mixed(new, "v"))
                    by_channel(new, "kp", w["wk"], mixed(new, "k"))
                if b is not None:
                    head_sums(b, 1)
                if old is not None:
                    turn(old, "xt2", xn2, xn2_ready)
                if new is not None:
                    decay_1(new)
                    by_channel(new, "rp", w["wr"], mixed(new, "r"))
                if old is not None:
                    pe.wait_ge(xk2_ready, per_batch(old, 2, 1))
                    by_channel(old, "kk", w["wfk"], xk2)
                    pe.wait_ge(xk2_ready, per_batch(old, 2, 2))
                    by_token(old, "rr", xr2, w["wfr"])
                if new is not None:
                    decay_2(new)
                if b is not None:
                    head_sums(b, 2)
                if old is not None:
                    pe.wait_ge(kk_ready, once(old))
                    by_token(old, "kvp", kk, w["wfv"])
                if new is not None:
                    by_channel(new, "gp", w["wg"], mixed(new, "g"))
                if b is not None:
                    head_sums(b, 3)

            rotate(pe, NI, step)

        @block.vector
        def _(dve):
            for name in ("m2v", "m2k", "m2w", "m2r", "m2g", "gm", "gr", "wo", "kvp", "gp"):
                dve.sem_inc(used[name], 1)
            dve.sem_inc(read_ready, 2)
            dve.tensor_scalar(w["wo"], w["wo"], 0.5, None, ALU.mult).then_inc(halved, 1)

            def bn_sums(chain, rows, to):
                for g in range(G):
                    last = dve.bn_stats(to[:, g, :], rows[:, g, :])
                chain.add(last)

            def bn_variance(chain, to, aggregated, variance):
                chain.settle_before_aggregate()
                for g in range(G):
                    last = dve.bn_aggr(aggregated[:, g, :], to[:, g, :])
                chain.link(last)
                return dve.tensor_scalar(variance[:], aggregated[:, :, 1], 1e-5, None, ALU.add)

            def normalised(rows, to, aggregated, inv_std):
                for g in range(G):
                    last = dve.tensor_scalar(to[:, g, :], rows[:, g, :], aggregated[:, g, 0:1], inv_std[:, g:g + 1], ALU.subtract, ALU.mult)
                return last

            def a_sums(i, chain):
                dve.wait_ge(a_loaded, per_batch(i, 32, 32))
                bn_sums(chain, x, stats)

            def a_variance(chain):
                bn_variance(chain, stats, mv, ve).then_inc(ve_ready, 1)
                chain.close()

            def a_norm(i):
                dve.wait_ge(rstd_ready, once(i))
                normalised(x, xn, mv, rstd).then_inc(xn_ready, 1)

            def a_shift(i):
                dve.wait_ge(used["xt"], once(i, 1))
                dve.wait_ge(used["ct"], once(i, 1))
                sx4, xx4 = (t[:].rearrange("p k (g t) -> p k g t", g=G) for t in (sx, xx))
                dve.tensor_tensor(sx4, xa[:, :, :, 0:P], xa[:, :, :, 1:P + 1], ALU.subtract).then_inc(sx_ready, 1)
                dve.wait_ge(sx_ready, once(i))
                for hf in range(KT):
                    last = dve.scalar_tensor_tensor(xx4[:, hf], sx4[:, hf], col("maa_x")[:, hf:hf + 1], xa[:, hf, :, 1:P + 1], ALU.mult, ALU.add)
                last.then_inc(xx_ready, 1)

            def a_mix(i, name):
                f, n = MIX[name], ORDER.index(name)
                dve.wait_ge(ready["m2" + name], once(i))
                if n:
                    dve.wait_ge(xm_ready, per_batch(i, 5, n))
                for hf in range(KT):
                    last = dve.scalar_tensor_tensor(mix_tmp[:, hf, :], at["m2" + name][:, hf * N:(hf + 1) * N], col(f"stack{f}")[:, hf:hf + 1],
                                                    sx[:, hf, :], ALU.add, ALU.mult)
                last.then_inc(used["m2" + name], 1)
                dve.wait_ge(used["m2" + name], once(i, 1))
                dve.tensor_tensor(xm[:, f].rearrange("p k (g t) -> p k g t", g=G), mix_tmp[:].rearrange("p k (g t) -> p k g t", g=G), xa[:, :, :, 1:P + 1], ALU.add)\
                    .then_inc(xm_ready, 1)

            def a_gate(i):
                dve.wait_ge(th_ready, once(i))
                dve.scalar_tensor_tensor(flat(sg[:, parity(i)]), flat(th[:]), 1.0, at["gp"][:], ALU.add, ALU.mult).then_inc(used["gp"], 1)

            def unit_scan(i, n):
                g, hf = UNITS[n]
                sw = swept[n % 2].rearrange("p (j t) -> p j t", j=HS)
                kv3 = kv[n % 2].rearrange("p (j t) -> p j t", j=HS)
                now = slice(g * P, (g + 1) * P)
                if n == 0:
                    dve.wait_ge(decay_ready, once(i))
                dve.wait_ge(kv_ready, per_batch(i, NU, n + 3))
                dve.wait_ge(col0_ready, per_batch(i, NU, n + 1))
                for j in range(HS):
                    last = dve.tensor_tensor_scan(sw[:, j, 1:P + 1], decay[:, parity(i), hf, now], kv3[:, j, :], sw[:, j, 0:1], ALU.mult, ALU.add)
                last.then_inc(swept_ready, 1)

            def unit_read(i, n):
                g, hf = UNITS[n]
                sw = swept[n % 2].rearrange("p (j t) -> p j t", j=HS)
                kv3, ro3 = (t[n % 2].rearrange("p (j t) -> p j t", j=HS) for t in (kv, read_out))
                dve.wait_ge(swept_ready, per_batch(i, NU, n + 1))
                dve.wait_ge(units_done, per_batch(i, NU, n + 1))
                dve.scalar_tensor_tensor(ro3, kv3, col("u")[:, hf:hf + 1], sw[:, :, 0:P], ALU.mult, ALU.add).then_inc(read_ready, 1)

            def c_group_centre(i):
                dve.wait_ge(ready["gm"], once(i))
                dve.tensor_tensor(flat(oc[:]), flat(oc[:]), at["gm"][:], ALU.subtract).then_inc(used["gm"], 1)
                dve.wait_ge(used["gm"], once(i, 1))
                dve.sem_inc(oc_ready, 1)

            def c_inverse_std(i, chain):
                dve.wait_ge(gstd_ready, once(i))
                chain.link(dve.reciprocal(grstd[:], gstd[:]))
                dve.tensor_copy(grstd8[:].rearrange("p k (g h j) -> p (k g) h j", g=G, j=HS), grstd[:].unsqueeze(3).broadcast_to([P, KT * G, NH, HS])).then_inc(grstd_ready, 1)

            def c_group_norm(i):
                dve.wait_ge(ready["gr"], once(i))
                for hf in range(KT):
                    last = dve.scalar_tensor_tensor(og[:, hf, :], oc[:, hf, :], col("gn_w")[:, hf:hf + 1], at["gr"][:, hf * N:(hf + 1) * N], ALU.mult, ALU.mult)
                last.then_inc(used["gr"], 1)

            def c_gate(i):
                dve.wait_ge(used["gr"], once(i, 1))
                dve.wait_ge(used["gp"], once(i, 1))
                for hf in range(KT):
                    last = dve.scalar_tensor_tensor(og[:, hf, :], og[:, hf, :], col("gn_b")[:, hf:hf + 1], sg[:, parity(i), hf, :], ALU.add, ALU.mult)
                last.then_inc(og_ready, 1)

            def c_stats(i, chain):
                dve.wait_ge(ready["wo"], once(i))
                dve.wait_ge(c_loaded, per_batch(i, 32, 32))
                dve.tensor_tensor(x1[:], at["wo"][:].rearrange("p (g e) -> p g e", g=G), x_again[:], ALU.add).then_inc(used["wo"], 1)
                dve.wait_ge(used["wo"], once(i, 1))
                bn_sums(chain, x1, stats2)
                bn_variance(chain, stats2, mv2, ve2).then_inc(ve2_ready, 1)

            def c_norm(i):
                dve.wait_ge(rstd2_ready, once(i))
                normalised(x1, xn2, mv2, rstd2).then_inc(xn2_ready, 1)

            def c_shift(i):
                dve.wait_ge(used["xt2"], once(i, 1))
                sx4 = sx2[:].rearrange("p k (g t) -> p k g t", g=G)
                dve.tensor_tensor(sx4, xc[:, :, :, 0:P], xc[:, :, :, 1:P + 1], ALU.subtract).then_inc(sx2_ready, 1)
                dve.wait_ge(sx2_ready, once(i))
                for name, to in (("ffn_k", xk2), ("ffn_r", xr2)):
                    to4 = (to if name == "ffn_r" else to[:]).rearrange("p k (g t) -> p k g t", g=G)
                    for hf in range(KT):
                        last = dve.scalar_tensor_tensor(to4[:, hf], sx4[:, hf], col(name)[:, hf:hf + 1], xc[:, hf, :, 1:P + 1], ALU.mult, ALU.add)
                    last.then_inc(xk2_ready, 1)

            def c_receptance(i, chain):
                dve.wait_ge(used["rr"], once(i, 1))
                chain.link(dve.tensor_scalar(rr[:], rr[:], 0.5, 0.5, ALU.mult, ALU.add))

            def c_output(i, chain):
                dve.wait_ge(ready["kvp"], once(i))
                chain.link(dve.tensor_tensor(rr[:], at["kvp"][:].rearrange("p (g e) -> p g e", g=G), rr[:], ALU.mult))
                dve.sem_inc(used["kvp"], 1)
                dve.wait_ge(stored, per_batch(i, 16, 16))
                dve.tensor_tensor(out[:], rr[:], x1[:], ALU.add).then_inc(out_ready, 1)
                chain.close()

            def step(old, b, new):
                chain = Chain(dve, c_chain, 3 + 1 + 2, old)
                a_steps = Chain(dve, a_chain, 3, new)
                if new is not None:
                    a_sums(new, a_steps)
                    a_variance(a_steps)
                if old is not None:
                    c_group_centre(old)
                if new is not None:
                    a_norm(new)
                if b is not None:
                    unit_scan(b, 0)
                if old is not None:
                    c_inverse_std(old, chain)
                if new is not None:
                    a_shift(new)
                if old is not None:
                    c_group_norm(old)
                    c_gate(old)
                if b is not None:
                    unit_read(b, 0)
                    unit_scan(b, 1)
                if new is not None:
                    a_mix(new, "v")
                if b is not None:
                    unit_read(b, 1)
                if new is not None:
                    a_mix(new, "k")
                if old is not None:
                    c_stats(old, chain)
                if new is not None:
                    a_mix(new, "w")
                if old is not None:
                    c_norm(old)
                if b is not None:
                    unit_scan(b, 2)
                if new is not None:
                    a_mix(new, "r")
                if old is not None:
                    c_shift(old)
                if b is not None:
                    unit_read(b, 2)
                if new is not None:
                    a_mix(new, "g")
                if b is not None:
                    unit_scan(b, 3)
                if old is not None:
                    c_receptance(old, chain)
                if b is not None:
                    unit_read(b, 3)
                if old is not None:
                    c_output(old, chain)
                if new is not None:
                    a_gate(new)

            rotate(dve, NI, step)

        @block.gpsimd
        def _(pool):
            pool.sem_inc(kv_ready, 2)
            pool.memset(eps[:], 1e-5).then_inc(eps_set, 1)
            if prefetch:
                prefetch[0](pool)

            def key_value(i, n):
                g, hf = UNITS[n]
                if n == 0:
                    pool.wait_ge(used["kp"], once(i, 1))
                pool.wait_ge(v_rep_loaded[n % 2], per_batch(i, 32, 16 * (n // 2) + 16))
                pool.wait_ge(read_ready, per_batch(i, NU, n + 1))
                kv3, vr3 = (t[n % 2].rearrange("p (j t) -> p j t", j=HS) for t in (kv, v_rep))
                pool.tensor_tensor(kv3, vr3, k[:, parity(i), hf, g * P:(g + 1) * P].unsqueeze(1).broadcast_to([P, HS, P]), ALU.mult).then_inc(kv_ready, 1)

            def times_r(i, n):
                g, hf = UNITS[n]
                if n == 0:
                    pool.wait_ge(used["rp"], once(i, 1))
                pool.wait_ge(read_ready, per_batch(i, NU, n + 3))
                ro3 = read_out[n % 2].rearrange("p (j t) -> p j t", j=HS)
                pool.tensor_tensor(ro3, ro3, r[:, parity(i), hf, g * P:(g + 1) * P].unsqueeze(1).broadcast_to([P, HS, P]), ALU.mult).then_inc(out_prod_ready, 1)

            def inverse_std(i, signal, variance, to, done):
                pool.wait_ge(signal, once(i))
                pool.tensor_tensor(to[:], variance[:], mhalf[:, 0:G], ALU.pow).then_inc(done, 1)

            def step(old, b, new):
                if b is not None:
                    key_value(b, 0)
                if new is not None:
                    inverse_std(new, ve_ready, ve, rstd, rstd_ready)
                if b is not None:
                    key_value(b, 1)
                    times_r(b, 0)
                    key_value(b, 2)
                    times_r(b, 1)
                if old is not None:
                    inverse_std(old, ve2_ready, ve2, rstd2, rstd2_ready)
                if b is not None:
                    key_value(b, 3)
                    times_r(b, 2)
                    times_r(b, 3)

            rotate(pool, NI, step)

        @block.scalar
        def _(act):
            for name in ("xt", "ct", "m1", "vp", "kp", "td1", "td2", "rp", "wkv", "gv", "xt2", "ct2", "rr", "kk"):
                act.sem_inc(used[name], 1)
            act.wait_ge(eps_set, 1)

            def got(name, i):
                act.wait_ge(ready[name], once(i))
                return at[name]

            def affine(to, name, i, scale_name, bias_name):
                o = got(name, i)
                for hf in range(KT):
                    last = act.activation(to(hf), by_batch(o[:, hf * N:(hf + 1) * N]), ACT.Identity, bias=col(bias_name)[:, hf:hf + 1], scale=col(scale_name)[:, hf:hf + 1])
                last.then_inc(used[name], 1)

            def a_first(i):
                first = got("ct", i)[:, 0:2 * KT * G].rearrange("p (k g r) -> p k g r", k=KT, g=G)
                act.activation(xa[:, :, :, 0], first[:, :, :, 1], ACT.Copy).then_inc(used["ct"], 1)

            def a_turned(i):
                affine(lambda hf: xa[:, hf, :, 1:P + 1], "xt", i, "ln1_w", "ln1_b")

            def a_tanh(i):
                o = got("m1", i)
                act.activation(mix_a[:], o[:, 0:N], ACT.Tanh).then_inc(mix_ready, 1)
                act.activation(mix_b[:], o[0:32, N:2 * N], ACT.Tanh).then_inc(mix_ready, 1)
                act.wait_ge(mix_ready, per_batch(i, 2, 2))
                act.sem_inc(used["m1"], 1)

            def a_copy(name, to, i):
                act.activation(flat(to), got(name, i)[:], ACT.Copy).then_inc(used[name], 1)

            def a_decay_1(i):
                act.activation(td[:], got("td1", i)[0:64, 0:N], ACT.Tanh).then_inc(used["td1"], 1)

            def a_decay_2(i):
                o = got("td2", i)
                for hf in range(KT):
                    last = act.activation(decay_log[:, hf, :], o[:, hf * N:(hf + 1) * N], ACT.Exp, bias=col("time_decay")[:, hf:hf + 1])
                last.then_inc(used["td2"], 1)
                act.wait_ge(used["td2"], once(i, 1))
                act.activation(decay[:, parity(i)], decay_log[:], ACT.Exp, scale=-1.0).then_inc(decay_ready, 1)

            def a_gate(i):
                act.wait_ge(decay_ready, once(i))
                act.activation(flat(th[:]), got("gp", i)[:], ACT.Tanh, scale=0.5).then_inc(th_ready, 1)

            def back_to_tanh():
                act.activation(tanh_table[:], ident[:, 0:1], ACT.Tanh)

            def column_0(i, n):
                g, hf = UNITS[n]
                if n == 0:
                    act.wait_ge(s0_loaded, per_batch(i, 32, 32))
                act.wait_ge(read_ready, per_batch(i, NU, n + 1))
                act.activation(swept[n % 2].rearrange("p (j t) -> p j t", j=HS)[:, :, 0], s0[:, parity(i), hf, g, :], ACT.Copy).then_inc(col0_ready, 1)

            def c_group(i):
                act.wait_ge(units_done, per_batch(i, NU, NU + 2))
                act.activation(flat(oc[:]), at["wkv"][:], ACT.Copy).then_inc(used["wkv"], 1)

            def c_square(i):
                act.wait_ge(oc_ready, once(i))
                act.activation(oc_sq[:], oc[:], ACT.Square).then_inc(oc_sq_ready, 1)

            def c_std(i):
                act.activation(gstd[:].rearrange("p a h -> p (a h)"), got("gv", i)[:, 0:KT * G * NH], ACT.Sqrt, bias=eps[:]).then_inc(used["gv"], 1)
                act.wait_ge(used["gv"], once(i, 1))
                act.sem_inc(gstd_ready, 1)

            def c_turned_2(i):
                act.activation(xc[:, :, :, 0], got("ct2", i)[:, 0:KT * G].rearrange("p (k g) -> p k g", k=KT), ACT.Copy).then_inc(used["ct2"], 1)
                affine(lambda hf: xc[:, hf, :, 1:P + 1], "xt2", i, "ln2_w", "ln2_b")

            def c_relu(i):
                act.activation(flat(relu[:]), got("kk", i)[:], ACT.Relu).then_inc(used["kk"], 1)
                act.wait_ge(used["kk"], once(i, 1))
                act.activation(flat(kk[:]), flat(relu[:]), ACT.Square).then_inc(kk_ready, 1)

            def c_receptance(i):
                act.activation(rr[:].rearrange("p g e -> p (g e)"), got("rr", i)[:], ACT.Tanh, scale=0.5).then_inc(used["rr"], 1)

            def step(old, b, new):
                if old is not None:
                    c_group(old)
                if b is not None:
                    column_0(b, 0)
                    column_0(b, 1)
                if new is not None:
                    a_first(new)
                if old is not None:
                    c_square(old)
                if new is not None:
                    a_turned(new)
                if old is not None:
                    c_std(old)
                    back_to_tanh()
                if new is not None:
                    a_tanh(new)
                if b is not None:
                    column_0(b, 2)
                if new is not None:
                    act.wait_ge(v_stored, per_batch(new, 32, 32))
                    a_copy("vp", v[:], new)
                    a_copy("kp", k[:, parity(new)], new)
                if b is not None:
                    column_0(b, 3)
                if old is not None:
                    c_turned_2(old)
                if new is not None:
                    a_decay_1(new)
                    a_copy("rp", r[:, parity(new)], new)
                if old is not None:
                    c_relu(old)
                    c_receptance(old)
                if new is not None:
                    a_decay_2(new)
                    a_gate(new)

            rotate(act, NI, step)


def deq_attention(nc, NB, w, consts, src, ctx_in, dst, prefetch):
    H, D, L = 16, 64, 256
    M = H * D // P
    ident, ones, mhalf = consts["ident"], consts["ones"], consts["mhalf"]

    J_GROUPS = [("q", 0), ("k", 0), ("v", 0, 0), ("v", 1, 0), ("q", 1), ("k", 1), ("q", 2), ("k", 2), ("v", 0, 1), ("v", 1, 1), ("q", 3), ("k", 3)]
    J_SLOT = {4: 0, 5: 1, 6: 4, 7: 5, 8: 6, 9: 7, 10: 9, 11: 10}
    NJ = len(J_GROUPS)
    TA0, WO, MEAN, VAR, BCAST, NL = 0, 4, 5, 6, 7, 8
    TA_SLOT = {0: 8, 1: 12, 2: 16}
    TAIL_SLOT = {1: 3, 2: WO, 3: MEAN, 4: VAR, 5: BCAST}

    with ExitStack() as st:
        sems = st.enter_context(Semaphores(nc))

        def sb(name, shape, dt=F32):
            return st.enter_context(nc.sbuf_tensor("l1_" + name, shape, dt))

        def sem(name):
            return sems.new("l1_" + name)

        z, u, z_res = sb("z", [P, L]), sb("u", [P, L]), sb("z_res", [P, L])
        q_full, v = w["spare"][:, 0:2 * L].rearrange("p (m l) -> p m l", m=2), sb("v", [P, 2, H * D])
        q_hi, q_lo, k_hi, k_lo = (sb(n, [P, M, L], F32R) for n in ("q_hi", "q_lo", "k_hi", "k_lo"))
        prob, probT = sb("prob", [P, 2, 2, L]), sb("probT", [P, 2, 2, L])
        negmax, rowsum, rinv = sb("negmax", [P, H, 2]), sb("rowsum", [P, H, 2]), sb("rinv", [P, H, 2])
        att, attT = w["spare"][:, 2 * L:2 * L + 2 * H * D].rearrange("p (i e) -> p i e", i=2), sb("attT", [P, M, L])
        x1, xc, sq, out = sb("x1", [P, L]), sb("xc", [P, L]), sb("sq", [P, L]), sb("out", [P, L])
        var, rstd, diag = sb("var", [P, 2]), sb("rstd", [P, 2]), sb("diag", [P, 2, P])
        J = [st.enter_context(nc.psum_tensor(f"l1_J{i}", [P, 512], F32)) for i in range(2)]
        S = [st.enter_context(nc.psum_tensor(f"l1_S{i}", [P, 2, L], F32)) for i in range(2)]
        T = [st.enter_context(nc.psum_tensor(f"l1_T{i}", [P, 2, L], F32)) for i in range(2)]
        A = st.enter_context(nc.psum_tensor("l1_A", [P, 2, 4, D], F32))
        LB = st.enter_context(nc.psum_tensor("l1_L", [P, 512], F32))

        zu_loaded, zres_loaded, stored = sem("zu_loaded"), sem("zres_loaded"), sem("stored")
        j_ready, j_used = sem("j_ready"), [sem("j0_used"), sem("j1_used")]
        q_steps, k_hi_ready = sem("q_steps"), sem("k_hi_ready")
        l_ready, l_used = sem("l_ready"), sem("l_used")
        scores_ready, max_ready = sem("scores_ready"), sem("max_ready")
        exp_done, t_ready, pv_done = sem("exp_done"), sem("t_ready"), sem("pv_done")
        probT_ready = [sem("probT0_ready"), sem("probT1_ready")]
        rinv_ready, att_ready = sem("rinv_ready"), sem("att_ready")
        x1_ready, xc_ready, sq_ready = sem("x1_ready"), sem("xc_ready"), sem("sq_ready")
        var_ready, rstd_ready, diag_ready, out_ready = sem("var_ready"), sem("rstd_ready"), sem("diag_ready"), sem("out_ready")
        block = st.enter_context(nc.Block())

        def batches(eng, boundary, main):
            boundary(None, 0)
            main(0, None)
            if NB > 1:
                with eng.Fori(1, NB) as b:
                    boundary(Batch(b, -1), b)
                    main(b, Batch(b, -1))
            boundary(NB - 1, None)
            main(None, NB - 1)

        @block.sync
        def _(sp):
            sp.sem_inc(stored, 16)

            def load(b, done):
                if done is not None:
                    sp.wait_ge(j_ready, per_batch(done, NJ, NJ + 1))
                sp.dma_start(z[:], src[b]).then_inc(zu_loaded, 16)
                sp.dma_start(u[:], ctx_in[b]).then_inc(zu_loaded, 16)
                if done is not None:
                    sp.wait_ge(x1_ready, per_batch(done, 1, 2))
                sp.dma_start(z_res[:], src[b]).then_inc(zres_loaded, 16)

            load(0, None)
            if NB > 1:
                with sp.Fori(0, NB - 1) as b:
                    load(b + 1, b)
                    sp.wait_ge(out_ready, b + 1)
                    sp.dma_start(dst[b], out[:]).then_inc(stored, 16)
            sp.wait_ge(out_ready, NB)
            sp.dma_start(dst[NB - 1], out[:]).then_inc(stored, 16)
            sp.wait_ge(stored, 16 * NB + 16)
            if prefetch:
                prefetch[1](sp)

        @block.tensor
        def _(pe):
            pe.sem_inc(t_ready, 2)
            pe.sem_inc(pv_done, 2)
            pe.sem_inc(j_ready, 1)

            def project(b, g):
                kind = J_GROUPS[g]
                bank = J[g % 2]
                pe.wait_ge(j_used[g % 2], per_batch(b, NJ // 2, g // 2 + 1))
                if kind[0] == "v":
                    _, s, c = kind
                    f0 = 2 * H * D + c * 512
                    pe.matmul(bank[:], z[:, s * P:(s + 1) * P], w["wq"][s][:, f0:f0 + 512], start=True, stop=False)
                    last = pe.matmul(bank[:], u[:, s * P:(s + 1) * P], w["wi"][s][:, f0:f0 + 512], start=False, stop=True)
                else:
                    for mm in range(2):
                        f0 = (0 if kind[0] == "q" else H * D) + (2 * kind[1] + mm) * P
                        for s in range(2):
                            o = bank[:, mm * L + s * P:mm * L + (s + 1) * P]
                            pe.matmul(o, w["wq"][s][:, f0:f0 + P], z[:, s * P:(s + 1) * P], start=True, stop=False)
                            last = pe.matmul(o, w["wi"][s][:, f0:f0 + P], u[:, s * P:(s + 1) * P], start=False, stop=True)
                last.then_inc(j_ready, 1)

            def j_evacuated(b, g):
                pe.wait_ge(j_used[g % 2], per_batch(b, NJ // 2, g // 2 + 2))

            def scores(b, n):
                m, r0 = n // 2, D * (n % 2)
                if n % 4 == 0:
                    q = J_GROUPS.index(("q", n // 4))
                    j_evacuated(b, q), j_evacuated(b, q + 1)
                pe.wait_ge(exp_done, per_batch(b, H, n + 1))
                for it in range(2):
                    rows, tokens = slice(r0, r0 + D), slice(it * P, (it + 1) * P)
                    last = split_matmul(pe, S[n % 2][:, it, :], (q_hi[rows, m, tokens], q_lo[rows, m, tokens]), (k_hi[rows, m, :], k_lo[rows, m, :]))
                last.then_inc(scores_ready, 1)

            def transposes(b, n):
                pe.wait_ge(exp_done, per_batch(b, H, n + 3))
                pe.wait_ge(probT_ready[n % 2], per_batch(b, H // 2, n // 2 + 1))
                for jt in range(2):
                    for it in range(2):
                        last = pe.transpose(T[n % 2][:, jt, it * P:(it + 1) * P], prob[:, n % 2, it, jt * P:(jt + 1) * P], ident[:])
                last.then_inc(t_ready, 1)

            def attend(b, n):
                if n % 8 == 0:
                    g = J_GROUPS.index(("v", 0, n // 8))
                    j_evacuated(b, g), j_evacuated(b, g + 1)
                pe.wait_ge(probT_ready[n % 2], per_batch(b, H // 2, n // 2 + 2))
                if n % 4 == 0:
                    pe.wait_ge(att_ready, per_batch(b, 4, n // 4 + 1))
                for it in range(2):
                    for jt in range(2):
                        last = pe.matmul(A[:, it, n % 4, :], probT[:, n % 2, jt, it * P:(it + 1) * P],
                                         v[:, jt, n * D:(n + 1) * D], start=(jt == 0), stop=(jt == 1))
                last.then_inc(pv_done, 1)

            def into_l(b, g):
                pe.wait_ge(l_used, per_batch(b, NL, g + 1))
                if g < WO:
                    pe.wait_ge(att_ready, per_batch(b, 4, g + 2))
                    for c in range(2):
                        for it in range(2):
                            last = pe.transpose(LB[:, c * L + it * P:c * L + (it + 1) * P], att[:, it, (2 * g + c) * P:(2 * g + c + 1) * P], ident[:])
                elif g == WO:
                    for kt in range(M):
                        last = pe.matmul(LB[:, :L], w["wo"][:, kt, :], attT[:, kt, :], start=(kt == 0), stop=(kt == M - 1))
                elif g == MEAN:
                    last = pe.matmul(LB[:, :L], ones[:], x1[:], start=True, stop=True)
                elif g == VAR:
                    pe.wait_ge(sq_ready, per_batch(b, 1, 1))
                    for c in range(2):
                        last = pe.matmul(LB[:, c:c + 1], sq[:, c * P:(c + 1) * P], ones[:, 0:1], start=True, stop=True)
                else:
                    pe.wait_ge(diag_ready, per_batch(b, 1, 1))
                    for c in range(2):
                        last = pe.matmul(LB[:, c * P:(c + 1) * P], consts["full1"][:], diag[:, c, :], start=True, stop=True)
                last.then_inc(l_ready, 1)

            def boundary(old, new):
                if new is not None:
                    pe.wait_ge(zu_loaded, per_batch(new, 32, 32))
                for i in range(3):
                    if old is not None and i < 2:
                        transposes(old, H - 2 + i)
                    if new is not None:
                        project(new, i)
                    if old is not None:
                        attend(old, H - 3 + i)
                        if H + i in TA_SLOT.values():
                            into_l(old, 2)
                if new is not None:
                    project(new, 3)

            def main(b, old):
                for n in range(H):
                    if b is not None:
                        scores(b, n)
                        for g, slot in J_SLOT.items():
                            if slot == n:
                                project(b, g)
                        if n >= 2:
                            transposes(b, n - 2)
                        if n >= 3:
                            attend(b, n - 3)
                        for a, slot in TA_SLOT.items():
                            if slot == n:
                                into_l(b, TA0 + a)
                    if old is not None and n in TAIL_SLOT:
                        into_l(old, TAIL_SLOT[n])

            batches(pe, boundary, main)

        @block.vector
        def _(dve):
            dve.sem_inc(j_used[0], 1)
            dve.sem_inc(l_used, 1)
            dve.sem_inc(probT_ready[0], 1)
            dve.sem_inc(att_ready, 1)
            dve.sem_inc(x1_ready, 1)

            def evacuate(b, g):
                kind = J_GROUPS[g]
                dve.wait_ge(j_ready, per_batch(b, NJ, g + 2))
                if kind[0] == "q":
                    both = slice(2 * kind[1], 2 * kind[1] + 2)
                    for mm in range(2):
                        m = 2 * kind[1] + mm
                        last = dve.tensor_scalar(q_full[:, mm, :], J[0][:, mm * L:(mm + 1) * L], w["bias"][:, m:m + 1], 0.125, ALU.add, ALU.mult)
                    last.then_inc(q_steps, 1)
                    dve.wait_ge(q_steps, per_batch(b, M, 2 * kind[1] + 1))
                    dve.tensor_copy(q_hi[:, both, :], q_full).then_inc(q_steps, 1)
                    dve.wait_ge(q_steps, per_batch(b, M, 2 * kind[1] + 2))
                    last = dve.tensor_tensor(q_lo[:, both, :], q_full, q_hi[:, both, :].bitcast(F32), ALU.subtract)
                else:
                    last = dve.tensor_copy(v[:, kind[1], kind[2] * 512:(kind[2] + 1) * 512], J[0][:])
                last.then_inc(j_used[0], 1)

            def low_half_of_k(b, g):
                c = J_GROUPS[g][1]
                dve.wait_ge(k_hi_ready, per_batch(b, M // 2, c + 1))
                both = slice(2 * c, 2 * c + 2)
                dve.tensor_tensor(k_lo[:, both, :], J[1][:].rearrange("p (m l) -> p m l", m=2), k_hi[:, both, :].bitcast(F32), ALU.subtract).then_inc(j_used[1], 1)

            def head_max(b, n):
                dve.wait_ge(scores_ready, per_batch(b, H, n + 1))
                dve.tensor_reduce(negmax[:, n, :], S[n % 2][:], X_AXIS, ALU.max, negate=True).then_inc(max_ready, 1)

            def take_turned(b, n):
                dve.wait_ge(t_ready, per_batch(b, H, n + 3))
                dve.wait_ge(pv_done, per_batch(b, H, n + 1))
                dve.tensor_copy(probT[:, 0], T[0][:]).then_inc(probT_ready[0], 1)

            def divide(b, a):
                dve.wait_ge(pv_done, per_batch(b, H, 4 * a + 6))
                dve.reciprocal(rinv[:, 4 * a:4 * a + 4, :], rowsum[:, 4 * a:4 * a + 4, :]).then_inc(rinv_ready, 1)
                dve.wait_ge(rinv_ready, per_batch(b, 4, a + 1))
                dve.tensor_tensor(att[:, :, 4 * a * D:(4 * a + 4) * D].rearrange("p i (h d) -> p i h d", h=4), A[:],
                                  rinv[:, 4 * a:4 * a + 4, :].rearrange("p h i -> p i h").unsqueeze(3).broadcast_to([P, 2, 4, D]),
                                  ALU.mult).then_inc(att_ready, 1)

            def from_l(b, g):
                if g < WO and g % 2:
                    return
                dve.wait_ge(l_ready, per_batch(b, NL, g + 1))
                if g < WO:
                    dve.tensor_copy(attT[:, 2 * g:2 * g + 2, :], LB[:].rearrange("p (c l) -> p c l", c=2)).then_inc(l_used, 1)
                elif g == WO:
                    dve.wait_ge(zres_loaded, per_batch(b, 16, 16))
                    dve.scalar_tensor_tensor(x1[:], LB[:, :L], w["bo"], z_res[:], ALU.add, ALU.add).then_inc(l_used, 1)
                    dve.wait_ge(l_used, per_batch(b, NL, WO + 2))
                    dve.sem_inc(x1_ready, 1)
                elif g == MEAN:
                    dve.tensor_tensor(xc[:], x1[:], LB[:, :L], ALU.subtract).then_inc(l_used, 1)
                    dve.wait_ge(l_used, per_batch(b, NL, MEAN + 2))
                    dve.sem_inc(xc_ready, 1)
                elif g == VAR:
                    dve.tensor_scalar(var[:], LB[:, 0:2], 1e-5, None, ALU.add).then_inc(l_used, 1)
                    dve.wait_ge(l_used, per_batch(b, NL, VAR + 2))
                    dve.sem_inc(var_ready, 1)
                    dve.wait_ge(rstd_ready, per_batch(b, 1, 1))
                    for c in range(2):
                        last = dve.tensor_scalar(diag[:, c, :], ident[:], rstd[:, c:c + 1], None, ALU.mult)
                    last.then_inc(diag_ready, 1)
                else:
                    dve.wait_ge(stored, per_batch(b, 16, 16))
                    dve.tensor_tensor(out[:], xc[:], LB[:, :L], ALU.mult).then_inc(l_used, 1)
                    dve.wait_ge(l_used, per_batch(b, NL, BCAST + 2))
                    dve.sem_inc(out_ready, 1)

            def boundary(old, new):
                for i in range(3):
                    if old is not None and i == 0:
                        take_turned(old, H - 2)
                    if new is not None and i % 2 == 0:
                        evacuate(new, i)
                    if new is not None and i == 1:
                        low_half_of_k(new, 1)
                    if old is not None and i == 0:
                        from_l(old, 2)
                if old is not None:
                    divide(old, 3)

            def main(b, old):
                for n in range(H):
                    if b is not None:
                        head_max(b, n)
                        for g, slot in J_SLOT.items():
                            if slot == n and g % 2 == 0:
                                evacuate(b, g)
                            if slot == n - 1 and J_GROUPS[g][0] == "k":
                                low_half_of_k(b, g)
                        if n >= 2 and n % 2 == 0:
                            take_turned(b, n - 2)
                        if n >= 6 and n % 4 == 2:
                            divide(b, n // 4 - 1)
                        for a, slot in TA_SLOT.items():
                            if slot == n:
                                from_l(b, TA0 + a)
                    if old is not None and n in TAIL_SLOT:
                        from_l(old, TAIL_SLOT[n])

            batches(dve, boundary, main)

        @block.gpsimd
        def _(pool):
            if prefetch:
                prefetch[0](pool)
            with pool.Fori(0, NB) as b:
                pool.wait_ge(var_ready, b + 1)
                pool.tensor_tensor(rstd[:], var[:], mhalf[:, 0:2], ALU.pow).then_inc(rstd_ready, 1)

        @block.scalar
        def _(act):
            act.sem_inc(j_used[1], 1)
            act.sem_inc(probT_ready[1], 1)
            act.sem_inc(exp_done, 2)

            def evacuate(b, g):
                kind = J_GROUPS[g]
                act.wait_ge(j_ready, per_batch(b, NJ, g + 2))
                if kind[0] == "k":
                    o = k_hi[:, 2 * kind[1]:2 * kind[1] + 2, :].rearrange("p m l -> p (m l)")
                    act.activation(o, J[1][:], ACT.Copy).then_inc(k_hi_ready, 1)
                else:
                    o = v[:, kind[1], kind[2] * 512:(kind[2] + 1) * 512]
                    act.activation(o, J[1][:], ACT.Copy).then_inc(j_used[1], 1)

            def exponentials(b, n):
                act.wait_ge(max_ready, per_batch(b, H, n + 1))
                act.wait_ge(t_ready, per_batch(b, H, n + 1))
                for it in range(2):
                    last = act.activation(prob[:, n % 2, it, :], S[n % 2][:, it, :], ACT.Exp, bias=negmax[:, n, it:it + 1],
                                          accum_out=rowsum[:, n, it:it + 1])
                last.then_inc(exp_done, 1)

            def take_turned(b, n):
                act.wait_ge(t_ready, per_batch(b, H, n + 3))
                act.wait_ge(pv_done, per_batch(b, H, n + 1))
                act.activation(probT[:, 1], T[1][:], ACT.Copy).then_inc(probT_ready[1], 1)

            def from_l(b, g):
                if g < WO and g % 2:
                    act.wait_ge(l_ready, per_batch(b, NL, g + 1))
                    act.activation(attT[:, 2 * g:2 * g + 2, :], LB[:].rearrange("p (c l) -> p c l", c=2), ACT.Copy).then_inc(l_used, 1)
                elif g == MEAN:
                    act.wait_ge(xc_ready, per_batch(b, 1, 1))
                    act.activation(sq[:], xc[:], ACT.Square).then_inc(sq_ready, 1)

            def boundary(old, new):
                if new is not None:
                    evacuate(new, 1)
                if old is not None:
                    take_turned(old, H - 1)
                if new is not None:
                    evacuate(new, 3)

            def main(b, old):
                for n in range(H):
                    if b is not None:
                        exponentials(b, n)
                        for g, slot in J_SLOT.items():
                            if slot == n and g % 2:
                                evacuate(b, g)
                        if n >= 3 and n % 2:
                            take_turned(b, n - 2)
                        for a, slot in TA_SLOT.items():
                            if slot == n:
                                from_l(b, TA0 + a)
                    if old is not None and n in TAIL_SLOT:
                        from_l(old, TAIL_SLOT[n])

            batches(act, boundary, main)


def perceiver_attention(nc, NB, w, consts, src, kv_in, mask, row16_in, dst, prefetch):
    H, D, NK = 16, 16, 2 * P
    M = H // 4
    ident, mhalf = consts["ident"], consts["mhalf"]
    CTX_T, LAT_T, K0, Q, V, NJ = 0, 1, 2, 4, 5, 6
    HJ = NJ // 2
    HALVES = {1: [(K0, 0)], 2: [(K0, 1)], 3: [(K0 + 1, 0)], 4: [(K0 + 1, 1)], 5: [(Q, 0)], 6: [(Q, 1)], 7: [(V, 0), (V, 1)]}
    AT_T, OUT, NL = 0, 1, 2
    L_SLOT = {3: AT_T, 4: OUT}
    NP = H // 2

    def head(n, i):
        m, g = 2 * (n // 4) + i, n % 4
        return m, g, 4 * m + g

    with ExitStack() as st:
        sems = st.enter_context(Semaphores(nc))

        def sb(name, shape, dt=F32):
            return st.enter_context(nc.sbuf_tensor("l2_" + name, shape, dt))

        def sem(name):
            return sems.new("l2_" + name)

        lat, ctx, resid = sb("lat", [P, E]), sb("ctx", [P, E]), sb("resid", [P, 2, E])
        allT = sb("allT", [P, KT, NK])
        qT, kT, v = sb("qT", [P, 2, M, 4, P]), sb("kT", [P, 2, M, NK]), sb("v", [P, 2, 2, E])
        prob, probT = sb("prob", [P, 2, 2, NK]), sb("probT", [P, 2, 2, 2, P])
        negmax, rowsum, rinv = sb("negmax", [P, NP, 2]), sb("rowsum", [P, 2, NP, 2]), sb("rinv", [P, NP, 2])
        att, attT, out = sb("att", [P, E]), sb("attT", [P, KT, P]), sb("out", [P, E])
        J = [st.enter_context(nc.psum_tensor(f"l2_J{i}", [P, 512], F32)) for i in range(2)]
        S = [st.enter_context(nc.psum_tensor(f"l2_S{i}", [P, 2, NK], F32)) for i in range(2)]
        T = [st.enter_context(nc.psum_tensor(f"l2_T{i}", [P, 2, 2, P], F32)) for i in range(2)]
        A = st.enter_context(nc.psum_tensor("l2_A", [P, 512], F32))
        LB = st.enter_context(nc.psum_tensor("l2_L", [P, 512], F32))

        mask_in, mask_bias = sb("mask_in", [1, NB * P], I32), sb("mask_bias", [1, NB * P])
        row16, qb16 = sb("row16", [1, 512]), sb("qb16", [P, M])
        mask_loaded, mask_set, qb16_set = sem("mask_loaded"), sem("mask_set"), sem("qb16_set")
        loaded, stored = sem("loaded"), sem("stored")
        j_ready = sem("j_ready")
        j_used = [sem("j0_used"), sem("j1_used")]
        l_ready, l_used = sem("l_ready"), sem("l_used")
        scores_ready, max_ready = sem("scores_ready"), sem("max_ready")
        exp_done, t_ready, pv_done = sem("exp_done"), sem("t_ready"), sem("pv_done")
        probT_ready = [sem("probT0_ready"), sem("probT1_ready")]
        rinv_ready, att_ready, out_ready, resid_ready = sem("rinv_ready"), sem("att_ready"), sem("out_ready"), sem("resid_ready")
        block = st.enter_context(nc.Block())

        @block.sync
        def _(sp):
            sp.sem_inc(stored, 16)
            sp.dma_start(mask_in[:], mask).then_inc(mask_loaded, 16)
            sp.dma_start(row16[:], row16_in).then_inc(mask_loaded, 16)

            def load(b, before):
                if before is not None:
                    sp.wait_ge(resid_ready, per_batch(before, 1, 1))
                    sp.wait_ge(j_ready, per_batch(before, NJ, LAT_T + 1))
                sp.dma_start(lat[:], src[index(b)]).then_inc(loaded, 16)
                sp.dma_start(ctx[:], kv_in[index(b)]).then_inc(loaded, 16)

            def store(b):
                sp.wait_ge(out_ready, per_batch(b, 1, 1))
                sp.dma_start(dst[index(b)], out[:]).then_inc(stored, 16)

            load(0, None)
            load(1, 0)
            with sp.Fori(0, NB - 2) as b:
                load(Batch(b, 2), Batch(b, 1))
                store(b)
            store(NB - 2)
            store(NB - 1)
            sp.wait_ge(stored, 16 * NB + 16)
            if prefetch:
                prefetch[1](sp)

        @block.tensor
        def _(pe):
            pe.sem_inc(t_ready, 2)
            pe.sem_inc(pv_done, 2)
            pe.wait_ge(mask_set, 1)

            def j_free(b, g):
                pe.wait_ge(j_used[g % 2], per_batch(b, HJ, g // 2 + 1))

            def j_evacuated(b, g):
                pe.wait_ge(j_used[g % 2], per_batch(b, HJ, g // 2 + 2))

            def turn_inputs(b):
                pe.wait_ge(loaded, per_batch(b, 32, 32))
                for g, rows in ((CTX_T, ctx), (LAT_T, lat)):
                    j_free(b, g)
                    for kt in range(KT):
                        last = pe.transpose(J[g][:, kt * P:(kt + 1) * P], rows[:, kt * P:(kt + 1) * P], ident[:])
                    last.then_inc(j_ready, 1)

            def project(b, g, half):
                if half == 0:
                    j_free(b, g)
                if g == K0 and half == 0:
                    j_evacuated(b, CTX_T), j_evacuated(b, LAT_T)
                bank = J[g % 2]
                if g < Q:
                    m = 2 * (g - K0) + half
                    o = bank[:, half * NK:(half + 1) * NK]
                    for kt in range(KT):
                        pe.matmul(o, w["kw"][:, kt, m * P:(m + 1) * P], allT[:, kt, :], start=(kt == 0), stop=False)
                    last = pe.matmul(o[:, 0:P], row16[:, m * P:(m + 1) * P], mask_bias[0:1, bass.ds(per_batch(b, P, 0), P)], start=False, stop=True)
                elif g == Q:
                    for m in (2 * half, 2 * half + 1):
                        for kt in range(KT):
                            last = pe.matmul(bank[:, m * P:(m + 1) * P], w["qw"][:, kt, m * P:(m + 1) * P], allT[:, kt, P:NK], start=(kt == 0), stop=(kt == KT - 1))
                else:
                    for kt in range(KT):
                        last = pe.matmul(bank[:, half * E:(half + 1) * E], allT[:, kt, half * P:(half + 1) * P], w["vw"][:, kt, :], start=(kt == 0), stop=(kt == KT - 1))
                if half == 1:
                    last.then_inc(j_ready, 1)

            def scores(b, n):
                if n == 0:
                    j_evacuated(b, K0), j_evacuated(b, K0 + 1), j_evacuated(b, Q)
                pe.wait_ge(exp_done, per_batch(b, NP, n + 1))
                for i in range(2):
                    m, g, _ = head(n, i)
                    last = pe.matmul(S[n % 2][:, i, :], qT[:, parity(b), m, g, :], kT[:, parity(b), m, :], start=True, stop=True)
                last.then_inc(scores_ready, 1)

            def turn(b, n):
                pe.wait_ge(exp_done, per_batch(b, NP, n + 3))
                pe.wait_ge(probT_ready[n % 2], per_batch(b, NP // 2, n // 2 + 1))
                for i in range(2):
                    for t in range(2):
                        last = pe.transpose(T[n % 2][:, i, t, :], prob[:, n % 2, i, t * P:(t + 1) * P], ident[:])
                last.then_inc(t_ready, 1)

            def attend(b, n):
                if n == 0:
                    j_evacuated(b, V)
                    pe.wait_ge(att_ready, per_batch(b, 1, 1))
                pe.wait_ge(probT_ready[n % 2], per_batch(b, NP // 2, n // 2 + 2))
                for i in range(2):
                    _, _, h = head(n, i)
                    for t in range(2):
                        last = pe.matmul(A[:, h * D:(h + 1) * D], probT[:, n % 2, i, t, :], v[:, parity(b), t, h * D:(h + 1) * D], start=(t == 0), stop=(t == 1))
                last.then_inc(pv_done, 1)

            def into_l(b, g):
                pe.wait_ge(l_used, per_batch(b, NL, g + 1))
                if g == AT_T:
                    pe.wait_ge(att_ready, per_batch(b, 1, 2))
                for kt in range(KT):
                    if g == AT_T:
                        last = pe.transpose(LB[:, kt * P:(kt + 1) * P], att[:, kt * P:(kt + 1) * P], ident[:])
                    else:
                        last = pe.matmul(LB[:, 0:E], attT[:, kt, :], w["ow"][:, kt, :], start=(kt == 0), stop=(kt == KT - 1))
                last.then_inc(l_ready, 1)

            def step(old, b, new):
                for n in range(NP):
                    if b is not None:
                        scores(b, n)
                    if new is not None:
                        if n == 0:
                            turn_inputs(new)
                        for g, half in HALVES.get(n, []):
                            project(new, g, half)
                    if old is not None and n in L_SLOT:
                        into_l(old, L_SLOT[n])
                    if n < 2 and old is not None:
                        attend(old, NP - 2 + n)
                    if n >= 2 and b is not None:
                        attend(b, n - 2)
                    if n == 0 and old is not None:
                        turn(old, NP - 1)
                    if n >= 1 and b is not None:
                        turn(b, n - 1)

            rotate(pe, NB, step)

        @block.vector
        def _(dve):
            dve.wait_ge(mask_loaded, 32)
            dve.tensor_scalar(mask_bias[:], mask_in[:], 0.0, -1e30, ALU.is_equal, ALU.mult).then_inc(mask_set, 1)
            dve.tensor_scalar(qb16[:], w["qb"], 1.0 / D, None, ALU.mult).then_inc(qb16_set, 1)
            dve.memset(qT[:], 0.0).then_inc(qb16_set, 1)
            dve.sem_inc(j_used[0], 1)
            dve.sem_inc(l_used, 1)
            dve.sem_inc(probT_ready[0], 1)
            dve.sem_inc(att_ready, 1)
            dve.wait_ge(qb16_set, 2)

            def evacuate(b, g):
                dve.wait_ge(j_ready, per_batch(b, NJ, g + 1))
                bank, p = J[g % 2], parity(b)
                if g == CTX_T:
                    last = dve.tensor_copy(allT[:, :, 0:P], bank[:, 0:E].rearrange("p (k t) -> p k t", k=KT))
                elif g == K0:
                    last = dve.tensor_tensor(kT[:, p, 0:2, :], bank[:].rearrange("p (m n) -> p m n", m=2), w["kb"][:, 0:2].unsqueeze(2).broadcast_to([P, 2, NK]), ALU.add)
                elif g == Q:
                    for slot in range(4):
                        r = slice(32 * slot, 32 * slot + 32)
                        last = dve.scalar_tensor_tensor(qT[r, p, :, slot, :], bank[r, :].rearrange("p (m t) -> p m t", m=M), 1.0 / D,
                                                        qb16[r, :].unsqueeze(2).broadcast_to([32, M, P]), ALU.mult, ALU.add)
                else:
                    last = dve.tensor_tensor(v[:, p], bank[:].rearrange("p (n e) -> p n e", n=2), w["vb"].unsqueeze(1).broadcast_to([P, 2, E]), ALU.add)
                last.then_inc(j_used[g % 2], 1)

            def take_turned(b, n):
                dve.wait_ge(t_ready, per_batch(b, NP, n + 3))
                dve.wait_ge(pv_done, per_batch(b, NP, n + 1))
                dve.tensor_copy(probT[:, 0], T[0][:]).then_inc(probT_ready[0], 1)

            def divide(b):
                dve.wait_ge(pv_done, per_batch(b, NP, NP + 2))
                dve.wait_ge(rinv_ready, per_batch(b, 1, 1))
                for mp in range(2):
                    cols = slice(mp * P, (mp + 1) * P)
                    last = dve.tensor_tensor(att[:, cols].rearrange("p (i g d) -> p i g d", i=2, g=4), A[:, cols].rearrange("p (i g d) -> p i g d", i=2, g=4),
                                             rinv[:, 4 * mp:4 * mp + 4, :].rearrange("p g i -> p i g").unsqueeze(3).broadcast_to([P, 2, 4, D]), ALU.mult)
                last.then_inc(att_ready, 1)

            def from_l(b, g):
                dve.wait_ge(l_ready, per_batch(b, NL, g + 1))
                if g == AT_T:
                    dve.tensor_copy(attT[:], LB[:, 0:E].rearrange("p (k t) -> p k t", k=KT)).then_inc(l_used, 1)
                else:
                    dve.wait_ge(resid_ready, per_batch(b, 1, 1))
                    dve.wait_ge(stored, per_batch(b, 16, 16))
                    dve.tensor_tensor(out[:], LB[:, 0:E], resid[:, parity(b), :], ALU.add).then_inc(l_used, 1)
                    dve.wait_ge(l_used, per_batch(b, NL, NL + 1))
                    dve.sem_inc(out_ready, 1)

            def step(old, b, new):
                for n in range(NP):
                    if n == 2 and old is not None:
                        divide(old)
                    if n >= 2 and n % 2 == 0 and b is not None:
                        take_turned(b, n - 2)
                    if n == 0 and old is not None:
                        take_turned(old, NP - 2)
                    if b is not None:
                        dve.wait_ge(scores_ready, per_batch(b, NP, n + 1))
                        dve.tensor_reduce(negmax[:, n, :], S[n % 2][:], X_AXIS, ALU.max, negate=True).then_inc(max_ready, 1)
                    if n == 1 and old is not None:
                        dve.wait_ge(exp_done, per_batch(old, NP, NP + 2))
                        dve.reciprocal(rinv[:], rowsum[:, parity(old)]).then_inc(rinv_ready, 1)
                    if new is not None:
                        for g, slot in ((CTX_T, 0), (K0, 2), (Q, 6), (V, 7)):
                            if slot == n:
                                evacuate(new, g)
                    if old is not None and n in L_SLOT:
                        from_l(old, L_SLOT[n])
                    if n == 6 and new is not None:
                        dve.wait_ge(loaded, per_batch(new, 32, 32))
                        dve.tensor_tensor(resid[:, parity(new), :], lat[:], w["ob"], ALU.add).then_inc(resid_ready, 1)

            rotate(dve, NB, step)

        @block.gpsimd
        def _(pool):
            if prefetch:
                prefetch[0](pool)

        @block.scalar
        def _(act):
            act.sem_inc(j_used[1], 1)
            act.sem_inc(probT_ready[1], 1)
            act.sem_inc(exp_done, 2)

            def evacuate(b, g):
                act.wait_ge(j_ready, per_batch(b, NJ, g + 1))
                if g == LAT_T:
                    last = act.activation(allT[:, :, P:NK], J[1][:, 0:E].rearrange("p (k t) -> p k t", k=KT), ACT.Copy)
                else:
                    for mm in range(2):
                        last = act.activation(kT[:, parity(b), 2 + mm, :], J[1][:, mm * NK:(mm + 1) * NK], ACT.Identity, bias=w["kb"][:, 2 + mm:3 + mm])
                last.then_inc(j_used[1], 1)

            def take_turned(b, n):
                act.wait_ge(t_ready, per_batch(b, NP, n + 3))
                act.wait_ge(pv_done, per_batch(b, NP, n + 1))
                act.activation(probT[:, 1], T[1][:], ACT.Copy).then_inc(probT_ready[1], 1)

            def exponentials(b, n):
                act.wait_ge(max_ready, per_batch(b, NP, n + 1))
                act.wait_ge(t_ready, per_batch(b, NP, n + 1))
                for i in range(2):
                    last = act.activation(prob[:, n % 2, i, :], S[n % 2][:, i, :], ACT.Exp, bias=negmax[:, n, i:i + 1], accum_out=rowsum[:, parity(b), n, i:i + 1])
                last.then_inc(exp_done, 1)

            def step(old, b, new):
                for n in range(NP):
                    if n >= 2 and n % 2 == 1 and b is not None:
                        take_turned(b, n - 2)
                    if n == 1 and old is not None:
                        take_turned(old, NP - 1)
                    if n == 0 and new is not None:
                        evacuate(new, LAT_T)
                    if b is not None:
                        exponentials(b, n)
                    if n == 4 and new is not None:
                        evacuate(new, K0 + 1)

            rotate(act, NB, step)


def gelu_mlp(nc, NB, w, consts, src, resid_in, dst, gelu, rms, tag, prefetch):
    G = 4
    F = 1024
    M = F // P
    ident, mhalf = consts["ident"], consts["mhalf"]
    NI = NB // G

    with ExitStack() as st:
        sems = st.enter_context(Semaphores(nc))

        def sb(name, shape, dt=F32):
            return st.enter_context(nc.sbuf_tensor(tag + name, shape, dt))

        def sem(name):
            return sems.new(tag + name)

        x, xn, out, resb = sb("x", [P, G, E]), sb("xn", [P, G, E]), sb("out", [P, G, E]), sb("resb", [P, 2, G, E])
        res = sb("res", [P, G, E])
        stats, mv, ve, rstd, sqm = sb("stats", [P, G, 6]), sb("mv", [P, G, 2]), sb("ve", [P, G]), sb("rstd", [P, G]), sb("sqm", [P, G])
        xnT, hT = sb("xnT", [P, KT, G * P]), sb("hT", [P, M, G * P])
        XT = [st.enter_context(nc.psum_tensor(f"{tag}XT{i}", [P, 512], F32)) for i in range(KT)]
        H = [st.enter_context(nc.psum_tensor(f"{tag}H{i}", [P, 512], F32)) for i in range(4)]
        Y = [st.enter_context(nc.psum_tensor(f"{tag}Y{i}", [P, 2, E], F32)) for i in range(2)]

        x_loaded, res_loaded, stored = sem("x_loaded"), sem("res_loaded"), sem("stored")
        chain_sem, ve_ready, rstd_ready, xn_ready, resb_ready = sem("chain"), sem("ve_ready"), sem("rstd_ready"), sem("xn_ready"), sem("resb_ready")
        xt_ready, xnT_ready = sem("xt_ready"), sem("xnT_ready")
        h_ready, h_done = sem("h_ready"), sem("h_done")
        y_ready, y_done = sem("y_ready"), sem("y_done")
        block = st.enter_context(nc.Block())

        def rows(ap, i):
            return ap.rearrange("(n g) t e -> n t g e", g=G)[index(i)]

        def steps(eng, prepare, main):
            assert NI % 2 == 0
            prepare(0)
            if NI > 2:
                with eng.Fori(0, NI // 2 - 1) as reg:
                    for half in range(2):
                        main(Batch(reg, half, 2), Batch(reg, half + 1, 2))
            main(NI - 2, NI - 1)
            main(NI - 1, None)

        @block.sync
        def _(sp):
            sp.sem_inc(stored, 16)

            def load(i, before):
                if before is not None:
                    sp.wait_ge(xn_ready, per_batch(before, 1, 1))
                    sp.wait_ge(resb_ready, per_batch(before, 1, 1))
                sp.dma_start(x[:], rows(src, i)).then_inc(x_loaded, 16)
                sp.dma_start(res[:], rows(resid_in, i)).then_inc(res_loaded, 16)

            def store(i):
                sp.wait_ge(y_done, per_batch(i, 2, 4))
                sp.dma_start(rows(dst, i), out[:]).then_inc(stored, 16)

            load(0, None)
            load(1, 0)
            with sp.Fori(0, NI - 2) as i:
                load(Batch(i, 2), Batch(i, 1))
                store(i)
            store(NI - 2)
            store(NI - 1)
            sp.wait_ge(stored, 16 * NI + 16)
            if prefetch:
                prefetch[1](sp)

        @block.tensor
        def _(pe):
            def prepare(i):
                pe.wait_ge(xn_ready, per_batch(i, 1, 1))
                for kt in range(KT):
                    for g in range(G):
                        last = pe.transpose(XT[kt][:, g * P:(g + 1) * P], xn[:, g, kt * P:(kt + 1) * P], ident[:])
                    last.then_inc(xt_ready, 1)

            def main(i, new):
                pe.wait_ge(xnT_ready, per_batch(i, KT, KT))
                for m in range(M):
                    pe.wait_ge(h_done, per_batch(i, M, m + 1))
                    for kt in range(KT):
                        last = pe.matmul(H[m % 4][:], w["w1"][:, kt, m * P:(m + 1) * P], xnT[:, kt, :], start=(kt == 0), stop=(kt == KT - 1))
                    last.then_inc(h_ready, 1)
                if new is not None:
                    prepare(new)
                for pair in range(G // 2):
                    pe.wait_ge(y_done, per_batch(i, 2, pair + 1))
                    for k in range(2):
                        g = 2 * pair + k
                        for m in range(M):
                            if g == 0:
                                pe.wait_ge(h_done, per_batch(i, M, m + 5))
                            last = pe.matmul(Y[pair][:, k, :], hT[:, m, g * P:(g + 1) * P], w["w2"][:, m, :], start=(m == 0), stop=(m == M - 1))
                    last.then_inc(y_ready, 1)

            steps(pe, prepare, main)

        @block.vector
        def _(dve):
            dve.sem_inc(y_done, 2)

            def normalise(i):
                dve.wait_ge(x_loaded, per_batch(i, 16, 16))
                chain = Chain(dve, chain_sem, 5 if rms else 3, i)
                for g in range(G):
                    last = dve.bn_stats(stats[:, g, :], x[:, g, :])
                chain.link_before_aggregate(last)
                for g in range(G):
                    last = dve.bn_aggr(mv[:, g, :], stats[:, g, :])
                chain.link(last)
                if rms:
                    chain.link(dve.tensor_tensor(sqm[:], mv[:, :, 0], mv[:, :, 0], ALU.mult))
                    chain.link(dve.tensor_tensor(sqm[:], mv[:, :, 1], sqm[:], ALU.add))
                    dve.tensor_scalar(ve[:], sqm[:], 1e-6, None, ALU.add).then_inc(ve_ready, 1)
                else:
                    dve.tensor_scalar(ve[:], mv[:, :, 1], 1e-5, None, ALU.add).then_inc(ve_ready, 1)
                chain.close()
                dve.wait_ge(rstd_ready, per_batch(i, 1, 1))
                for g in range(G):
                    if rms:
                        last = dve.tensor_scalar(xn[:, g, :], x[:, g, :], rstd[:, g:g + 1], None, ALU.mult)
                    else:
                        last = dve.tensor_scalar(xn[:, g, :], x[:, g, :], mv[:, g, 0:1], rstd[:, g:g + 1], ALU.subtract, ALU.mult)
                last.then_inc(xn_ready, 1)
                dve.wait_ge(res_loaded, per_batch(i, 16, 16))
                dve.tensor_tensor(resb[:, parity(i)], res[:], w["b2"].unsqueeze(1).broadcast_to([P, G, E]), ALU.add).then_inc(resb_ready, 1)

            def take_turned(i):
                for kt in range(KT):
                    dve.wait_ge(xt_ready, per_batch(i, KT, kt + 1))
                    dve.tensor_scalar(xnT[:, kt, :], XT[kt][:], w["scale"][:, kt:kt + 1], w["offset"][:, kt:kt + 1], ALU.mult, ALU.add).then_inc(xnT_ready, 1)

            def prepare(i):
                normalise(i)
                take_turned(i)

            def main(i, new):
                if new is not None:
                    prepare(new)
                dve.wait_ge(resb_ready, per_batch(i, 1, 1))
                dve.wait_ge(stored, per_batch(i, 16, 16))
                for pair in range(G // 2):
                    dve.wait_ge(y_ready, per_batch(i, 2, pair + 1))
                    dve.tensor_tensor(out[:, 2 * pair:2 * pair + 2, :], Y[pair][:], resb[:, parity(i), 2 * pair:2 * pair + 2, :], ALU.add).then_inc(y_done, 1)

            steps(dve, prepare, main)

        @block.gpsimd
        def _(pool):
            if prefetch:
                prefetch[0](pool)
            with pool.Fori(0, NI) as i:
                pool.wait_ge(ve_ready, i + 1)
                pool.tensor_tensor(rstd[:], ve[:], mhalf[:, 0:G], ALU.pow).then_inc(rstd_ready, 1)

        @block.scalar
        def _(act):
            act.sem_inc(h_done, 4)
            with act.Fori(0, NI) as i:
                for m in range(M):
                    act.wait_ge(h_ready, per_batch(i, M, m + 1))
                    act.activation(hT[:, m, :], H[m % 4][:], gelu, bias=w["b1"][:, m:m + 1]).then_inc(h_done, 1)


def cross_attention(nc, NB, w, consts, src, kv_in, dst, tag, prefetch):
    H, D = 16, 128
    scale = float(D) ** -0.5
    ident, mhalf = consts["ident"], consts["mhalf"]
    HPG = 4
    NG, NP = H // HPG, H // 2
    JS = ["ctx_T", "xn_T", "k0", "q0", "k1", "q1", "v0", "k2", "q2", "v1", "k3", "q3", "v2", "v3"]
    NJ = len(JS)
    HJ = NJ // 2
    BY_SCALAR = ("xn_T", "v0", "v1", "v2", "v3")

    with ExitStack() as st:
        sems = st.enter_context(Semaphores(nc))

        def sb(name, shape, dt=F32):
            return st.enter_context(nc.sbuf_tensor(tag + name, shape, dt))

        def sem(name):
            return sems.new(tag + name)

        x, ctx = sb("x", [P, E]), sb("ctx", [P, E])
        stats, mv, ve, rstd = sb("stats", [P, 6]), sb("mv", [P, 2]), sb("ve", [P, 1]), sb("rstd", [P, 1])
        xn, resid, out = sb("xn", [P, E]), sb("resid", [P, 2, E]), sb("out", [P, E])
        xnT, ctxT = sb("xnT", [P, KT, P]), sb("ctxT", [P, 2, KT, P])
        qT, kT, v = sb("qT", [P, H, P]), sb("kT", [P, H, P + 1]), sb("v", [P, H * D])
        prob, probT, attT = sb("prob", [P, H, P + 1]), sb("probT", [P, H, P]), sb("attT", [P, H, P])
        negmax, rowsum, rinv = sb("negmax", [P, H]), sb("rowsum", [P, H]), sb("rinv", [P, H])
        learned, learnedT = sb("learned", [P, 2, H]), sb("learnedT", [H, P])
        bqs = sb("bqs", [P, H])
        diag_bv, biasv_wo, row_bias = sb("diag_bv", [P, H, H]), sb("biasv_wo", [H, E]), sb("row_bias", [P, E])
        J = [st.enter_context(nc.psum_tensor(f"{tag}J{i}", [P, 512], F32)) for i in range(2)]
        S = [st.enter_context(nc.psum_tensor(f"{tag}S{i}", [P, 512], F32)) for i in range(2)]
        T = st.enter_context(nc.psum_tensor(tag + "T", [P, HPG, P], F32))
        C = st.enter_context(nc.psum_tensor(tag + "C", [P, HPG, P], F32))
        LT = st.enter_context(nc.psum_tensor(tag + "LT", [P, 512], F32))
        Y = st.enter_context(nc.psum_tensor(tag + "Y", [P, 512], F32))

        x_loaded, ctx_loaded, stored = sem("x_loaded"), sem("ctx_loaded"), sem("stored")
        setup_v, setup_pe, setup_done = sem("setup_v"), sem("setup_pe"), sem("setup_done")
        ln_chain, ve_ready, rstd_ready = sem("ln_chain"), sem("ve_ready"), sem("rstd_ready")
        xn_ready, resid_ready = sem("xn_ready"), sem("resid_ready")
        j_ready = sem("j_ready")
        j_used = [sem("j0_used"), sem("j1_used")]
        scores_ready, max_ready, exp_done = sem("scores_ready"), sem("max_ready"), sem("exp_done")
        rinv_ready, prob_ready = sem("rinv_ready"), sem("prob_ready")
        t_ready, t_used = sem("t_ready"), sem("t_used")
        c_ready, c_used = sem("c_ready"), sem("c_used")
        lt_ready, lt_used, y_ready, y_used = sem("lt_ready"), sem("lt_used"), sem("y_ready"), sem("y_used")
        out_ready = sem("out_ready")
        block = st.enter_context(nc.Block())

        @block.sync
        def _(sp):
            sp.sem_inc(stored, 16)

            def load(b, before):
                if before is not None:
                    sp.wait_ge(resid_ready, per_batch(before, 1, 1))
                    sp.wait_ge(j_ready, per_batch(before, NJ, 1))
                sp.dma_start(x[:], src[index(b)]).then_inc(x_loaded, 16)
                sp.dma_start(ctx[:], kv_in[index(b)]).then_inc(ctx_loaded, 16)

            def store(b):
                sp.wait_ge(out_ready, per_batch(b, 1, 1))
                sp.dma_start(dst[index(b)], out[:]).then_inc(stored, 16)

            load(0, None)
            load(1, 0)
            with sp.Fori(0, NB - 2) as b:
                load(Batch(b, 2), Batch(b, 1))
                store(b)
            store(NB - 2)
            store(NB - 1)
            sp.wait_ge(stored, 16 * NB + 16)
            if prefetch:
                prefetch[1](sp)

        @block.tensor
        def _(pe):
            pe.wait_ge(setup_v, 3)
            for h in range(H):
                last = pe.matmul(J[0][0:H, 0:E], diag_bv[:, h, :], w["wo"][:, h, :], start=(h == 0), stop=(h == H - 1))
            last.then_inc(setup_pe, 1)
            for h in range(H):
                last = pe.matmul(J[1][:, 0:E], w["bv"][:, h:h + 1].broadcast_to([P, P]), w["wo"][:, h, :], start=(h == 0), stop=(h == H - 1))
            last.then_inc(setup_pe, 1)
            pe.wait_ge(setup_done, 3)

            def j_free(b, name):
                g = JS.index(name)
                pe.wait_ge(j_used[g % 2], per_batch(b, HJ, g // 2 + 1))
                return J[g % 2]

            def j_evacuated(b, name):
                g = JS.index(name)
                pe.wait_ge(j_used[g % 2], per_batch(b, HJ, g // 2 + 2))

            def turn_inputs(b):
                bank = j_free(b, "ctx_T")
                pe.wait_ge(ctx_loaded, per_batch(b, 16, 16))
                for kt in range(KT):
                    last = pe.transpose(bank[:, kt * P:(kt + 1) * P], ctx[:, kt * P:(kt + 1) * P], ident[:])
                last.then_inc(j_ready, 1)
                bank = j_free(b, "xn_T")
                pe.wait_ge(xn_ready, per_batch(b, 1, 1))
                for kt in range(KT):
                    last = pe.transpose(bank[:, kt * P:(kt + 1) * P], xn[:, kt * P:(kt + 1) * P], ident[:])
                last.then_inc(j_ready, 1)

            def project(b, name):
                bank = j_free(b, name)
                kind, c = name[0], int(name[1])
                if name in ("k0", "q0"):
                    j_evacuated(b, "ctx_T" if kind == "k" else "xn_T")
                if kind == "v":
                    for kt in range(KT):
                        last = pe.matmul(bank[:], ctxT[:, parity(b), kt, :], w["wv"][:, kt, c * 512:(c + 1) * 512], start=(kt == 0), stop=(kt == KT - 1))
                else:
                    wt = w["wk"] if kind == "k" else w["wq"]
                    for i in range(HPG):
                        h = HPG * c + i
                        for kt in range(KT):
                            moving = ctxT[:, parity(b), kt, :] if kind == "k" else xnT[:, kt, :]
                            last = pe.matmul(bank[:, i * P:(i + 1) * P], wt[:, kt, h * D:(h + 1) * D], moving, start=(kt == 0), stop=(kt == KT - 1))
                last.then_inc(j_ready, 1)

            def scores(b, n):
                if n % 2 == 0:
                    j_evacuated(b, f"k{n // 2}"), j_evacuated(b, f"q{n // 2}")
                pe.wait_ge(exp_done, per_batch(b, NP, n + 1))
                for i in range(2):
                    h = 2 * n + i
                    last = pe.matmul(S[n % 2][:, i * (P + 1):(i + 1) * (P + 1)], qT[:, h, :], kT[:, h, :], start=True, stop=True)
                last.then_inc(scores_ready, 1)

            def turn(b, g):
                pe.wait_ge(prob_ready, per_batch(b, NP, 2 * g + 2))
                pe.wait_ge(t_used, per_batch(b, NG, g + 1))
                for i in range(HPG):
                    last = pe.transpose(T[:, i, :], prob[:, HPG * g + i, 0:P], ident[:])
                last.then_inc(t_ready, 1)

            def attend(b, g):
                j_evacuated(b, f"v{g}")
                pe.wait_ge(t_used, per_batch(b, NG, g + 2))
                pe.wait_ge(c_used, per_batch(b, NG, g + 1))
                for i in range(HPG):
                    h = HPG * g + i
                    last = pe.matmul(C[:, i, :], v[:, h * D:(h + 1) * D], probT[:, h, :], start=True, stop=True)
                last.then_inc(c_ready, 1)

            def output(b, g):
                pe.wait_ge(c_used, per_batch(b, NG, g + 2))
                if g == 0:
                    pe.wait_ge(y_used, per_batch(b, 1, 1))
                for h in range(HPG * g, HPG * g + HPG):
                    pe.matmul(Y[:, 0:E], attT[:, h, :], w["wo"][:, h, :], start=(h == 0), stop=False)

            def step(old, b, new):
                for g in range(NG):
                    done, last_group = (old, NG - 1) if g == 0 else (b, g - 1)
                    if b is not None:
                        scores(b, 2 * g)
                    if done is not None:
                        turn(done, last_group)
                    if b is not None:
                        scores(b, 2 * g + 1)
                    if g == 0:
                        if old is not None:
                            pe.transpose(LT[0:H, 0:P], learned[:, parity(old), :], ident[:]).then_inc(lt_ready, 1)
                            attend(old, NG - 1)
                        if b is not None:
                            project(b, "v3")
                        if new is not None:
                            turn_inputs(new)
                        if old is not None:
                            output(old, NG - 1)
                            pe.wait_ge(lt_used, per_batch(old, 1, 1))
                            pe.matmul(Y[:, 0:E], learnedT[:], biasv_wo[:], start=False, stop=True).then_inc(y_ready, 1)
                        if new is not None:
                            project(new, "k0")
                            project(new, "q0")
                    else:
                        if new is not None:
                            project(new, f"k{g}")
                        if b is not None:
                            attend(b, g - 1)
                        if new is not None:
                            project(new, f"q{g}")
                            project(new, f"v{g - 1}")
                        if b is not None:
                            output(b, g - 1)

            rotate(pe, NB, step)

        @block.vector
        def _(dve):
            dve.tensor_scalar(bqs[:], w["bq"], scale, None, ALU.mult).then_inc(setup_v, 1)
            dve.memset(diag_bv[:], 0.0).then_inc(setup_v, 1)
            dve.wait_ge(setup_v, 2)
            dve.tensor_tensor(diag_bv[:].rearrange("p a c -> p (a c)")[:, 0:H * H:H + 1], w["bias_v"], w["bv"], ALU.subtract).then_inc(setup_v, 1)
            dve.tensor_copy(kT[:, :, P], w["bias_k"]).then_inc(setup_done, 1)
            dve.wait_ge(setup_pe, 1)
            dve.tensor_copy(biasv_wo[:], J[0][0:H, 0:E]).then_inc(setup_done, 1)
            dve.wait_ge(setup_pe, 2)
            dve.tensor_tensor(row_bias[:], J[1][:, 0:E], w["bo"], ALU.add).then_inc(setup_done, 1)
            dve.wait_ge(setup_done, 3)
            dve.sem_inc(t_used, 1)
            dve.sem_inc(y_used, 1)
            for j in range(2):
                dve.sem_inc(j_used[j], 1)

            def evacuate(b, name):
                i = JS.index(name)
                dve.wait_ge(j_ready, per_batch(b, NJ, i + 1))
                bank = J[i % 2]
                if name == "ctx_T":
                    last = dve.tensor_copy(ctxT[:, parity(b)], bank[:, 0:E].rearrange("p (k t) -> p k t", k=KT))
                else:
                    h = HPG * int(name[1])
                    heads = bank[:].rearrange("p (h t) -> p h t", h=HPG)
                    if name[0] == "k":
                        last = dve.tensor_tensor(kT[:, h:h + HPG, 0:P], heads, w["bk"][:, h:h + HPG].unsqueeze(2).broadcast_to([P, HPG, P]), ALU.add)
                    else:
                        last = dve.scalar_tensor_tensor(qT[:, h:h + HPG, :], heads, scale, bqs[:, h:h + HPG].unsqueeze(2).broadcast_to([P, HPG, P]), ALU.mult, ALU.add)
                last.then_inc(j_used[i % 2], 1)

            def pair_max(b, n):
                dve.wait_ge(scores_ready, per_batch(b, NP, n + 1))
                dve.tensor_reduce(negmax[:, 2 * n:2 * n + 2], S[n % 2][:, 0:2 * (P + 1)].rearrange("p (h t) -> p h t", h=2),
                                  X_AXIS, ALU.max, negate=True).then_inc(max_ready, 1)

            def invert_sums(b, n):
                dve.wait_ge(exp_done, per_batch(b, NP, n + 3))
                dve.reciprocal(rinv[:, 2 * n:2 * n + 2], rowsum[:, 2 * n:2 * n + 2]).then_inc(rinv_ready, 1)

            def normalise_input(b):
                dve.wait_ge(x_loaded, per_batch(b, 16, 16))
                chain = Chain(dve, ln_chain, 3, b)
                chain.link_before_aggregate(dve.bn_stats(stats[:], x[:]))
                chain.link(dve.bn_aggr(mv[:], stats[:]))
                chain.close()
                dve.tensor_scalar(ve[:], mv[:, 1:2], 1e-5, None, ALU.add).then_inc(ve_ready, 1)
                dve.wait_ge(rstd_ready, per_batch(b, 1, 1))
                dve.tensor_scalar(xn[:], x[:], mv[:, 0:1], rstd[:], ALU.subtract, ALU.mult).then_inc(xn_ready, 1)

            def step(old, b, new):
                for g in range(NG):
                    done, last_group = (old, NG - 1) if g == 0 else (b, g - 1)
                    if b is not None:
                        pair_max(b, 2 * g)
                    if done is not None:
                        dve.wait_ge(t_ready, per_batch(done, NG, last_group + 1))
                        h = HPG * last_group
                        dve.tensor_copy(probT[:, h:h + HPG, :], T[:]).then_inc(t_used, 1)
                    if b is not None:
                        pair_max(b, 2 * g + 1)
                        invert_sums(b, 2 * g)
                    if g == 0:
                        if new is not None:
                            normalise_input(new)
                        if old is not None:
                            dve.wait_ge(lt_ready, per_batch(old, 1, 1))
                            dve.tensor_copy(learnedT[:], LT[0:H, 0:P]).then_inc(lt_used, 1)
                        if new is not None:
                            evacuate(new, "ctx_T")
                    if b is not None:
                        invert_sums(b, 2 * g + 1)
                    if g == 0 and old is not None:
                        dve.wait_ge(y_ready, per_batch(old, 1, 1))
                        dve.wait_ge(resid_ready, per_batch(old, 1, 1))
                        dve.wait_ge(stored, per_batch(old, 16, 16))
                        dve.tensor_tensor(out[:], Y[:, 0:E], resid[:, parity(old), :], ALU.add).then_inc(y_used, 1)
                        dve.wait_ge(y_used, per_batch(old, 1, 2))
                        dve.sem_inc(out_ready, 1)
                    if new is not None:
                        evacuate(new, f"k{g}")
                        evacuate(new, f"q{g}")
                        if g == 1:
                            dve.tensor_tensor(resid[:, parity(new), :], x[:], row_bias[:], ALU.add).then_inc(resid_ready, 1)

            rotate(dve, NB, step)

        @block.gpsimd
        def _(pool):
            if prefetch:
                prefetch[0](pool)

            def probabilities(b, n):
                pool.wait_ge(rinv_ready, per_batch(b, NP, n + 1))
                pr, ri = prob[:, 2 * n:2 * n + 2, 0:P], rinv[:, 2 * n:2 * n + 2]
                pool.tensor_tensor(learned[:, parity(b), 2 * n:2 * n + 2], prob[:, 2 * n:2 * n + 2, P], ri, ALU.mult)
                pool.tensor_tensor(pr, pr, ri.unsqueeze(2).broadcast_to([P, 2, P]), ALU.mult).then_inc(prob_ready, 1)

            def step(old, b, new):
                for g in range(NG):
                    if b is not None:
                        probabilities(b, 2 * g)
                    if g == 0 and new is not None:
                        pool.wait_ge(ve_ready, per_batch(new, 1, 1))
                        pool.tensor_tensor(rstd[:], ve[:], mhalf[:, 0:1], ALU.pow).then_inc(rstd_ready, 1)
                    if b is not None:
                        probabilities(b, 2 * g + 1)

            rotate(pool, NB, step)

        @block.scalar
        def _(act):
            act.sem_inc(c_used, 1)
            act.sem_inc(exp_done, 2)

            def evacuate(b, name):
                i = JS.index(name)
                act.wait_ge(j_ready, per_batch(b, NJ, i + 1))
                bank = J[i % 2]
                if name == "xn_T":
                    for kt in range(KT):
                        last = act.activation(xnT[:, kt, :], bank[:, kt * P:(kt + 1) * P], ACT.Identity, bias=w["offset"][:, kt:kt + 1], scale=w["scale"][:, kt:kt + 1])
                else:
                    c = int(name[1])
                    last = act.activation(v[:, c * 512:(c + 1) * 512], bank[:], ACT.Copy)
                last.then_inc(j_used[i % 2], 1)

            def exponentials(b, n):
                act.wait_ge(max_ready, per_batch(b, NP, n + 1))
                for i in range(2):
                    h = 2 * n + i
                    last = act.activation(prob[:, h, :], S[n % 2][:, i * (P + 1):(i + 1) * (P + 1)], ACT.Exp, bias=negmax[:, h:h + 1], accum_out=rowsum[:, h:h + 1])
                last.then_inc(exp_done, 1)

            def take_attended(b, g):
                act.wait_ge(c_ready, per_batch(b, NG, g + 1))
                act.activation(attT[:, HPG * g:HPG * g + HPG, :], C[:], ACT.Copy).then_inc(c_used, 1)

            def step(old, b, new):
                for g in range(NG):
                    if b is not None:
                        exponentials(b, 2 * g)
                        exponentials(b, 2 * g + 1)
                    if g == 0:
                        if old is not None:
                            take_attended(old, NG - 1)
                        if b is not None:
                            evacuate(b, "v3")
                        if new is not None:
                            evacuate(new, "xn_T")
                    else:
                        if b is not None:
                            take_attended(b, g - 1)
                        if new is not None:
                            evacuate(new, f"v{g - 1}")

            rotate(act, NB, step)


L0_COLS = ["ln1_w", "ln1_b", "ln2_w", "ln2_b", "maa_x", "time_decay", "u", "gn_w", "gn_b", "ffn_k", "ffn_r",
           "stack0", "stack1", "stack2", "stack3", "stack4"]
HEAD_COLS = ["bq", "bk", "bv", "bias_k", "bias_v"]
COLUMNS = ([("l0_" + n, 2) for n in L0_COLS] + [("l1_bias", 8), ("l1_bo", 1)]
           + [("l2_qb", 4), ("l2_kb", 4), ("l2m_b1", 8), ("l2m_scale", 2), ("l2m_offset", 2)]
           + [(f"l3{s}_{n}", 16) for s in "ab" for n in HEAD_COLS]
           + [(f"l3{s}_{n}", 2) for s in "ab" for n in ("scale", "offset")]
           + [("l3m_b1", 8), ("l3m_scale", 2), ("l3m_offset", 2)])
ROWS = ["l2_vb", "l2_ob", "l2m_b2", "l3a_bo", "l3b_bo", "l3m_b2"]
N_COLS = sum(n for _, n in COLUMNS)


def col_at(name):
    at = 0
    for n, width in COLUMNS:
        if n == name:
            return at, width
        at += width
    raise KeyError(name)


L0_W = [("l0_maa_w1", 2 * 160, P), ("l0_maa_w2", 1024, P), ("l0_maa_w2b", 256, 32), ("l0_wv", 512, P), ("l0_wk", 512, P), ("l0_td_w1", 128, P),
        ("l0_td_w2", 256, 64), ("l0_wr", 512, P), ("l0_wg", 512, P), ("l0_wo", 512, P), ("l0_wfk", 512, P), ("l0_wfr", 512, P), ("l0_wfv", 512, P),
        ("l0_spread", 1024, P), ("l0_head_mean", P, P)]
L1_W = [("l1_wq0", 3072, P), ("l1_wi0", 3072, P), ("l1_wq1", 3072, P), ("l1_wi1", 3072, P), ("l1_wo", 1024, P)]
L2_W = [("l2_kw", 1024, P), ("l2_vw", 512, P), ("l2_qw", 1024, P), ("l2_ow", 512, P), ("l2m_w1", 2048, P), ("l2m_w2", 2048, P)]
L3A_W = [("l3a_wk", 4096, P), ("l3a_wq", 4096, P), ("l3a_wv", 4096, P), ("l3a_wo", 4096, P)]
L3B_W = [("l3b" + n[3:], c, p) for n, c, p in L3A_W]
L3M_W = [("l3m_w1", 2048, P), ("l3m_w2", 2048, P)]


def program(nc, dram, out):
    NB = dram["x"].shape[0]
    hidden = [nc.dram_tensor(f"hidden{n}", [NB, P, E], F32, kind="Internal").ap() for n in range(6)]
    v_dram = nc.dram_tensor("v_dram", [NB // 2, 2, E, P], F32, kind="Internal").ap()

    with ExitStack() as st:
        def sb(name, shape, dt=F32):
            return st.enter_context(nc.sbuf_tensor(name, shape, dt))

        region = [sb("region0", [P, REGION]), sb("region1", [P, REGION])]
        columns, rows = sb("columns", [P, N_COLS]), sb("rows", [P, len(ROWS), E])
        ident = sb("ident", [P, P])
        mean_of, full1, mhalf = sb("mean_of", [P, P]), sb("full1", [P, P]), sb("mhalf", [P, 64])
        loaded = {name: st.enter_context(nc.semaphore("loaded_" + name)) for name in ("small", "l0", "l1", "l2", "l3a", "l3b", "l3m")}
        constants_set = st.enter_context(nc.semaphore("constants_set"))
        consts = dict(ident=ident, ones=mean_of, full1=full1, mhalf=mhalf)

        def col(name):
            at, width = col_at(name)
            return columns[:, at:at + width]

        def row(name):
            return rows[:, ROWS.index(name), :]

        def places(weights, reg):
            at, out_ = 0, {}
            for name, words, parts in weights:
                out_[name] = region[reg][0:parts, at:at + words]
                at += words
            return out_

        place = {}
        for weights, reg in ((L0_W, 0), (L1_W, 1), (L2_W, 0), (L3A_W, 1), (L3B_W, 0), (L3M_W, 1)):
            place.update(places(weights, reg))

        def loader(name, weights):
            def start(eng):
                for n, _, _ in weights:
                    eng.dma_start(place[n], dram[n]).then_inc(loaded[name], 16)

            def wait(eng):
                eng.wait_ge(loaded[name], 16 * len(weights))
            return start, wait

        def tiles(name, k):
            return place[name].rearrange("p (k n) -> p k n", k=k)

        start_l0, wait_l0 = loader("l0", L0_W)
        with nc.Block() as block:
            @block.sync
            def _(sp):
                for to, name in ((columns, "columns"), (ident, "ident")):
                    sp.dma_start(to[:], dram[name]).then_inc(loaded["small"], 16)
                sp.dma_start(rows[:].rearrange("p r e -> p (r e)"), dram["rows"].partition_broadcast(P)).then_inc(loaded["small"], 16)
                start_l0(sp)
                sp.wait_ge(loaded["small"], 48)
                wait_l0(sp)

            @block.vector
            def _(dve):
                dve.memset(mean_of[:], 1.0 / P).then_inc(constants_set, 1)
                dve.memset(full1[:], 1.0).then_inc(constants_set, 1)
                dve.memset(mhalf[:], -0.5).then_inc(constants_set, 1)
                dve.wait_ge(constants_set, 3)

        w0 = {n[3:]: place[n] for n, _, _ in L0_W}
        for n in ("maa_w1", "td_w1", "wr", "wk", "wv", "wg", "wo", "wfk", "wfr", "wfv"):
            w0[n] = tiles("l0_" + n, 2)
        w0["maa_w2"], w0["spread"] = tiles("l0_maa_w2", 4), tiles("l0_spread", 8)
        w0["col"] = lambda name: col("l0_" + name)
        rwkv_block(nc, NB, w0, dict(region=region[0], at=REGION), consts, dram["x"], dram["ctx"], v_dram, hidden[0], loader("l1", L1_W))

        w1 = dict(wq=[place["l1_wq0"], place["l1_wq1"]], wi=[place["l1_wi0"], place["l1_wi1"]], wo=tiles("l1_wo", 8), bias=col("l1_bias"), bo=col("l1_bo"),
                  spare=region[1][:, sum(words for _, words, _ in L1_W):])
        deq_attention(nc, NB, w1, consts, hidden[0], dram["ctx"], hidden[1], loader("l2", L2_W))

        w2 = dict(kw=tiles("l2_kw", 2), vw=tiles("l2_vw", 2), qw=tiles("l2_qw", 2), ow=tiles("l2_ow", 2), qb=col("l2_qb"), kb=col("l2_kb"),
                  vb=row("l2_vb"), ob=row("l2_ob"))
        perceiver_attention(nc, NB, w2, consts, hidden[1], dram["ctx"], dram["mask"], dram["row16"], hidden[2], loader("l3a", L3A_W))

        def mlp_weights(tag):
            return dict(w1=tiles(tag + "_w1", 2), w2=tiles(tag + "_w2", 8), b1=col(tag + "_b1"), b2=row(tag + "_b2"), scale=col(tag + "_scale"), offset=col(tag + "_offset"))

        gelu_mlp(nc, NB, mlp_weights("l2m"), consts, hidden[2], hidden[1], hidden[3], ACT.Gelu_apprx_tanh, True, "l2m_", None)

        def attention_weights(tag):
            w = {n: col(f"{tag}_{n}") for n in HEAD_COLS + ["scale", "offset"]}
            w.update({n: tiles(f"{tag}_{n}", 2) for n in ("wq", "wk", "wv")})
            w.update(wo=tiles(tag + "_wo", 16), bo=row(tag + "_bo"))
            return w

        cross_attention(nc, NB, attention_weights("l3a"), consts, hidden[3], dram["ctx"], hidden[4], "l3a_", loader("l3b", L3B_W))
        cross_attention(nc, NB, attention_weights("l3b"), consts, hidden[4], dram["ctx"], hidden[5], "l3b_", loader("l3m", L3M_W))
        gelu_mlp(nc, NB, mlp_weights("l3m"), consts, hidden[5], hidden[5], out, ACT.Gelu, False, "l3m_", None)


def layout(inputs, np):
    def c(a):
        return np.ascontiguousarray(a)

    def tiled(a):
        return c(a.reshape(-1, P, a.shape[1]).transpose(1, 0, 2)).reshape(P, -1)

    def columns_of(a):
        return a.reshape(-1, P).T

    def slots(a):
        o = np.zeros(a.shape[:-1] + (32,), a.dtype)
        o[..., :16] = a
        return o.reshape(a.shape[:-2] + (512,))

    l0 = {k[9:]: v for k, v in inputs.items() if k.startswith("L0_xattn_")}
    l1 = {k[9:]: v for k, v in inputs.items() if k.startswith("L1_xattn_")}
    l2 = {k[9:]: v for k, v in inputs.items() if k.startswith("L2_xattn_")}
    l3 = {k[9:]: v for k, v in inputs.items() if k.startswith("L3_xattn_")}
    a = dict(x=inputs["x"], ctx=inputs["ctx_2048"], mask=inputs["mask_BxS2_ik0"].reshape(1, -1))
    a["l0_maa_w1"], a["l0_maa_w2"], a["l0_maa_w2b"] = tiled(l0["maa_w1"]), np.zeros((4, 32, 4, E), np.float32), l0["maa_w2"][4]
    for f in range(4):
        a["l0_maa_w2"][f, :, f] = l0["maa_w2"][f]
    a["l0_maa_w2"] = a["l0_maa_w2"].reshape(P, 4 * E)
    a["l0_td_w1"], a["l0_td_w2"] = tiled(l0["td_w1"]), l0["td_w2"]
    for n in ("r", "k", "v", "g", "o", "fk", "fr", "fv"):
        a["l0_w" + n] = tiled(l0["W" + n].T)
    for s in "01":
        a["l1_wq" + s], a["l1_wi" + s] = l1["Wqkv" + s].T, l1["Winj" + s].T
    a["l1_wo"] = tiled(l1["Wo"].T)
    kv = l2["kv_w"].reshape(E, 16, 16, 2)
    a["l2_qw"], a["l2_kw"] = tiled(slots(l2["q_w"].reshape(E, 16, 16))), tiled(slots(kv[..., 0]))
    a["l2_vw"], a["l2_ow"] = tiled(kv[..., 1].reshape(E, E)), tiled(l2["out_w"])
    a["l2m_w1"], a["l2m_w2"] = tiled(l2["mlp_w1"]), tiled(l2["mlp_w2"])
    for s, n in (("a", "1"), ("b", "2")):
        for m in ("wq", "wk", "wv", "wo"):
            a[f"l3{s}_{m}"] = tiled(l3[m + n])
    a["l3m_w1"], a["l3m_w2"] = tiled(l3["w_fc1"]), tiled(l3["w_fc2"])

    kv_b = l2["kv_b"].reshape(16, 16, 2)
    one16 = np.zeros((16, 32), np.float32)
    one16[:, 16] = 1.0
    q_b = slots(l2["q_b"].reshape(16, 16)).reshape(16, 32)
    q_b[:, 16] = 1.0
    v = {"l1_bias": l1["r_w_bias"], "l1_bo": l1["bo"], "l2_qb": q_b, "l2_kb": slots(kv_b[..., 0]), "l2m_b1": l2["mlp_b1"],
         "l2m_scale": l2["postnorm_w"], "l2m_offset": np.zeros(E, np.float32),
         "l3m_b1": l3["b_fc1"], "l3m_scale": l3["ln_mlp_scale"], "l3m_offset": l3["ln_mlp_offset"]}
    for n in L0_COLS:
        v["l0_" + n] = l0["maa_stack"][0, int(n[5:])] if n.startswith("stack") else l0[n.replace("ffn_", "ffn_maa_")]
    for s, n in (("a", "1"), ("b", "2")):
        for m in HEAD_COLS:
            v[f"l3{s}_{m}"] = l3[m + n]
        v[f"l3{s}_scale"], v[f"l3{s}_offset"] = l3[f"ln{n}_scale"], l3[f"ln{n}_offset"]
    a["columns"] = np.concatenate([columns_of(v[n]) for n, _ in COLUMNS], axis=1)
    r = {"l2_vb": kv_b[..., 1].reshape(E), "l2_ob": l2["out_b"], "l2m_b2": l2["mlp_b2"], "l3a_bo": l3["bo1"], "l3b_bo": l3["bo2"], "l3m_b2": l3["b_fc2"]}
    a["rows"] = np.concatenate([r[n] for n in ROWS])
    a["ident"] = np.eye(P, dtype=np.float32)
    row, column = np.arange(P)[:, None, None], np.arange(P)[None, None, :]
    same_head = row // 8 == column // 8
    a["l0_spread"] = (same_head & (column % 8 == np.arange(8)[None, :, None])).astype(np.float32).reshape(P, -1)
    a["l0_head_mean"] = np.where(same_head[:, 0], 0.125, 0.0).astype(np.float32)
    a["row16"] = one16.reshape(1, 512)
    return {k: c(x) for k, x in a.items()}


def kernel(**inputs):
    import numpy as _np
    import concourse.bacc as _bacc
    from concourse import mybir as _mybir
    from concourse.bass_utils import run_bass_kernel_spmd as _run

    nc = _bacc.Bacc("TRN2", target_bir_lowering=False, num_devices=1)
    arrays = layout({k: _np.asarray(v) for k, v in inputs.items()}, _np)
    dram = {n: nc.dram_tensor(n + "_dram", a.shape, _mybir.dt.from_np(a.dtype), kind="ExternalInput").ap() for n, a in arrays.items()}
    out = nc.dram_tensor("out_dram", arrays["x"].shape, _mybir.dt.float32, kind="ExternalOutput").ap()
    program(nc, dram, out)
    r = _run(nc, [{n + "_dram": a for n, a in arrays.items()}], core_ids=[0])
    return r.results[0]["out_dram"]
```
